# Optimizing a Trainium2 kernel written in Bass

```python
import numpy as np
import jax
import jax.numpy as jnp

def _softmax(x, axis=-1):
    return jax.nn.softmax(x, axis=axis)
def _gelu(x):
    return jax.nn.gelu(x, approximate=True)
def _silu(x):
    return jax.nn.silu(x)
def _sigmoid(x):
    return jax.nn.sigmoid(x)
def _layernorm(x, axis=-1, eps=1e-5):
    m = jnp.mean(x, axis=axis, keepdims=True)
    v = jnp.var(x, axis=axis, keepdims=True)
    return (x - m) / jnp.sqrt(v + eps)
def _scatter_add(tgt, idx, src, axis=0):
    return tgt.at[idx].add(src)
def _segment_sum(src, seg, n):
    return jax.ops.segment_sum(src, seg, n)

kernel_name = 'mk_metaformer_d1_conv_nhwc128_992316'

def setup_inputs(seed: int = 0):
    np.random.seed(seed)
    _w = jnp.asarray
    def _rec_inputs():
        import jax
        import jax.numpy as jnp
        _gk = jax.random.key(seed)
        x = -0.0002928 + 1 * jax.random.normal(jax.random.fold_in(_gk, 1), (4, 64, 128, 128), jnp.float32)
        return x
    x = _rec_inputs()
    def _L0_conv_setup():
        import jax, jax.numpy as jnp
        import numpy as np
        B, C0, H, W = (4, 64, 128, 128)
        C = 2 * C0
        HEADS = 8
        BH = HEADS // 2
        SS = 4
        EPS = 1e-05

        def _ln(x, g, b):
            m = x.mean(-1, keepdims=True)
            v = ((x - m) ** 2).mean(-1, keepdims=True)
            return (x - m) * jax.lax.rsqrt(v + EPS) * g + b

        def _img2win(img, H_sp, W_sp):
            b, c = (img.shape[0], img.shape[1])
            x = img.reshape(b, c, H // H_sp, H_sp, W // W_sp, W_sp)
            return x.transpose(0, 2, 4, 3, 5, 1).reshape(-1, H_sp * W_sp, c)

        def _win2img(wins, H_sp, W_sp):
            c = wins.shape[-1]
            x = wins.reshape(-1, H // H_sp, W // W_sp, H_sp, W_sp, c)
            return x.transpose(0, 1, 3, 2, 4, 5).reshape(-1, H * W, c)

        def _lepe_attn(q, k, v, cw, cbias, H_sp, W_sp):
            b, L, cb = q.shape
            d = cb // BH
            scale = d ** (-0.5)

            def to_win(t):
                img = t.transpose(0, 2, 1).reshape(b, cb, H, W)
                w = _img2win(img, H_sp, W_sp)
                return w.reshape(-1, H_sp * W_sp, BH, d).transpose(0, 2, 1, 3)
            qw = to_win(q) * scale
            kw = to_win(k)
            vimg = v.transpose(0, 2, 1).reshape(b, cb, H // H_sp, H_sp, W // W_sp, W_sp)
            vwin = vimg.transpose(0, 2, 4, 1, 3, 5).reshape(-1, cb, H_sp, W_sp)
            lepe = jax.lax.conv_general_dilated(vwin, cw, (1, 1), 'SAME', feature_group_count=cb)
            lepe = lepe + cbias[None, :, None, None]
            lepe = lepe.reshape(-1, BH, d, H_sp * W_sp).transpose(0, 1, 3, 2)
            vw = vwin.reshape(-1, BH, d, H_sp * W_sp).transpose(0, 1, 3, 2)
            attn = jax.nn.softmax(jnp.einsum('whnd,whmd->whnm', qw, kw), axis=-1)
            o = jnp.einsum('whnm,whmd->whnd', attn, vw) + lepe
            o = o.transpose(0, 2, 1, 3).reshape(-1, H_sp * W_sp, cb)
            return _win2img(o, H_sp, W_sp)
        key = jax.random.key(seed)
        ks = jax.random.split(key, 16)
        s = 0.02
        d_ff = 4 * C
        return {'x': jax.random.normal(ks[0], (B, C0, H, W), jnp.float32), 'w_embed': jax.random.normal(ks[1], (C0, C), jnp.float32) * s, 'g1': 1.0 + jax.random.normal(ks[2], (C,), jnp.float32) * s, 'b1': jax.random.normal(ks[3], (C,), jnp.float32) * s, 'w_qkv': jax.random.normal(ks[4], (C, 3 * C), jnp.float32) * s, 'conv_w0': jax.random.normal(ks[5], (C // 2, 1, 3, 3), jnp.float32) * s, 'conv_b0': jax.random.normal(ks[6], (C // 2,), jnp.float32) * s, 'conv_w1': jax.random.normal(ks[7], (C // 2, 1, 3, 3), jnp.float32) * s, 'conv_b1': jax.random.normal(ks[8], (C // 2,), jnp.float32) * s, 'w_proj': jax.random.normal(ks[9], (C, C), jnp.float32) * s, 'b_proj': jax.random.normal(ks[10], (C,), jnp.float32) * s, 'g2': 1.0 + jax.random.normal(ks[11], (C,), jnp.float32) * s, 'b2': jax.random.normal(ks[12], (C,), jnp.float32) * s, 'w_fc1': jax.random.normal(ks[13], (C, d_ff), jnp.float32) * s, 'b_fc1': jnp.zeros((d_ff,), jnp.float32), 'w_fc2': jax.random.normal(ks[14], (d_ff, C), jnp.float32) * s, 'b_fc2': jnp.zeros((C,), jnp.float32), 'w_out': jax.random.normal(ks[15], (C, C0), jnp.float32) * s}
    _L0_conv_all = _L0_conv_setup()
    _L0_conv_in = {k: v for k, v in _L0_conv_all.items() if k in ('w_embed', 'g1', 'b1', 'w_qkv', 'conv_w0', 'conv_b0', 'conv_w1', 'conv_b1', 'w_proj', 'b_proj', 'g2', 'b2', 'w_fc1', 'b_fc1', 'w_fc2', 'b_fc2', 'w_out', )}
    del _L0_conv_all

    def _L0_ffn_setup():
        import jax, jax.numpy as jnp
        import numpy as np
        B, N, D, C, E, K = (8, 8192, 128, 128, 8, 2)
        key = jax.random.key(seed)
        k0, k1, k2 = jax.random.split(key, 3)
        x = jax.random.normal(k0, (B, N, D), dtype=jnp.float32)
        router_w = jax.random.normal(k1, (D, E), dtype=jnp.float32) * 0.05
        router_b = jnp.zeros((E,), dtype=jnp.float32)
        expert_w = jax.random.normal(k2, (E, D, C), dtype=jnp.float32) * (1.0 / np.sqrt(D))
        expert_b = jnp.zeros((E, C), dtype=jnp.float32)
        return {'x': x, 'router_w': router_w, 'router_b': router_b, 'expert_w': expert_w, 'expert_b': expert_b}
    _L0_ffn_all = _L0_ffn_setup()
    _L0_ffn_in = {k: v for k, v in _L0_ffn_all.items() if k in ('router_w', 'router_b', 'expert_w', 'expert_b', )}
    del _L0_ffn_all

    return {
        "x": x,
        "L0_conv_w_embed": _L0_conv_in["w_embed"],
        "L0_conv_g1": _L0_conv_in["g1"],
        "L0_conv_b1": _L0_conv_in["b1"],
        "L0_conv_w_qkv": _L0_conv_in["w_qkv"],
        "L0_conv_conv_w0": _L0_conv_in["conv_w0"],
        "L0_conv_conv_b0": _L0_conv_in["conv_b0"],
        "L0_conv_conv_w1": _L0_conv_in["conv_w1"],
        "L0_conv_conv_b1": _L0_conv_in["conv_b1"],
        "L0_conv_w_proj": _L0_conv_in["w_proj"],
        "L0_conv_b_proj": _L0_conv_in["b_proj"],
        "L0_conv_g2": _L0_conv_in["g2"],
        "L0_conv_b2": _L0_conv_in["b2"],
        "L0_conv_w_fc1": _L0_conv_in["w_fc1"],
        "L0_conv_b_fc1": _L0_conv_in["b_fc1"],
        "L0_conv_w_fc2": _L0_conv_in["w_fc2"],
        "L0_conv_b_fc2": _L0_conv_in["b_fc2"],
        "L0_conv_w_out": _L0_conv_in["w_out"],
        "L0_ffn_router_w": _L0_ffn_in["router_w"],
        "L0_ffn_router_b": _L0_ffn_in["router_b"],
        "L0_ffn_expert_w": _L0_ffn_in["expert_w"],
        "L0_ffn_expert_b": _L0_ffn_in["expert_b"],
    }

def reference(x, L0_conv_w_embed, L0_conv_g1, L0_conv_b1, L0_conv_w_qkv, L0_conv_conv_w0, L0_conv_conv_b0, L0_conv_conv_w1, L0_conv_conv_b1, L0_conv_w_proj, L0_conv_b_proj, L0_conv_g2, L0_conv_b2, L0_conv_w_fc1, L0_conv_b_fc1, L0_conv_w_fc2, L0_conv_b_fc2, L0_conv_w_out, L0_ffn_router_w, L0_ffn_router_b, L0_ffn_expert_w, L0_ffn_expert_b):
    import jax
    import jax.numpy as jnp
    def _L0_conv_ref(x, w_embed, g1, b1, w_qkv, conv_w0, conv_b0, conv_w1, conv_b1, w_proj, b_proj, g2, b2, w_fc1, b_fc1, w_fc2, b_fc2, w_out):
        import jax, jax.numpy as jnp
        import numpy as np
        B, C0, H, W = (4, 64, 128, 128)
        C = 2 * C0
        HEADS = 8
        BH = HEADS // 2
        SS = 4
        EPS = 1e-05

        def _ln(x, g, b):
            m = x.mean(-1, keepdims=True)
            v = ((x - m) ** 2).mean(-1, keepdims=True)
            return (x - m) * jax.lax.rsqrt(v + EPS) * g + b

        def _img2win(img, H_sp, W_sp):
            b, c = (img.shape[0], img.shape[1])
            x = img.reshape(b, c, H // H_sp, H_sp, W // W_sp, W_sp)
            return x.transpose(0, 2, 4, 3, 5, 1).reshape(-1, H_sp * W_sp, c)

        def _win2img(wins, H_sp, W_sp):
            c = wins.shape[-1]
            x = wins.reshape(-1, H // H_sp, W // W_sp, H_sp, W_sp, c)
            return x.transpose(0, 1, 3, 2, 4, 5).reshape(-1, H * W, c)

        def _lepe_attn(q, k, v, cw, cbias, H_sp, W_sp):
            b, L, cb = q.shape
            d = cb // BH
            scale = d ** (-0.5)

            def to_win(t):
                img = t.transpose(0, 2, 1).reshape(b, cb, H, W)
                w = _img2win(img, H_sp, W_sp)
                return w.reshape(-1, H_sp * W_sp, BH, d).transpose(0, 2, 1, 3)
            qw = to_win(q) * scale
            kw = to_win(k)
            vimg = v.transpose(0, 2, 1).reshape(b, cb, H // H_sp, H_sp, W // W_sp, W_sp)
            vwin = vimg.transpose(0, 2, 4, 1, 3, 5).reshape(-1, cb, H_sp, W_sp)
            lepe = jax.lax.conv_general_dilated(vwin, cw, (1, 1), 'SAME', feature_group_count=cb)
            lepe = lepe + cbias[None, :, None, None]
            lepe = lepe.reshape(-1, BH, d, H_sp * W_sp).transpose(0, 1, 3, 2)
            vw = vwin.reshape(-1, BH, d, H_sp * W_sp).transpose(0, 1, 3, 2)
            attn = jax.nn.softmax(jnp.einsum('whnd,whmd->whnm', qw, kw), axis=-1)
            o = jnp.einsum('whnm,whmd->whnd', attn, vw) + lepe
            o = o.transpose(0, 2, 1, 3).reshape(-1, H_sp * W_sp, cb)
            return _win2img(o, H_sp, W_sp)
        b = x.shape[0]
        t = x.reshape(b, C0, H * W).transpose(0, 2, 1)
        h = t @ w_embed
        img = _ln(h, g1, b1)
        qkv = (img @ w_qkv).reshape(b, H * W, 3, C).transpose(2, 0, 1, 3)
        q, k, v = (qkv[0], qkv[1], qkv[2])
        half = C // 2
        x1 = _lepe_attn(q[..., :half], k[..., :half], v[..., :half], conv_w0, conv_b0, H, SS)
        x2 = _lepe_attn(q[..., half:], k[..., half:], v[..., half:], conv_w1, conv_b1, SS, W)
        att = jnp.concatenate([x1, x2], axis=2) @ w_proj + b_proj
        h = h + att
        m = _ln(h, g2, b2)
        m = jax.nn.gelu(m @ w_fc1 + b_fc1, approximate=False) @ w_fc2 + b_fc2
        h = h + m
        y = h @ w_out
        return y.transpose(0, 2, 1).reshape(b, C0, H, W)

    def _L0_ffn_ref(x, router_w, router_b, expert_w, expert_b):
        import jax, jax.numpy as jnp
        import numpy as np
        B, N, D, C, E, K = (8, 8192, 128, 128, 8, 2)
        router_probs = jax.nn.softmax(x @ router_w + router_b, axis=-1)
        top_p, top_i = jax.lax.top_k(router_probs, K)
        top_p = top_p / jnp.sum(top_p, axis=-1, keepdims=True)
        expert_out = jnp.einsum('bnd,edc->bnec', x, expert_w) + expert_b
        gathered = jnp.take_along_axis(expert_out, top_i[..., None], axis=2)
        return jnp.einsum('bnk,bnkc->bnc', top_p, gathered)

    def _gn(v, G=32, eps=1e-5):
        B_, H_, W_, C_ = v.shape
        g = v.reshape(B_, H_, W_, G, C_ // G)
        m = jnp.mean(g, axis=(1, 2, 4), keepdims=True)
        s = jnp.var(g, axis=(1, 2, 4), keepdims=True)
        return ((g - m) / jnp.sqrt(s + eps)).reshape(v.shape)

    def _ln_c(v, eps=1e-6):
        m = jnp.mean(v, axis=-1, keepdims=True)
        s = jnp.var(v, axis=-1, keepdims=True)
        return (v - m) / jnp.sqrt(s + eps)

    def _ln_t(v, eps=1e-5):
        m = jnp.mean(v, axis=-1, keepdims=True)
        s = jnp.var(v, axis=-1, keepdims=True)
        return (v - m) / jnp.sqrt(s + eps)

    def _to_tokens(v):
        B_, H_, W_, C_ = v.shape
        return v.reshape(B_, H_ * W_, C_)
    def _from_tokens(t, like):
        return t.reshape(like.shape)

    x = x + _L0_conv_ref(_ln_c(x), L0_conv_w_embed, L0_conv_g1, L0_conv_b1, L0_conv_w_qkv, L0_conv_conv_w0, L0_conv_conv_b0, L0_conv_conv_w1, L0_conv_conv_b1, L0_conv_w_proj, L0_conv_b_proj, L0_conv_g2, L0_conv_b2, L0_conv_w_fc1, L0_conv_b_fc1, L0_conv_w_fc2, L0_conv_b_fc2, L0_conv_w_out)
    t = _to_tokens(x)
    t = t + _L0_ffn_ref(_ln_t(t), L0_ffn_router_w, L0_ffn_router_b, L0_ffn_expert_w, L0_ffn_expert_b)
    x = _from_tokens(t, x)
    return x


_drawn_inputs = setup_inputs


def setup_inputs(seed=0):
    import zlib

    import numpy as np

    out = dict(_drawn_inputs(seed))
    spreads = {'L0_conv_b_fc1': (0.0, 1.193),
     'L0_conv_b_fc2': (0.0, 0.47),
     'L0_ffn_router_b': (0.0, 0.1),
     'L0_ffn_expert_b': (0.0, 0.295)}
    factors = {'L0_conv_g1': 8.0,
     'L0_conv_b1': 8.0,
     'L0_conv_w_qkv': 4.535,
     'L0_conv_conv_w0': 6.375,
     'L0_conv_conv_b0': 34.957,
     'L0_conv_conv_w1': 6.815,
     'L0_conv_conv_b1': 39.438,
     'L0_conv_w_proj': 5.123,
     'L0_conv_b_proj': 23.762,
     'L0_conv_g2': 163.707,
     'L0_conv_b2': 200.0}
    for name, (base, spread) in spreads.items():
        noise = np.random.default_rng([zlib.crc32(name.encode()), seed]).standard_normal(out[name].shape)
        drawn = base * np.exp(spread * noise) if base else spread * noise
        out[name] = jnp.asarray(drawn.astype(out[name].dtype))
    for name, factor in factors.items():
        out[name] = (out[name] * factor).astype(out[name].dtype)
    return out
```

```python
from contextlib import ExitStack

import concourse.bass as bass
from concourse import mybir

F32 = mybir.dt.float32
FP16 = mybir.dt.float16
ALU = mybir.AluOpType
ACT = mybir.ActivationFunctionType
AX = mybir.AxisListType

P = 128
B, C0, H, W = 4, 64, 128, 128
C = 2 * C0
NBR = 2
HB = C // 2
NH = 4
D = HB // NH
SS = 4
WT = H * SS
NW = H // SS
TOK = H * W
KC = WT // P
FF = 4 * C
NF = FF // P
E = 8
U = NH * KC
CATQ = 4
PAIRS = 4 * D
MAXROW = 96
MAXUNIT = 1024.0
G8 = 8
STEPS = B * C0 // G8
DMA = 16
CAT_DMAS = 4 * NH


class Window:

    def __init__(self, b, it, k):
        self.branch = 1 if k >= NW else 0
        self.q = k % CATQ
        self.w = 4 * it + (k - NW * self.branch)
        self.g = b * (NBR * NW) + 4 * it + k
        before = [b * NW + (self.w if self.branch == br else NW * self.branch) for br in range(NBR)]
        self.conv_free = (2 * DMA * before[0], DMA * before[1])
        self._quads = b * (NBR * NW // 4) + it
        self._k = k

    def fills(self, back):
        return self._quads + (self._k - back) // 4 + 1


class Step:

    def __init__(self, it, k, u):
        self.i, self.k, self.fill = u * it + k, k % u, it + k // u + 1


def lookahead(eng, n, u, body):
    body(None, Step(0, 0, u))
    its = (n - 1) // u
    with eng.Fori(0, its) as it:
        for k in range(u):
            body(Step(it, k, u), Step(it, k + 1, u))
    for k in range(n - its * u):
        last = k == n - its * u - 1
        body(Step(its, k, u), None if last else Step(its, k + 1, u))


class Slot:

    def __init__(self, b, it, s, loop):
        def stage(ahead):
            c = s + ahead
            n = NBR * NW
            inside = loop or 0 <= c < n
            window = Window(b, it, c) if inside else None
            count = window.g if inside else b * n + min(max(c, 0), n)
            return window, count

        self.P, self.nP = stage(3)
        self.L, self.nL = stage(2)
        self.M, self.nM = stage(1)
        self.T, self.nT = stage(0)
        self.F, self.nF = stage(-1)


def pipeline(eng, b, body):
    for s in range(-3, 1):
        body(Slot(b, 0, s, False))
    with eng.Fori(0, 7) as it:
        for k in range(1, 5):
            body(Slot(b, it, k, True))
    for s in range(29, 33):
        body(Slot(b, 0, s, False))
    with eng.Fori(0, 7) as it:
        for k in range(1, 5):
            body(Slot(b, it, NW + k, True))
    for s in range(61, 65):
        body(Slot(b, 0, s, False))


def build(nc, x, w_embed, g1, b1, w_qkv, conv_w0, conv_b0, conv_w1, conv_b1, w_proj, b_proj, g2, b2,
          w_fc1, b_fc1, w_fc2, b_fc2, w_out, router_w, router_b, expert_w, expert_b, out):
    xn_d = nc.dram_tensor("xn_scratch", (B * C0, H, W), F32).ap()
    x2_d = nc.dram_tensor("x2_scratch", (B * C0, H, W), F32).ap()
    conv0_d = nc.dram_tensor("conv0_scratch", (B, NW, HB, WT), F32).ap()
    conv1_d = nc.dram_tensor("conv1_scratch", (B, NW, 2, HB, WT // 2), F32).ap()
    x_rows = x.rearrange("b c h m -> (b c) h m")
    out_rows = out.rearrange("b c h m -> (b c) h m")

    with ExitStack() as ctx:
        def sb(name, shape, dt=F32):
            return ctx.enter_context(nc.sbuf_tensor(name, shape, dt))

        def sem(name):
            return ctx.enter_context(nc.semaphore(name))

        imgT = sb("imgT", [P, TOK])
        att0 = sb("att0", [P, TOK])
        work = sb("work", [P, 12288])
        vaug = sb("vaug", [P, 4, KC, NH, 32])
        parts = sb("parts", [P, 2, 2, WT], FP16)
        o_sb = sb("o_sb", [P, WT])
        vT = [sb("vT0", [P, 66, 6]), sb("vT1", [P, 6, 66])]
        v_own = sb("v_own", [P, 256])
        cv_acc = sb("cv_acc", [P, 256])
        cv_tmp = sb("cv_tmp", [P, 256])
        cv_out = sb("cv_out", [P, 256])
        wqk = sb("wqk", [P, NBR, P])
        wv = sb("wv", [P, NBR, 2, P])
        ident = sb("ident", [P, P])
        wemb = sb("wemb", [C0, C])
        wpr = sb("wpr", [P, NBR, C])
        wprc = sb("wprc", [P, C])
        wout = sb("wout", [P, C0])
        cw = sb("cw", [P, NBR, 9])
        cb = sb("cb", [P, NBR])
        cols = sb("cols", [P, 10 + NF])
        mx = sb("mx", [P, 2, 32])
        mxh = sb("mxh", [P, U], FP16)
        mxb = sb("mxb", [2 * U, P], FP16)
        rec = sb("rec", [P, KC, NH])
        rec_wide = sb("rec_wide", [P, WT])
        stat = sb("stat", [P, 2, 8, 6])
        mv = sb("mv", [P, 2, 8, 2])
        lnr = sb("lnr", [P, 2, 4, 8])
        konst = sb("konst", [P, 6, 8])
        G1, B1, G2, B2, BP, BF2 = (cols[:, i:i + 1] for i in range(6))
        BF1 = [cols[:, 10 + i:11 + i] for i in range(NF)]
        EPS6, EPS5, NHALF, NEG1 = (konst[:, i, :] for i in range(4))
        RANK = konst[:, 5, :]

        workb = work[:, :].bitcast(FP16)
        qcat = workb[:, 0:8192].rearrange("p (q j n) -> p q j n", q=CATQ, j=NH)
        kcat = workb[:, 8192:16384].rearrange("p (q j n) -> p q j n", q=CATQ, j=NH)
        probs = work[:, 8192:12288].rearrange("p (u n) -> p u n", u=8)
        rows_in = work[:, 0:2048].rearrange("p (q t m) -> p q t m", q=2, t=G8)
        rows_out = work[:, 2048:4096].rearrange("p (q t m) -> p q t m", q=2, t=G8)
        xa = work[0:C0, 0:2048].rearrange("p (q n) -> p q n", q=4)
        ihat = work[:, 2048:3072].rearrange("p (q n) -> p q n", q=2)
        cx = work[:, 0:3072].rearrange("p (t q n) -> p t q n", t=3, q=2)
        cxo = work[0:C0, 3072:4096].rearrange("p (q n) -> p q n", q=2)
        c_hT = work[:, 4096:5120].rearrange("p (q n) -> p q n", q=2)
        c_nh, c_mT, c_hfin = work[:, 5120:5632], work[:, 5632:6144], work[:, 8192:8704]
        c_g = work[:, 6144:8192].rearrange("p (f n) -> p f n", f=NF)
        fc1 = work[:, 8704:9216]
        fc2 = work[:, 9216:9728].rearrange("p (f n) -> p f n", f=NF)
        d_x = work[:, 0:2048].rearrange("p (q t m) -> p q t m", q=2, t=G8)
        d_acc = work[:, 2048:4096].rearrange("p (q t m) -> p q t m", q=2, t=G8)
        d_xl = work[:, 4096:5120].rearrange("p (t m) -> p t m", t=G8)
        d_xT = work[:, 5120:7168].rearrange("p (q t m) -> p q t m", q=2, t=G8)
        d_ew = work[:, 7168:8192].rearrange("p (e m) -> p e m", e=E)
        d_eb = work[0:E * G8, 8192:9216].rearrange("p (t m) -> p t m", t=G8)
        d_gT = work[0:E * G8, 9216:9344]
        d_gate = work[:, 9344:9472].rearrange("p (q t e) -> p q t e", q=2, t=G8)
        d_t = work[:, 9472:9792].rearrange("p (i t e) -> p i t e", i=5, t=G8)
        d_s = work[:, 9792:9856].rearrange("p (i t) -> p i t", i=8)
        d_rw, d_rb = work[:, 9856:9864], work[:, 9864:9872]

        ps = ctx.enter_context(nc.psum_tensor("ps", [P, 8, 512], F32))
        bank = [ps[:, i, :] for i in range(8)]
        SM, ST, O, X0, X1, X2 = bank[0:2], bank[2:4], bank[4], bank[5], bank[6], bank[7]
        EA, TB = bank[0:2], bank[2:4]
        CH, CT, CF, CM, CY = bank[0:2], bank[2], bank[3:5], bank[5], bank[6]
        DT, DL, DB, DY = bank[0:2], bank[2][:, 0:E * G8], bank[3], [ps[:, 4:6, :], ps[:, 6:8, :]]

        s_settled = sem("settled")
        s_phase = sem("phase")
        s_w, s_fc, d_w = sem("weights"), sem("mlp_weights"), sem("expert_weights")
        n_ld = [sem(f"n_load{i}") for i in range(2)]
        n_st = [sem(f"n_written{i}") for i in range(2)]
        a_ld = [sem(f"a_load{i}") for i in range(4)]
        s_cat = [sem(f"cat_filled{i}") for i in range(CATQ)]
        s_mrow = sem("max_rows_filled")
        s_cvd0, s_cvd1 = sem("conv0_written"), sem("conv1_written")
        c_ld = [sem(f"c_load{i}") for i in range(2)]
        c_st = [sem(f"c_written{i}") for i in range(2)]
        d_ld = [sem(f"d_load{i}") for i in range(2)]
        d_st = [sem(f"d_written{i}") for i in range(2)]
        SP_OWNS = {DMA: n_st + s_cat + [s_mrow, s_cvd0, s_cvd1] + c_st + d_st}

        s_qk, s_vt, s_vk = sem("qk_made"), sem("vT_made"), sem("v_by_key_made")
        s_mxt, s_sm, s_st = sem("max_turned"), sem("max_scores"), sem("scores")
        s_pv, s_ot, s_bt = sem("values_summed"), sem("out_turned"), sem("recip_spread")
        a_e, a_tr = sem("a_embedded"), sem("a_turned")
        c_h, c_t1, c_t2 = sem("c_h"), sem("c_turned"), sem("c_turned_back")
        c_f1, c_f2, c_y = sem("c_fc1"), sem("c_fc2"), sem("c_y")
        d_tr, d_lg, d_gt = sem("d_turned"), sem("d_logits"), sem("d_gates_turned")
        d_bm, d_y = sem("d_bias_made"), sem("d_experts")
        PE_OWNS = {1: [s_vk, s_bt, c_t2, c_f1, c_f2, c_y, d_tr, d_bm],
                   2: [s_mxt, a_tr, d_gt],
                   4: [a_e],
                   16: [s_pv, d_y],
                   64: [s_st]}

        s_qs, s_exp = sem("q_scaled"), sem("exp_done")
        s_hb = sem("high_part")
        s_vte, s_vke, s_mxe = sem("vT_stored"), sem("v_by_key_stored"), sem("max_stored")
        s_oev = sem("out_stored")
        n_nm, a_ev = sem("n_normed"), sem("a_image")
        c_hs, c_gl, c_m = sem("c_h_stored"), sem("c_gelu"), sem("c_mlp_in")
        d_nm, d_xt, d_gte, d_e2 = sem("d_normed"), sem("d_xT"), sem("d_gT"), sem("d_exp")
        ACT_OWNS = {1: [s_vte, s_vke, s_mxe, s_oev, c_m, d_xt, d_gte, d_e2],
                    2: [s_exp, n_nm, a_ev, c_hs, c_gl, d_nm]}

        s_dz, s_set, d_set = sem("zeros_set"), sem("constants_set"), sem("d_zeros_set")
        s_red, s_mh, s_mxs = sem("tile_max"), sem("max_high"), sem("max_split")
        s_lo, s_rec, s_att = sem("low_part"), sem("recip_done"), sem("att_stored")
        s_rw = sem("recip_widened")
        n_bn, n_mv, a_bn, a_mv = sem("n_stats"), sem("n_moments"), sem("a_stats"), sem("a_moments")
        c_bn, c_mv, d_bn, d_mv = sem("c_stats"), sem("c_moments"), sem("d_stats"), sem("d_moments")
        a_nm, c_nm, c_hf, c_xo = sem("a_normed"), sem("c_normed"), sem("c_sum"), sem("c_x_out")
        d_gs, d_df, d_g = sem("d_gate_step"), sem("d_logit_gap"), sem("d_gates")
        d_bi, d_ac, d_cb = sem("d_bias_added"), sem("d_expert_added"), sem("d_combined")
        DVE_OWNS = {1: [s_lo, s_rec, s_att, c_xo, d_g, d_bi],
                    2: [s_red, a_nm, c_nm, c_hf, d_cb]}

        s_id, s_kset = sem("identity_set"), sem("fixed_rows_set")
        s_cv, s_cvc = sem("conv_done"), sem("conv_step")
        n_ln, n_rs, a_ln, a_rs = sem("n_ln_step"), sem("n_rstd"), sem("a_ln_step"), sem("a_rstd")
        c_ln, c_rs, d_ln, d_rs = sem("c_ln_step"), sem("c_rstd"), sem("d_ln_step"), sem("d_rstd")
        POOL_OWNS = {1: [s_cv],
                     2: [n_rs, d_rs]}

        block = ctx.enter_context(nc.Block())
        ENGINES = 5

        def settle(eng):
            eng.sem_inc(s_settled, 1)

        def phase_end(eng, n):
            settle(eng)
            eng.drain().then_inc(s_phase, 1)
            eng.wait_ge(s_phase, ENGINES * n)
            settle(eng)

        n_weights = 37

        def start_up(eng, owns):
            for start, sems in owns.items():
                for s in sems:
                    eng.sem_inc(s, start)

        def qk_view(win):
            if win.branch == 0:
                return imgT[:, :].rearrange("p (h m c) -> p h m c", m=NW, c=SS)[:, :, win.w, :]
            return imgT[:, bass.ds(win.w * WT, WT)].rearrange("p (y a c) -> p a y c", y=SS, a=2)

        def half_view(win, a):
            if win.branch == 0:
                return imgT[:, :].rearrange("p (h m c) -> p h m c", m=NW, c=SS)[:, 63 * a:63 * a + 65, win.w, :]
            return imgT[:, bass.ds(win.w * WT, WT)].rearrange("p (y c) -> p y c", y=SS)[:, :, 63 * a:63 * a + 65]

        def vt_psum(win, a):
            lo = 1 - a
            if win.branch == 0:
                return X1[:, 0:264].rearrange("p (y c) -> p y c", c=SS)[:, lo:lo + 65, :]
            return X1[:, 0:264].rearrange("p (y c) -> p y c", y=SS)[:, :, lo:lo + 65]

        def by_column(ap):
            return ap.rearrange("p (y m c) -> p m y c", y=SS, m=NW)

        @block.sync
        def _(sp):
            start_up(sp, SP_OWNS)

            def load(dst, src):
                sp.dma_start(dst, src).then_inc(s_w, DMA)

            sp.wait_ge(s_set, 1)
            load(wemb[:, :], w_embed)
            load(wout[:, :], w_out)
            load(wprc[:, :], w_proj)
            for br in range(NBR):
                load(wqk[:, br, 0:HB], w_qkv[:, HB * br:HB * br + HB])
                load(wqk[:, br, HB:P], w_qkv[:, C + HB * br:C + HB * br + HB])
                for a in range(2):
                    load(wv[:, br, a, HB * a:HB * a + HB], w_qkv[:, 2 * C + HB * br:2 * C + HB * br + HB])
                    load(cw[HB * a:HB * a + HB, br, :],
                         (conv_w0, conv_w1)[br].rearrange("c o y s -> c (o y s)"))
                    load(cb[HB * a:HB * a + HB, br:br + 1], (conv_b0, conv_b1)[br].rearrange("(c o) -> c o", o=1))
                for j in range(NH):
                    load(wpr[32 * j:32 * j + D, br, :], w_proj[HB * br + D * j:HB * br + D * j + D, :])
            for i, v in enumerate((g1, b1, g2, b2, b_proj, b_fc2)):
                load(cols[:, i:i + 1], v.rearrange("(c o) -> c o", o=1))
            for f in range(NF):
                load(cols[:, 10 + f:11 + f], b_fc1[P * f:P * f + P].rearrange("(c o) -> c o", o=1))

            def n_load(s, q):
                sp.dma_start(rows_in[:, q], x_rows[bass.ds(s * G8, G8)].rearrange("c h m -> h c m")) \
                    .then_inc(n_ld[q], DMA)

            def n_store(s, q):
                sp.wait_ge(n_nm, s + 3)
                settle(sp)
                sp.dma_start(xn_d[bass.ds(s * G8, G8)].rearrange("c h m -> h c m"), rows_out[:, q]) \
                    .then_inc(n_st[q], DMA)

            for q in range(2):
                n_load(q, q)
            with sp.Fori(0, STEPS // 2 - 1) as it:
                for q in range(2):
                    n_store(it * 2 + q, q)
                    n_load(it * 2 + q + 2, q)
            for q in range(2):
                n_store(STEPS - 2 + q, q)
            for q in range(2):
                sp.wait_ge(n_st[q], DMA * (STEPS // 2 + 1))
                settle(sp)
            phase_end(sp, 1)

            with sp.Fori(0, B) as b:
                with sp.Fori(0, NW // 4) as it:
                    for q in range(4):
                        i = it * 4 + q
                        sp.wait_ge(a_e, b * NW + i + 1)
                        settle(sp)
                        sp.dma_start(xa[:, q, :], xn_d[bass.ds(b * C0, C0), bass.ds(i * SS, SS), :]
                                     .rearrange("c y m -> c (y m)")).then_inc(a_ld[q], DMA)
                phase_end(sp, b * 3 + 2)

                def slot(t):
                    if t.L:
                        sp.wait_ge(s_cv, t.nL + 2)
                        settle(sp)
                        if t.L.branch == 0:
                            for a in range(2):
                                sp.dma_start(conv0_d[b, 16 * a:16 * a + 16, :, bass.ds(t.L.w * 16, 16)]
                                             .rearrange("i c x -> c i x"),
                                             cv_out[HB * a:HB * a + HB, :].rearrange("p (i x) -> p i x", x=16)) \
                                    .then_inc(s_cvd0, DMA)
                        else:
                            sp.dma_start(conv1_d[b, t.L.w].rearrange("a c n -> (a c) n"), cv_out[:, :]) \
                                .then_inc(s_cvd1, DMA)
                    if t.M:
                        sp.wait_ge(s_mxe, t.nM + 2)
                        settle(sp)
                        sp.dma_start(qcat[MAXROW:MAXROW + 2, t.M.q].rearrange("p j n -> p (j n)"), mxb[:, :]) \
                            .then_inc(s_mrow, DMA)
                    if t.P:
                        sp.wait_ge(s_lo, t.nP + 2)
                        settle(sp)
                        sp.wait_ge(s_st, U * (t.nP - 3) + 64)
                        settle(sp)
                        for j in range(NH):
                            for side, cat in ((0, qcat), (1, kcat)):
                                for half in range(2):
                                    s = parts[HB * side + D * j:HB * side + D * j + D, t.P.q % 2, :, :]
                                    rows = bass.AP(tensor=s.tensor, offset=s.offset + (0 if side else WT * half),
                                                   ap=[[s.ap[0][0], D], [WT if side else 0, 2], [1, WT]])
                                    sp.dma_start(cat[2 * D * half:2 * D * half + 2 * D, t.P.q, j, :], rows) \
                                        .then_inc(s_cat[t.P.q], DMA)

                pipeline(sp, b, slot)
                sp.wait_ge(s_cvd0, (b + 1) * (NW * 2 * DMA) + DMA)
                settle(sp)
                sp.wait_ge(s_cvd1, (b + 1) * (NW * DMA) + DMA)
                settle(sp)
                phase_end(sp, b * 3 + 3)

                sp.dma_start(fc1, w_fc1).then_inc(s_fc, DMA)
                sp.dma_start(fc2, w_fc2.rearrange("(f p) n -> p f n", p=P)).then_inc(s_fc, DMA)

                def c_load(i, q):
                    for t, src in enumerate((xn_d, x_rows)):
                        sp.dma_start(cx[0:C0, t, q, :], src[bass.ds(b * C0, C0), bass.ds(i * SS, SS), :]
                                     .rearrange("c y m -> c (y m)")).then_inc(c_ld[q], DMA)
                    sp.dma_start(cx[0:HB, 2, q, :], conv0_d[b, i]).then_inc(c_ld[q], DMA)
                    sp.dma_start(cx[HB:P, 2, q, :].rearrange("p (a n) -> p a n", a=2),
                                 conv1_d[b, i].rearrange("a c n -> c a n")).then_inc(c_ld[q], DMA)

                def c_store(i, q):
                    sp.wait_ge(c_xo, b * NW + i + 2)
                    settle(sp)
                    sp.dma_start(x2_d[bass.ds(b * C0, C0), bass.ds(i * SS, SS), :].rearrange("c y m -> c (y m)"),
                                 cxo[:, q, :]).then_inc(c_st[q], DMA)

                for q in range(2):
                    c_load(q, q)
                with sp.Fori(0, NW // 2 - 1) as it:
                    for q in range(2):
                        c_store(it * 2 + q, q)
                        c_load(it * 2 + q + 2, q)
                for q in range(2):
                    c_store(NW - 2 + q, q)
                for q in range(2):
                    sp.wait_ge(c_st[q], (b + 1) * (DMA * NW // 2) + DMA)
                    settle(sp)
                phase_end(sp, b * 3 + 4)

            def d_load(s, q):
                sp.dma_start(d_x[:, q], x2_d[bass.ds(s * G8, G8)].rearrange("c h m -> h c m")) \
                    .then_inc(d_ld[q], DMA)

            def d_store(s, q):
                sp.wait_ge(d_cb, G8 * (s + 1) + 2)
                settle(sp)
                sp.dma_start(out_rows[bass.ds(s * G8, G8)].rearrange("c h m -> h c m"), d_acc[:, q]) \
                    .then_inc(d_st[q], DMA)

            sp.dma_start(d_rw, router_w).then_inc(d_w, DMA)
            sp.dma_start(d_ew, expert_w.rearrange("e d c -> d e c")).then_inc(d_w, DMA)
            sp.wait_ge(d_set, 1)
            settle(sp)
            for t in range(G8):
                sp.dma_start(d_eb[E * t:E * t + E, t, :], expert_b).then_inc(d_w, DMA)
            sp.dma_start(d_rb, router_b.rearrange("(o e) -> o e", o=1).broadcast_to([P, E])) \
                .then_inc(d_w, DMA)
            for q in range(2):
                d_load(q, q)
            with sp.Fori(0, STEPS // 2 - 1) as it:
                for q in range(2):
                    d_store(it * 2 + q, q)
                    d_load(it * 2 + q + 2, q)
            for q in range(2):
                d_store(STEPS - 2 + q, q)
            for q in range(2):
                sp.wait_ge(d_st[q], DMA * (STEPS // 2 + 1))
                settle(sp)

        @block.tensor
        def _(pe):
            start_up(pe, PE_OWNS)
            phase_end(pe, 1)
            pe.wait_ge(s_w, DMA * n_weights)
            pe.wait_ge(s_id, 2)
            pe.wait_ge(s_qs, 1)
            with pe.Fori(0, B) as b:
                def a_step(cur, nxt):
                    if nxt:
                        n = b * NW + nxt.i
                        pe.wait_ge(a_ld[nxt.k], DMA * (b * (NW // 4) + nxt.fill))
                        pe.wait_ge(a_nm, n + 1)
                        for t in range(4):
                            mm = pe.matmul(EA[nxt.k % 2][:, P * t:P * t + P], xa[:, nxt.k, P * t:P * t + P],
                                           wemb[:, :], start=True, stop=True)
                        mm.then_inc(a_e, 1)
                    if cur:
                        n = b * NW + cur.i
                        pe.wait_ge(a_nm, n + 3)
                        pe.wait_ge(a_ev, n + 1)
                        for t in range(4):
                            mm = pe.transpose(TB[cur.k % 2][:, P * t:P * t + P],
                                              ihat[:, cur.k % 2, P * t:P * t + P], ident[:, :])
                        mm.then_inc(a_tr, 1)

                lookahead(pe, NW, 4, a_step)
                phase_end(pe, b * 3 + 2)
                pe.wait_ge(s_kset, b + 1)

                def scores_for_max(t, k):
                    j, i = k // KC, k % KC
                    if k == 0:
                        pe.wait_ge(s_cat[t.M.q], DMA * CAT_DMAS * t.M.fills(0) + DMA)
                    pe.wait_ge(s_red, U * t.nM + k + 1)
                    pe.matmul(SM[k % 2], qcat[0:MAXROW, t.M.q, j, P * i:P * i + P], kcat[0:MAXROW, t.M.q, j, :],
                              start=True, stop=True).then_inc(s_sm, 1)

                def scores(t, u):
                    i, j = u // NH, u % NH
                    if u == 0:
                        pe.wait_ge(s_mrow, DMA * (t.nT + 2))
                    pe.wait_ge(s_exp, U * t.nT + u + 1)
                    pe.matmul(ST[u % 2], kcat[0:MAXROW + 2, t.T.q, j, P * i:P * i + P],
                          qcat[0:MAXROW + 2, t.T.q, j, :],
                              start=True, stop=True).then_inc(s_st, 1)

                def values(t, g):
                    if g == 0:
                        pe.wait_ge(s_vke, t.nT + 2)
                        pe.wait_ge(s_oev, t.nT + 1)
                    pe.wait_ge(s_exp, U * t.nT + NH * g + NH + 2)
                    for j in range(NH):
                        mm = pe.matmul(O[32 * j:32 * j + 32, :], vaug[:, t.T.q, 2 * (g % 2) + g // 2, j, :],
                                       probs[:, (NH * g + j) % 8, :], start=(g == 0), stop=(g == KC - 1),
                                       tile_position=(0, 32 * j), skip_group_check=True)
                    mm.then_inc(s_pv, 1)

                def slot(t):
                    if t.F:
                        pe.wait_ge(s_oev, t.nF + 2)
                        pe.wait_ge(s_lo, t.nP + 1)
                        pe.wait_ge(s_rec, t.nF + 1)
                        for c in range(KC):
                            mm = pe.transpose(X0[:, P * c:P * c + P], o_sb[:, P * c:P * c + P], ident[:, :])
                        mm.then_inc(s_ot, 1)
                    sm = 0
                    for g in range(KC):
                        for j in range(NH):
                            if t.T:
                                scores(t, NH * g + j)
                            if t.M and sm < U:
                                scores_for_max(t, sm)
                                sm += 1
                        if t.M and sm < U and g < 3:
                            for _ in range(1 if g < 2 else 2):
                                if sm < U:
                                    scores_for_max(t, sm)
                                    sm += 1
                        if t.T and g > 0:
                            values(t, g - 1)
                        if g == 0 and t.F:
                            pe.wait_ge(s_rw, t.nF + 1)
                            pe.wait_ge(s_vte, t.nP + 1)
                            pe.wait_ge(s_att, t.nF + 1)
                            for c in range(KC):
                                mm = pe.transpose(X1[:, P * c:P * c + P],
                                                  rec_wide[:, P * c:P * c + P], ident[:, :])
                            mm.then_inc(s_bt, 1)
                        if g == 2 and t.P:
                            pe.wait_ge(s_lo, t.nP + 1)
                            pe.wait_ge(s_rec, t.nF + (1 if t.F else 0) + 1)
                            pe.matmul(X0, wqk[:, t.P.branch, :], qk_view(t.P), start=True, stop=True) \
                                .then_inc(s_qk, 1)
                    if t.M:
                        pe.wait_ge(s_mxs, t.nM + 1)
                        pe.wait_ge(s_mxe, t.nM + 1)
                        pe.wait_ge(s_vke, t.nP + 1)
                        pe.transpose(X2[0:2 * U, 0:P], mx[:, t.M.q % 2, :], ident[:, :]).then_inc(s_mxt, 1)
                    if t.P:
                        pe.wait_ge(s_vte, t.nP + 1)
                        pe.wait_ge(s_att, t.nF + (1 if t.F else 0) + 1)
                        for a in range(2):
                            mm = pe.matmul(vt_psum(t.P, a), wv[:, t.P.branch, a, :], half_view(t.P, a),
                                           start=(a == 0), stop=(a == 1), skip_group_check=True)
                        mm.then_inc(s_vt, 1)
                    if t.T:
                        values(t, KC - 1)
                    if t.P:
                        pe.wait_ge(s_vte, t.nP + 2)
                        pe.wait_ge(s_mxe, t.nM + (1 if t.M else 0) + 1)
                        pe.wait_ge(s_vke, t.nP + 1)
                        for i in range(2):
                            mm = pe.transpose(X2[:, P * i:P * i + P], v_own[:, P * i:P * i + P], ident[:, :])
                        mm.then_inc(s_vk, 1)

                pipeline(pe, b, slot)
                phase_end(pe, b * 3 + 3)
                pe.wait_ge(s_fc, (b + 1) * 2 * DMA)

                def c_step(cur, nxt):
                    if nxt:
                        n = b * NW + nxt.i
                        pe.wait_ge(c_ld[nxt.k], 4 * DMA * (b * (NW // 2) + nxt.fill))
                        pe.wait_ge(c_hs, n + 1)
                        terms = [(wemb[:, :], by_column(cx[0:C0, 0, nxt.k, :])),
                                 (wpr[:, 0, :], att0[:, :].rearrange("p (m i x) -> p m i x", m=NW, i=NW)[:, :, nxt.i, :]),
                                 (wpr[:, 1, :], by_column(imgT[:, bass.ds(nxt.i * WT, WT)])),
                                 (wprc[:, :], cx[:, 2, nxt.k, :])]
                        for m, (w, v) in enumerate(terms):
                            mm = pe.matmul(CH[nxt.k], w, v, start=(m == 0), stop=(m == 3))
                        mm.then_inc(c_h, 1)
                    if cur:
                        n = b * NW + cur.i
                        pe.wait_ge(c_m, n + 2)
                        for f in range(NF):
                            pe.wait_ge(c_gl, NF * n + f + 1)
                            pe.matmul(CF[f % 2], fc1[:, P * f:P * f + P], c_mT, start=True, stop=True) \
                                .then_inc(c_f1, 1)
                    if nxt:
                        n = b * NW + nxt.i
                        pe.wait_ge(c_hs, n + 3)
                        pe.wait_ge(c_m, n + 1)
                        for t in range(4):
                            mm = pe.transpose(CT[:, P * t:P * t + P], c_hT[:, nxt.k, P * t:P * t + P], ident[:, :])
                        mm.then_inc(c_t1, 1)
                    if cur:
                        n = b * NW + cur.i
                        pe.wait_ge(c_hf, n + 2)
                        for f in range(NF):
                            pe.wait_ge(c_gl, NF * n + f + 3)
                            mm = pe.matmul(CM, fc2[:, f, :], c_g[:, f, :], start=(f == 0), stop=(f == NF - 1))
                        mm.then_inc(c_f2, 1)
                    if nxt:
                        pe.wait_ge(c_nm, b * NW + nxt.i + 3)
                        for t in range(4):
                            mm = pe.transpose(CT[:, P * t:P * t + P], c_nh[:, P * t:P * t + P], ident[:, :])
                        mm.then_inc(c_t2, 1)
                    if cur:
                        n = b * NW + cur.i
                        pe.wait_ge(c_hf, n + 3)
                        pe.wait_ge(c_xo, n + 1)
                        pe.matmul(CY[0:C0, :], wout[:, :], c_hfin, start=True, stop=True).then_inc(c_y, 1)

                lookahead(pe, NW, 2, c_step)
                phase_end(pe, b * 3 + 4)

            pe.wait_ge(d_w, DMA * (G8 + 3))

            def d_step(cur, nxt):
                if nxt:
                    pe.wait_ge(d_nm, nxt.i + 3)
                    pe.wait_ge(d_xt, 2 * nxt.i + 1)
                    for h in range(2):
                        for t in range(4):
                            mm = pe.transpose(DT[h][:, P * t:P * t + P], d_xl[:, 4 * h + t, :], ident[:, :])
                        mm.then_inc(d_tr, 1)
                if nxt:
                    pe.wait_ge(d_xt, 2 * nxt.i + 3)
                    pe.wait_ge(d_g, nxt.i + 1)
                    for t in range(G8):
                        mm = pe.matmul(DL[:, E * t:E * t + E], d_xT[:, nxt.k, t, :], d_rw, start=True, stop=True)
                    mm.then_inc(d_lg, 1)
                if cur:
                    pe.wait_ge(d_g, cur.i + 2)
                    pe.wait_ge(d_bi, 2 * cur.i + 1)
                    settle(pe)
                    pe.transpose(DB[0:E * G8, 0:P], d_gate[:, cur.k, :, :].rearrange("p t e -> p (t e)"),
                                 ident[:, :]).then_inc(d_gt, 1)
                    for t in range(G8):
                        if t < 2:
                            pe.wait_ge(d_gte, cur.i + 2)
                            pe.wait_ge(d_bi, 2 * cur.i + t + 1)
                            pe.matmul(DB, d_gT, d_eb[:, 4 * t:4 * t + 4, :].rearrange("p t n -> p (t n)"),
                                      start=True, stop=True).then_inc(d_bm, 1)
                        pe.wait_ge(d_cb, G8 * cur.i + t + 1)
                        for h in range(2):
                            mm = pe.matmul(DY[t % 2][:, h, :], d_xT[:, cur.k, t, :],
                                           d_ew[:, 4 * h:4 * h + 4, :].rearrange("p e n -> p (e n)"),
                                           start=True, stop=True)
                        mm.then_inc(d_y, 1)

            lookahead(pe, STEPS, 2, d_step)

        @block.scalar
        def _(act):
            start_up(act, ACT_OWNS)
            act.wait_ge(s_w, DMA * n_weights)
            act.mul(wqk[:, :, 0:HB], wqk[:, :, 0:HB], float(D) ** -0.5).then_inc(s_qs, 1)

            def n_step(cur, nxt):
                if cur:
                    act.wait_ge(n_rs, cur.i + 3)
                    act.wait_ge(n_st[cur.k], DMA * cur.fill)
                    for t in range(G8):
                        a = act.activation(rows_out[:, cur.k, t, :], rows_in[:, cur.k, t, :], ACT.Identity,
                                           bias=lnr[:, cur.k, 3, t:t + 1], scale=lnr[:, cur.k, 1, t:t + 1])
                    a.then_inc(n_nm, 1)

            lookahead(act, STEPS, 2, n_step)
            phase_end(act, 1)
            with act.Fori(0, B) as b:
                def a_step(cur, nxt):
                    if cur:
                        act.wait_ge(a_tr, b * NW + cur.i + 3)
                        act.activation(imgT[:, bass.ds(cur.i * WT, WT)], TB[cur.k % 2], ACT.Identity,
                                       bias=B1, scale=G1).then_inc(a_ev, 1)

                lookahead(act, NW, 4, a_step)
                phase_end(act, b * 3 + 2)

                def exponentials(t, u):
                    if u % NH == 0:
                        act.wait_ge(s_pv, KC * t.nT + u // NH + 15)
                    act.wait_ge(s_st, U * t.nT + u + 65)
                    act.activation(probs[:, u % 8, :], ST[u % 2], ACT.Exp).then_inc(s_exp, 1)

                def slot(t):
                    if t.T:
                        for u in range(12):
                            exponentials(t, u)
                    if t.P:
                        act.wait_ge(s_qk, t.nP + 1)
                        act.wait_ge(s_cat[(t.P.q + 2) % CATQ], DMA * CAT_DMAS * t.P.fills(2) + DMA)
                        act.copy(parts[:, t.P.q % 2, 0, :], X0).then_inc(s_hb, 1)
                    if t.T:
                        for u in range(12, U):
                            exponentials(t, u)
                    if t.M:
                        act.wait_ge(s_mxt, t.nM + 3)
                        act.wait_ge(s_mrow, DMA * (t.nM + 1))
                        act.mul(mxb[:, :], X2[0:2 * U, 0:P], 1 / MAXUNIT).then_inc(s_mxe, 1)
                    if t.P:
                        act.wait_ge(s_vt, t.nP + 1)
                        act.wait_ge(s_cv, t.nP + 1)
                        act.wait_ge(s_vk, t.nP + 1)
                        if t.P.branch == 0:
                            padded, made = vT[0][:, :, 1:5], X1[:, 0:264].rearrange("p (y c) -> p y c", c=SS)
                            own, inner = v_own[:, :].rearrange("p (y c) -> p y c", c=SS), made[:, 1:65, :]
                        else:
                            padded, made = vT[1][:, 1:5, :], X1[:, 0:264].rearrange("p (y c) -> p y c", y=SS)
                            own, inner = v_own[:, :].rearrange("p (y c) -> p y c", y=SS), made[:, :, 1:65]
                        act.copy(own, inner)
                        act.copy(padded, made).then_inc(s_vte, 1)
                    if t.T:
                        act.wait_ge(s_pv, KC * t.nT + KC + 16)
                        act.wait_ge(s_att, t.nT + 1)
                        act.copy(o_sb[:, :], O).then_inc(s_oev, 1)
                    if t.P:
                        act.wait_ge(s_vk, t.nP + 2)
                        act.wait_ge(s_pv, KC * (t.nP - 3) + 16)
                        act.copy(vaug[:, t.P.q, :, :, 0:D],
                                 X2[:, 0:KC * HB].rearrange("p (c j d) -> p c j d", c=KC, j=NH)) \
                            .then_inc(s_vke, 1)

                pipeline(act, b, slot)
                phase_end(act, b * 3 + 3)

                def c_step(cur, nxt):
                    if nxt:
                        n = b * NW + nxt.i
                        act.wait_ge(c_h, n + 1)
                        act.wait_ge(c_hf, n + 1)
                        act.activation(c_hT[:, nxt.k, :], CH[nxt.k], ACT.Identity, bias=BP, scale=1.0) \
                            .then_inc(c_hs, 1)
                    if cur:
                        n = b * NW + cur.i
                        act.wait_ge(c_f2, n + 1)
                        for f in range(NF):
                            act.wait_ge(c_f1, NF * n + f + 2)
                            act.activation(c_g[:, f, :], CF[f % 2], ACT.Gelu, bias=BF1[f]).then_inc(c_gl, 1)
                    if nxt:
                        n = b * NW + nxt.i
                        act.wait_ge(c_t2, n + 2)
                        act.wait_ge(c_f1, NF * n + 1)
                        act.activation(c_mT, CT, ACT.Identity, bias=B2, scale=G2).then_inc(c_m, 1)

                lookahead(act, NW, 2, c_step)
                phase_end(act, b * 3 + 4)

            def d_step(cur, nxt):
                if nxt:
                    act.wait_ge(d_rs, nxt.i + 3)
                    act.wait_ge(d_tr, 2 * nxt.i + 1)
                    for t in range(G8):
                        a = act.activation(d_xl[:, t, :], d_x[:, nxt.k, t, :], ACT.Identity,
                                           bias=lnr[:, nxt.k, 3, t:t + 1], scale=lnr[:, nxt.k, 1, t:t + 1])
                    a.then_inc(d_nm, 1)
                    for h in range(2):
                        act.wait_ge(d_tr, 2 * nxt.i + h + 2)
                        act.wait_ge(d_y, G8 * (nxt.i - 1) + 16)
                        act.copy(d_xT[:, nxt.k, 4 * h:4 * h + 4, :].rearrange("p t n -> p (t n)"), DT[h]) \
                            .then_inc(d_xt, 1)
                if cur:
                    act.wait_ge(d_gt, cur.i + 3)
                    act.wait_ge(d_bm, 2 * cur.i + 1)
                    act.copy(d_gT, DB[0:E * G8, 0:P]).then_inc(d_gte, 1)
                if nxt:
                    act.wait_ge(d_df, nxt.i + 1)
                    act.activation(d_s[:, 1, :], d_s[:, 0, :], ACT.Exp).then_inc(d_e2, 1)

            lookahead(act, STEPS, 2, d_step)

        @block.vector
        def _(dve):
            start_up(dve, DVE_OWNS)
            for tile in (wpr, wv, vT[0], vT[1], vaug):
                shape = tile.shape
                dve.memset(tile[tuple(slice(None) for _ in shape)], 0.0).then_inc(s_dz, 1)
            dve.wait_ge(s_dz, 5)
            dve.memset(vaug[:, :, :, :, D:D + 1], 1.0)
            for i, v in enumerate((1e-6, 1e-5, -0.5, -1.0, 0.0)):
                dve.memset(konst[:, i, :], v)
            for e in range(E):
                dve.memset(konst[:, 5, e:e + 1], float(E - e))
            dve.drain().then_inc(s_set, 1)

            def moments(tiles, k, stats_sem, moments_sem, n):
                for t, tile in enumerate(tiles):
                    a = dve.bn_stats(stat[:, k, t, :], tile)
                a.then_inc(stats_sem, 1)
                dve.wait_ge(stats_sem, n + 1)
                settle(dve)
                for t in range(len(tiles)):
                    a = dve.bn_aggr(mv[:, k, t, :], stat[:, k, t, :])
                a.then_inc(moments_sem, 1)

            def n_step(cur, nxt):
                if nxt:
                    dve.wait_ge(n_ld[nxt.k], DMA * nxt.fill)
                    dve.wait_ge(n_rs, nxt.i + 1)
                    moments([rows_in[:, nxt.k, t, :] for t in range(G8)], nxt.k, n_bn, n_mv, nxt.i)

            lookahead(dve, STEPS, 2, n_step)
            phase_end(dve, 1)
            with dve.Fori(0, B) as b:
                def a_step(cur, nxt):
                    if nxt:
                        n = b * NW + nxt.i
                        dve.wait_ge(a_e, n + 5)
                        moments([EA[nxt.k % 2][:, P * t:P * t + P] for t in range(4)], nxt.k % 2, a_bn, a_mv, n)
                    if cur:
                        n = b * NW + cur.i
                        q = cur.k % 2
                        dve.wait_ge(a_rs, n + 1)
                        dve.wait_ge(a_tr, n + 1)
                        for t in range(4):
                            a = dve.tensor_scalar(ihat[:, q, P * t:P * t + P], EA[q][:, P * t:P * t + P],
                                                  lnr[:, q, 1, t:t + 1], lnr[:, q, 3, t:t + 1], ALU.mult, ALU.add)
                        a.then_inc(a_nm, 1)

                lookahead(dve, NW, 4, a_step)
                phase_end(dve, b * 3 + 2)

                def tile_max(t, k):
                    if k == 0:
                        dve.wait_ge(s_mxt, t.nM + 1)
                    j, i = k // KC, k % KC
                    dve.wait_ge(s_sm, U * t.nM + k + 1)
                    dve.tensor_reduce(mx[:, t.M.q % 2, k:k + 1], SM[k % 2], AX.X, ALU.max, negate=True) \
                        .then_inc(s_red, 1)

                def slot(t):
                    if t.M:
                        for k in range(3):
                            tile_max(t, k)
                    if t.F:
                        dve.wait_ge(s_ot, t.nF + 1)
                        dve.wait_ge(s_bt, t.nF + 1)
                        dve.reciprocal(rec[:, :, :], X0.rearrange("p (c j x) -> p c j x", c=KC, j=NH)[:, :, :, D]) \
                            .then_inc(s_rec, 1)
                        dve.wait_ge(s_rec, t.nF + 2)
                        dve.tensor_copy(rec_wide[:, :].rearrange("p (c j x) -> p (c j) x", c=KC, j=NH),
                                        rec[:, :, :].rearrange("p c j -> p (c j)").unsqueeze(2)
                                        .broadcast_to([P, KC * NH, 32])).then_inc(s_rw, 1)
                    if t.M:
                        for k in range(3, 9):
                            tile_max(t, k)
                    if t.F:
                        dve.wait_ge(s_bt, t.nF + 2)
                        if t.F.branch == 0:
                            dst, fold = att0[:, bass.ds(t.F.w * WT, WT)], lambda v: v
                        else:
                            dst = imgT[:, bass.ds(t.F.w * WT, WT)].rearrange("p (y a c) -> p a y c", y=SS, a=2)
                            fold = lambda v: v.rearrange("p (a y c) -> p a y c", a=2, y=SS)
                        dve.tensor_tensor(dst, fold(o_sb[:, :]), fold(X1), ALU.mult).then_inc(s_att, 1)
                    if t.M:
                        for k in range(9, U):
                            tile_max(t, k)
                        m = mx[:, t.M.q % 2, :]
                        dve.wait_ge(s_red, U * t.nM + U + 2)
                        dve.tensor_scalar(mxh[:, :], m[:, 0:U], 1 / MAXUNIT, None, ALU.mult).then_inc(s_mh, 1)
                        dve.wait_ge(s_mh, t.nM + 1)
                        dve.scalar_tensor_tensor(out=m[:, U:2 * U], in0=mxh[:, :], scalar=-MAXUNIT, in1=m[:, 0:U],
                                                 op0=ALU.mult, op1=ALU.add).then_inc(s_mxs, 1)
                    if t.P:
                        dve.wait_ge(s_hb, t.nP + 1)
                        dve.tensor_tensor(parts[:, t.P.q % 2, 1, :], X0, parts[:, t.P.q % 2, 0, :], ALU.subtract) \
                            .then_inc(s_lo, 1)

                pipeline(dve, b, slot)
                phase_end(dve, b * 3 + 3)

                def c_step(cur, nxt):
                    if nxt:
                        n = b * NW + nxt.i
                        dve.wait_ge(c_t1, n + 1)
                        moments([CT[:, P * t:P * t + P] for t in range(4)], nxt.k, c_bn, c_mv, n)
                        dve.wait_ge(c_rs, n + 1)
                        dve.wait_ge(c_t2, n + 1)
                        for t in range(4):
                            a = dve.tensor_scalar(c_nh[:, P * t:P * t + P], CT[:, P * t:P * t + P],
                                                  lnr[:, nxt.k, 1, t:t + 1], lnr[:, nxt.k, 3, t:t + 1],
                                                  ALU.mult, ALU.add)
                        a.then_inc(c_nm, 1)
                    if cur:
                        n = b * NW + cur.i
                        dve.wait_ge(c_f2, n + 2)
                        dve.wait_ge(c_y, n + 1)
                        dve.scalar_tensor_tensor(out=c_hfin, in0=CM, scalar=BF2, in1=c_hT[:, cur.k, :],
                                                 op0=ALU.add, op1=ALU.add).then_inc(c_hf, 1)
                        dve.wait_ge(c_y, n + 2)
                        dve.wait_ge(c_st[cur.k], DMA * (b * (NW // 2) + cur.fill))
                        dve.tensor_tensor(by_column(cxo[:, cur.k, :]),
                                          CY[0:C0, :].rearrange("p (m y c) -> p m y c", m=NW, y=SS),
                                          by_column(cx[0:C0, 1, cur.k, :]), ALU.add).then_inc(c_xo, 1)

                lookahead(dve, NW, 2, c_step)
                phase_end(dve, b * 3 + 4)

            dve.memset(d_eb, 0.0).then_inc(d_set, 1)
            dve.wait_ge(d_w, DMA * (G8 + 3))

            def spread(v):
                return v.unsqueeze(2).broadcast_to([P, G8, E])

            def over_tiles(v):
                return v.unsqueeze(1).broadcast_to([P, G8, E])

            GSTEP = 17

            def gating(j):
                base = GSTEP * j.i
                lg, pick, oh1, oh2, lg2 = (d_t[:, i, :, :] for i in range(5))
                m1, m2, top = d_s[:, 2, :], d_s[:, 3, :], d_s[:, 4, :]
                dve.tensor_tensor(lg, DL.rearrange("p (t e) -> p t e", e=E), over_tiles(d_rb), ALU.add) \
                    .then_inc(d_gs, 1)
                dve.wait_ge(d_gs, base + 1)
                dve.tensor_reduce(m1, lg, AX.X, ALU.max).then_inc(d_gs, 1)
                dve.wait_ge(d_gs, base + 2)
                dve.tensor_tensor(pick, lg, spread(m1), ALU.is_ge).then_inc(d_gs, 1)
                dve.wait_ge(d_gs, base + 3)
                dve.tensor_tensor(pick, pick, over_tiles(RANK), ALU.mult).then_inc(d_gs, 1)
                dve.wait_ge(d_gs, base + 4)
                dve.tensor_reduce(top, pick, AX.X, ALU.max).then_inc(d_gs, 1)
                dve.wait_ge(d_gs, base + 5)
                dve.tensor_tensor(oh1, pick, spread(top), ALU.is_equal).then_inc(d_gs, 1)
                dve.wait_ge(d_gs, base + 6)
                dve.scalar_tensor_tensor(out=lg2, in0=oh1, scalar=-1e38, in1=lg, op0=ALU.mult, op1=ALU.add) \
                    .then_inc(d_gs, 1)
                dve.wait_ge(d_gs, base + 7)
                dve.tensor_reduce(m2, lg2, AX.X, ALU.max).then_inc(d_gs, 1)
                dve.wait_ge(d_gs, base + 8)
                dve.wait_ge(d_e2, j.i + 1)
                dve.tensor_tensor(d_s[:, 0, :], m2, m1, ALU.subtract).then_inc(d_df, 1)
                dve.tensor_tensor(pick, lg2, spread(m2), ALU.is_ge).then_inc(d_gs, 1)
                dve.wait_ge(d_gs, base + 9)
                dve.tensor_tensor(pick, pick, over_tiles(RANK), ALU.mult).then_inc(d_gs, 1)
                dve.wait_ge(d_gs, base + 10)
                dve.tensor_reduce(top, pick, AX.X, ALU.max).then_inc(d_gs, 1)
                dve.wait_ge(d_gs, base + 11)
                dve.tensor_tensor(oh2, pick, spread(top), ALU.is_equal).then_inc(d_gs, 1)
                dve.wait_ge(d_gs, base + 12)
                dve.wait_ge(d_e2, j.i + 2)
                dve.tensor_scalar(d_s[:, 5, :], d_s[:, 1, :], 1.0, None, ALU.add).then_inc(d_gs, 1)
                dve.wait_ge(d_gs, base + 13)
                dve.reciprocal(d_s[:, 6, :], d_s[:, 5, :]).then_inc(d_gs, 1)
                dve.wait_ge(d_gs, base + 14)
                dve.tensor_tensor(d_s[:, 7, :], d_s[:, 6, :], d_s[:, 1, :], ALU.mult).then_inc(d_gs, 1)
                dve.wait_ge(d_gs, base + 15)
                dve.tensor_tensor(oh1, oh1, spread(d_s[:, 6, :]), ALU.mult).then_inc(d_gs, 1)
                dve.wait_ge(d_gs, base + 16)
                dve.tensor_tensor(oh2, oh2, spread(d_s[:, 7, :]), ALU.mult).then_inc(d_gs, 1)
                dve.wait_ge(d_gs, base + GSTEP)
                dve.wait_ge(d_gt, j.i + 1)
                dve.tensor_tensor(d_gate[:, j.k, :, :], oh1, oh2, ALU.add).then_inc(d_g, 1)

            def d_step(cur, nxt):
                if nxt:
                    dve.wait_ge(d_ld[nxt.k], DMA * nxt.fill)
                    dve.wait_ge(d_rs, nxt.i + 1)
                    moments([d_x[:, nxt.k, t, :] for t in range(G8)], nxt.k, d_bn, d_mv, nxt.i)
                if cur:
                    dve.wait_ge(d_st[cur.k], DMA * cur.fill)
                    for t in range(G8):
                        if t < 2:
                            dve.wait_ge(d_bm, 2 * cur.i + t + 2)
                            dve.tensor_tensor(d_acc[:, cur.k, 4 * t:4 * t + 4, :].rearrange("p t n -> p (t n)"), DB,
                                              d_x[:, cur.k, 4 * t:4 * t + 4, :].rearrange("p t n -> p (t n)"),
                                              ALU.add).then_inc(d_bi, 1)
                        if t == 0 or t == 1:
                            dve.wait_ge(d_bi, 2 * cur.i + t + 2)
                        dve.wait_ge(d_y, G8 * cur.i + t + 17)
                        acc = d_acc[:, cur.k, t, :]
                        for e in range(E):
                            ins = dve.scalar_tensor_tensor(
                                out=acc, in0=DY[t % 2][:, e // 4, P * (e % 4):P * (e % 4) + P],
                                scalar=d_gate[:, cur.k, t, e:e + 1], in1=acc, op0=ALU.mult, op1=ALU.add)
                            if e < E - 1:
                                ins.then_inc(d_ac, 1)
                                dve.wait_ge(d_ac, (E - 1) * (G8 * cur.i + t) + e + 1)
                            else:
                                ins.then_inc(d_cb, 1)
                if nxt:
                    dve.wait_ge(d_lg, nxt.i + 1)
                    gating(nxt)

            lookahead(dve, STEPS, 2, d_step)

        @block.gpsimd
        def _(pool):
            start_up(pool, POOL_OWNS)
            pool.memset(ident[:, :], 0.0).then_inc(s_id, 1)
            pool.wait_ge(s_id, 1)
            pool.affine_select(out=ident[:, :], in_=ident[:, :], compare_op=ALU.not_equal, fill=1.0, base=0,
                               pattern=[[-1, P]], channel_multiplier=1).then_inc(s_id, 1)
            pool.wait_ge(s_set, 1)

            def ln_small(m, to, n, eps, step, steps_before, done):
                pool.tensor_tensor(to[:, 0, 0:n], m[:, 0:n, 1], eps[:, 0:n], ALU.add).then_inc(step, 1)
                pool.wait_ge(step, steps_before + 1)
                pool.tensor_tensor(to[:, 1, 0:n], to[:, 0, 0:n], NHALF[:, 0:n], ALU.pow).then_inc(step, 1)
                pool.wait_ge(step, steps_before + 2)
                pool.tensor_tensor(to[:, 2, 0:n], m[:, 0:n, 0], to[:, 1, 0:n], ALU.mult).then_inc(step, 1)
                pool.wait_ge(step, steps_before + 3)
                pool.tensor_tensor(to[:, 3, 0:n], to[:, 2, 0:n], NEG1[:, 0:n], ALU.mult).then_inc(done, 1)

            def n_step(cur, nxt):
                if nxt:
                    pool.wait_ge(n_mv, nxt.i + 1)
                    pool.wait_ge(n_nm, nxt.i + 1)
                    ln_small(mv[:, nxt.k], lnr[:, nxt.k], G8, EPS6, n_ln, 3 * nxt.i, n_rs)

            lookahead(pool, STEPS, 2, n_step)
            phase_end(pool, 1)
            with pool.Fori(0, B) as b:
                def a_step(cur, nxt):
                    if nxt:
                        n = b * NW + nxt.i
                        pool.wait_ge(a_mv, n + 1)
                        pool.wait_ge(a_nm, n + 1)
                        ln_small(mv[:, nxt.k % 2], lnr[:, nxt.k % 2], 4, EPS5, a_ln, 3 * n, a_rs)

                lookahead(pool, NW, 4, a_step)
                phase_end(pool, b * 3 + 2)
                pool.memset(workb[PAIRS:MAXROW, 0:16384], 0.0)
                pool.memset(kcat[MAXROW:MAXROW + 2, :, :, :].rearrange("p q j n -> p (q j n)"), MAXUNIT)
                pool.drain().then_inc(s_kset, 1)
                CVS = 16

                def slot(t):
                    if not t.P:
                        return
                    br = t.P.branch
                    pool.wait_ge(s_vte, t.nP + 2)
                    pool.wait_ge(s_cvd0, t.P.conv_free[0] + DMA)
                    pool.wait_ge(s_cvd1, t.P.conv_free[1] + DMA)
                    shape = dict(y=64) if br == 0 else dict(y=SS)

                    def grid(v):
                        return v.rearrange("p (y c) -> p y c", **shape)

                    def tap(n):
                        y, c = n // 3, n % 3
                        return vT[0][:, y:y + 64, c:c + 4] if br == 0 else vT[1][:, y:y + 4, c:c + 64]

                    base = CVS * t.nP
                    pool.wait_ge(s_cv, t.nP + 1)
                    settle(pool)
                    pool.tensor_scalar(grid(cv_acc[:, :]), tap(0), cw[:, br, 0:1], cb[:, br:br + 1],
                                       ALU.mult, ALU.add).then_inc(s_cvc, 1)
                    for n in range(1, 9):
                        pool.tensor_scalar(grid(cv_tmp[:, :]), tap(n), cw[:, br, n:n + 1], 0.0,
                                           ALU.mult, ALU.add).then_inc(s_cvc, 1)
                        pool.wait_ge(s_cvc, base + 2 * n)
                        if n < 8:
                            pool.tensor_tensor(cv_acc[:, :], cv_acc[:, :], cv_tmp[:, :], ALU.add) \
                                .then_inc(s_cvc, 1)
                            pool.wait_ge(s_cvc, base + 2 * n + 1)
                            settle(pool)
                    if br == 0:
                        ins = pool.tensor_tensor(cv_out[:, :], cv_acc[:, :], cv_tmp[:, :], ALU.add)
                    else:
                        v = [z[:, :].rearrange("p (y m c) -> p y m c", y=SS, m=16) for z in (cv_acc, cv_tmp)]
                        ins = pool.tensor_tensor(cv_out[:, :].rearrange("p (m y c) -> p y m c", y=SS, m=16),
                                                 v[0], v[1], ALU.add)
                    ins.then_inc(s_cv, 1)

                pipeline(pool, b, slot)
                phase_end(pool, b * 3 + 3)

                def c_step(cur, nxt):
                    if nxt:
                        n = b * NW + nxt.i
                        pool.wait_ge(c_mv, n + 1)
                        pool.wait_ge(c_nm, n + 1)
                        ln_small(mv[:, nxt.k], lnr[:, nxt.k], 4, EPS5, c_ln, 3 * n, c_rs)

                lookahead(pool, NW, 2, c_step)
                phase_end(pool, b * 3 + 4)

            def d_step(cur, nxt):
                if nxt:
                    pool.wait_ge(d_mv, nxt.i + 1)
                    pool.wait_ge(d_nm, nxt.i + 1)
                    ln_small(mv[:, nxt.k], lnr[:, nxt.k], G8, EPS5, d_ln, 3 * nxt.i, d_rs)

            lookahead(pool, STEPS, 2, d_step)


_INS = ["x", "L0_conv_w_embed", "L0_conv_g1", "L0_conv_b1", "L0_conv_w_qkv", "L0_conv_conv_w0", "L0_conv_conv_b0",
        "L0_conv_conv_w1", "L0_conv_conv_b1", "L0_conv_w_proj", "L0_conv_b_proj", "L0_conv_g2", "L0_conv_b2",
        "L0_conv_w_fc1", "L0_conv_b_fc1", "L0_conv_w_fc2", "L0_conv_b_fc2", "L0_conv_w_out", "L0_ffn_router_w",
        "L0_ffn_router_b", "L0_ffn_expert_w", "L0_ffn_expert_b"]


def kernel(**inputs):
    import numpy as _np
    import concourse.bacc as _bacc
    from concourse.bass_utils import run_bass_kernel_spmd as _run

    nc = _bacc.Bacc("TRN2", target_bir_lowering=False, num_devices=1)
    arrays, args = {}, []
    for name in _INS:
        a = _np.ascontiguousarray(inputs[name])
        arrays[f"in_{name}"] = a
        args.append(nc.dram_tensor(f"in_{name}", a.shape, mybir.dt.from_np(a.dtype), kind="ExternalInput").ap())
    args.append(nc.dram_tensor("out", (B, C0, H, W), F32, kind="ExternalOutput").ap())
    build(nc, *args)
    r = _run(nc, [arrays], core_ids=[0])
    return r.results[0]["out"]
```

```python
from contextlib import ExitStack

import concourse.bass as bass
from concourse import mybir

F32 = mybir.dt.float32
FP16 = mybir.dt.float16
ALU = mybir.AluOpType
ACT = mybir.ActivationFunctionType
AX = mybir.AxisListType

P = 128
B, C0, H, W = 4, 64, 128, 128
C = 2 * C0
NBR = 2
HB = C // 2
NH = 4
D = HB // NH
SS = 4
WT = H * SS
NW = H // SS
TOK = H * W
KC = WT // P
FF = 4 * C
NF = FF // P
E = 8
E_ACT = 4
U = NH * KC
CATQ = 4
PAIRS = 4 * D
MAXROW = 96
MAXUNIT = 1024.0
G8 = 8
STEPS = B * C0 // G8
DMA = 16
CAT_DMAS = 4 * NH


class Window:

    def __init__(self, b, it, k):
        self.branch = 1 if k >= NW else 0
        self.q = k % CATQ
        self.w = 4 * it + (k - NW * self.branch)
        self.g = b * (NBR * NW) + 4 * it + k
        before = [b * NW + (self.w if self.branch == br else NW * self.branch) for br in range(NBR)]
        self.conv_free = (2 * DMA * before[0], DMA * before[1])
        self._quads = b * (NBR * NW // 4) + it
        self._k = k

    def fills(self, back):
        return self._quads + (self._k - back) // 4 + 1


class Step:

    def __init__(self, it, k, u):
        self.i, self.k, self.fill = u * it + k, k % u, it + k // u + 1


def stages(eng, n, u, depth, body):
    def peeled(slots):
        for s in slots:
            body([Step(0, s + a, u) if 0 <= s + a < n else None for a in range(depth)])

    its = (n - depth + 1) // u
    peeled(range(1 - depth, 0))
    with eng.Fori(0, its) as it:
        for k in range(u):
            body([Step(it, k + a, u) for a in range(depth)])
    peeled(range(its * u, n))


def lookahead(eng, n, u, body):
    stages(eng, n, u, 2, lambda steps: body(*steps))


class Slot:

    def __init__(self, b, it, s, loop):
        def stage(ahead):
            c = s + ahead
            n = NBR * NW
            inside = loop or 0 <= c < n
            window = Window(b, it, c) if inside else None
            count = window.g if inside else b * n + min(max(c, 0), n)
            return window, count

        self.P, self.nP = stage(3)
        self.L, self.nL = stage(2)
        self.M, self.nM = stage(1)
        self.T, self.nT = stage(0)
        self.F, self.nF = stage(-1)


def pipeline(eng, b, body):
    for s in range(-3, 1):
        body(Slot(b, 0, s, False))
    with eng.Fori(0, 7) as it:
        for k in range(1, 5):
            body(Slot(b, it, k, True))
    for s in range(29, 33):
        body(Slot(b, 0, s, False))
    with eng.Fori(0, 7) as it:
        for k in range(1, 5):
            body(Slot(b, it, NW + k, True))
    for s in range(61, 65):
        body(Slot(b, 0, s, False))


def build(nc, x, w_embed, g1, b1, w_qkv, conv_w0, conv_b0, conv_w1, conv_b1, w_proj, b_proj, g2, b2,
          w_fc1, b_fc1, w_fc2, b_fc2, w_out, router_w, router_b, expert_w, expert_b, out):
    xn_d = nc.dram_tensor("xn_scratch", (B * C0, H, W), F32).ap()
    x2_d = nc.dram_tensor("x2_scratch", (B * C0, H, W), F32).ap()
    conv0_d = nc.dram_tensor("conv0_scratch", (B, NW, HB, WT), F32).ap()
    conv1_d = nc.dram_tensor("conv1_scratch", (B, NW, 2, HB, WT // 2), F32).ap()
    x_rows = x.rearrange("b c h m -> (b c) h m")
    out_rows = out.rearrange("b c h m -> (b c) h m")

    with ExitStack() as ctx:
        def sb(name, shape, dt=F32):
            return ctx.enter_context(nc.sbuf_tensor(name, shape, dt))

        def sem(name):
            return ctx.enter_context(nc.semaphore(name))

        imgT = sb("imgT", [P, TOK])
        att0 = sb("att0", [P, TOK])
        work = sb("work", [P, 12288])
        vaug = sb("vaug", [P, 4, KC, NH, 32])
        parts = sb("parts", [P, 2, 2, WT], FP16)
        o_sb = sb("o_sb", [P, WT])
        vT = [sb("vT0", [P, 66, 6]), sb("vT1", [P, 6, 66])]
        v_own = sb("v_own", [P, 256])
        cv_acc = sb("cv_acc", [P, 256])
        cv_tmp = sb("cv_tmp", [P, 256])
        cv_out = sb("cv_out", [P, 256])
        wqk = sb("wqk", [P, NBR, P])
        wv = sb("wv", [P, NBR, 2, P])
        ident = sb("ident", [P, P])
        wemb = sb("wemb", [P, 2, C])
        wpr = sb("wpr", [P, NBR, C])
        wprc = sb("wprc", [P, C])
        wout = sb("wout", [P, P])
        cw = sb("cw", [P, NBR, 9])
        cb = sb("cb", [P, NBR])
        cols = sb("cols", [P, 10 + NF])
        mx = sb("mx", [P, 2, 32])
        mxh = sb("mxh", [P, U], FP16)
        mxb = sb("mxb", [2 * U, P], FP16)
        rec = sb("rec", [P, KC, NH])
        rec_wide = sb("rec_wide", [P, WT])
        stat = sb("stat", [P, 2, 8, 6])
        mv = sb("mv", [P, 2, 8, 2])
        lnr = sb("lnr", [P, 2, 4, 8])
        konst = sb("konst", [P, 6, 8])
        G1, B1, G2, B2, BP, BF2 = (cols[:, i:i + 1] for i in range(6))
        BF1 = [cols[:, 10 + i:11 + i] for i in range(NF)]
        EPS6, EPS5, NHALF, NEG1 = (konst[:, i, :] for i in range(4))
        RANK = konst[:, 5, :]

        workb = work[:, :].bitcast(FP16)
        qcat = workb[:, 0:8192].rearrange("p (q j n) -> p q j n", q=CATQ, j=NH)
        kcat = workb[:, 8192:16384].rearrange("p (q j n) -> p q j n", q=CATQ, j=NH)
        probs = work[:, 8192:12288].rearrange("p (u n) -> p u n", u=8)
        rows_in = work[:, 0:2048].rearrange("p (q t m) -> p q t m", q=2, t=G8)
        rows_out = work[:, 2048:4096].rearrange("p (q t m) -> p q t m", q=2, t=G8)
        xa = work[:, 0:2048].rearrange("p (q n) -> p q n", q=4)
        ihat = work[:, 2048:3072].rearrange("p (q n) -> p q n", q=2)
        cx = work[:, 0:4096].rearrange("p (t q n) -> p t q n", t=2, q=4)
        cxo = work[C0:P, 4096:5120].rearrange("p (q n) -> p q n", q=2)
        c_hT = work[:, 5120:7168].rearrange("p (q n) -> p q n", q=4)
        c_nh, c_mT, c_hfin = work[:, 7168:7680], work[:, 7680:8192], work[:, 8192:8704]
        fc1 = work[:, 8704:9216]
        fc2 = work[:, 9216:9728].rearrange("p (f n) -> p f n", f=NF)
        c_g = work[:, 9728:11776].rearrange("p (f n) -> p f n", f=NF)
        d_x = work[:, 0:2048].rearrange("p (q t m) -> p q t m", q=2, t=G8)
        d_acc = work[:, 2048:4096].rearrange("p (q t m) -> p q t m", q=2, t=G8)
        d_xl = work[:, 4096:5120].rearrange("p (t m) -> p t m", t=G8)
        d_xT = work[:, 5120:7168].rearrange("p (q t m) -> p q t m", q=2, t=G8)
        d_ew = work[:, 7168:8192].rearrange("p (e m) -> p e m", e=E)
        d_eb = work[0:E * G8, 8192:9216].rearrange("p (t m) -> p t m", t=G8)
        d_gT = work[0:E * G8, 9216:9344]
        d_gate = work[:, 9344:9472].rearrange("p (q t e) -> p q t e", q=2, t=G8)
        d_t = work[:, 9472:9792].rearrange("p (i t e) -> p i t e", i=5, t=G8)
        d_s = work[:, 9792:9856].rearrange("p (i t) -> p i t", i=8)
        d_scaled = imgT[:, 0:4096].rearrange("p (e u n) -> p e u n", e=8, u=4)
        d_rw, d_rb = work[:, 9856:9864], work[:, 9864:9872]

        ps = ctx.enter_context(nc.psum_tensor("ps", [P, 8, 512], F32))
        bank = [ps[:, i, :] for i in range(8)]
        SM, ST, O, X0, X1, X2 = bank[0:2], bank[2:4], bank[4], bank[5], bank[6], bank[7]
        EA, TB = bank[0:4], bank[4:6]
        CH, CT1, CT2, CF, CM, CY = bank[0], bank[1], bank[2], bank[3:5], bank[5], bank[6]
        DT, DL, DB, DY = bank[0:2], bank[2][:, 0:E * G8], bank[3], [ps[:, 4:6, :], ps[:, 6:8, :]]

        s_settled = sem("settled")
        s_phase = sem("phase")
        s_w, s_fc, d_w = sem("weights"), sem("mlp_weights"), sem("expert_weights")
        n_ld = [sem(f"n_load{i}") for i in range(2)]
        n_st = [sem(f"n_written{i}") for i in range(2)]
        a_ld = [sem(f"a_load{i}") for i in range(4)]
        s_cat = [sem(f"cat_filled{i}") for i in range(CATQ)]
        s_mrow = sem("max_rows_filled")
        s_cvd0, s_cvd1 = sem("conv0_written"), sem("conv1_written")
        c_ld = [sem(f"c_load{i}") for i in range(4)]
        c_st = [sem(f"c_written{i}") for i in range(2)]
        d_ld = [sem(f"d_load{i}") for i in range(2)]
        d_st = [sem(f"d_written{i}") for i in range(2)]
        SP_OWNS = {DMA: n_st + s_cat + [s_mrow, s_cvd0, s_cvd1] + c_st + d_st}

        s_qk, s_vt, s_vk = sem("qk_made"), sem("vT_made"), sem("v_by_key_made")
        s_mxt, s_sm, s_st = sem("max_turned"), sem("max_scores"), sem("scores")
        s_pv, s_ot, s_bt = sem("values_summed"), sem("out_turned"), sem("recip_spread")
        a_e, a_tr = sem("a_embedded"), sem("a_turned")
        c_h, c_t1, c_t2 = sem("c_h"), sem("c_turned"), sem("c_turned_back")
        c_f1, c_f2, c_y = sem("c_fc1"), sem("c_fc2"), sem("c_y")
        d_tr, d_lg, d_gt = sem("d_turned"), sem("d_logits"), sem("d_gates_turned")
        d_bm, d_y = sem("d_bias_made"), sem("d_experts")
        PE_OWNS = {1: [s_vk, s_bt, c_t2, c_f1, c_f2, c_y, d_tr, d_bm],
                   2: [s_mxt, a_tr, d_gt],
                   8: [a_e],
                   16: [s_pv],
                   64: [s_st]}

        s_qs, s_exp = sem("q_scaled"), sem("exp_done")
        s_hb = sem("high_part")
        s_vte, s_vke, s_mxe = sem("vT_stored"), sem("v_by_key_stored"), sem("max_stored")
        s_oev = sem("out_stored")
        n_nm, a_ev = sem("n_normed"), sem("a_image")
        c_hs, c_gl, c_m = sem("c_h_stored"), sem("c_gelu"), sem("c_mlp_in")
        d_nm, d_xt, d_gte, d_e2 = sem("d_normed"), sem("d_xT"), sem("d_gT"), sem("d_exp")
        d_sc = sem("d_experts_scaled")
        ACT_OWNS = {1: [s_vte, s_vke, s_mxe, s_oev, d_xt, d_gte, d_e2],
                    2: [s_exp, n_nm, a_ev, c_gl, d_nm],
                    3: [d_sc]}

        s_dz, s_set, d_set = sem("zeros_set"), sem("constants_set"), sem("d_zeros_set")
        s_red, s_mh, s_mxs = sem("tile_max"), sem("max_high"), sem("max_split")
        s_lo, s_rec, s_att = sem("low_part"), sem("recip_done"), sem("att_stored")
        s_rw = sem("recip_widened")
        n_bn, n_mv, a_bn, a_mv = sem("n_stats"), sem("n_moments"), sem("a_stats"), sem("a_moments")
        c_bn, c_mv, d_bn, d_mv = sem("c_stats"), sem("c_moments"), sem("d_stats"), sem("d_moments")
        a_nm, c_nm, c_hf, c_xo = sem("a_normed"), sem("c_normed"), sem("c_sum"), sem("c_x_out")
        d_gs, d_df, d_g = sem("d_gate_step"), sem("d_logit_gap"), sem("d_gates")
        d_bi, d_ac, d_cb = sem("d_bias_added"), sem("d_expert_added"), sem("d_combined")
        DVE_OWNS = {1: [s_lo, s_rec, s_att, c_m, c_hs, c_hf, c_xo, d_g, d_bi],
                    2: [s_red, c_nm],
                    4: [a_nm],
                    3: [d_cb]}

        s_id, s_kset = sem("identity_set"), sem("fixed_rows_set")
        s_cv, s_cvc = sem("conv_done"), sem("conv_step")
        n_ln, n_rs, a_ln, a_rs = sem("n_ln_step"), sem("n_rstd"), sem("a_ln_step"), sem("a_rstd")
        c_ln, c_rs, d_ln, d_rs = sem("c_ln_step"), sem("c_rstd"), sem("d_ln_step"), sem("d_rstd")
        d_sum, d_ps, d_out = sem("d_sum_step"), sem("d_partly_summed"), sem("d_summed")
        POOL_OWNS = {1: [s_cv],
                     2: [n_rs, d_rs],
                     3: [d_out]}

        block = ctx.enter_context(nc.Block())
        ENGINES = 5

        def settle(eng):
            eng.sem_inc(s_settled, 1)

        def phase_end(eng, n):
            settle(eng)
            eng.drain().then_inc(s_phase, 1)
            eng.wait_ge(s_phase, ENGINES * n)
            settle(eng)

        n_weights = 38

        def start_up(eng, owns):
            for start, sems in owns.items():
                for s in sems:
                    eng.sem_inc(s, start)

        def qk_view(win):
            if win.branch == 0:
                return imgT[:, :].rearrange("p (h m c) -> p h m c", m=NW, c=SS)[:, :, win.w, :]
            return imgT[:, bass.ds(win.w * WT, WT)].rearrange("p (y a c) -> p a y c", y=SS, a=2)

        def half_view(win, a):
            if win.branch == 0:
                return imgT[:, :].rearrange("p (h m c) -> p h m c", m=NW, c=SS)[:, 63 * a:63 * a + 65, win.w, :]
            return imgT[:, bass.ds(win.w * WT, WT)].rearrange("p (y c) -> p y c", y=SS)[:, :, 63 * a:63 * a + 65]

        def vt_psum(win, a):
            lo = 1 - a
            if win.branch == 0:
                return X1[:, 0:264].rearrange("p (y c) -> p y c", c=SS)[:, lo:lo + 65, :]
            return X1[:, 0:264].rearrange("p (y c) -> p y c", y=SS)[:, :, lo:lo + 65]

        def by_column(ap):
            return ap.rearrange("p (y m c) -> p m y c", y=SS, m=NW)

        @block.sync
        def _(sp):
            start_up(sp, SP_OWNS)

            def load(dst, src):
                sp.dma_start(dst, src).then_inc(s_w, DMA)

            sp.wait_ge(s_set, 1)
            for h in range(2):
                load(wemb[C0 * h:C0 * h + C0, h, :], w_embed)
            load(wout[:, C0:P], w_out)
            load(wprc[:, :], w_proj)
            for br in range(NBR):
                load(wqk[:, br, 0:HB], w_qkv[:, HB * br:HB * br + HB])
                load(wqk[:, br, HB:P], w_qkv[:, C + HB * br:C + HB * br + HB])
                for a in range(2):
                    load(wv[:, br, a, HB * a:HB * a + HB], w_qkv[:, 2 * C + HB * br:2 * C + HB * br + HB])
                    load(cw[HB * a:HB * a + HB, br, :],
                         (conv_w0, conv_w1)[br].rearrange("c o y s -> c (o y s)"))
                    load(cb[HB * a:HB * a + HB, br:br + 1], (conv_b0, conv_b1)[br].rearrange("(c o) -> c o", o=1))
                for j in range(NH):
                    load(wpr[32 * j:32 * j + D, br, :], w_proj[HB * br + D * j:HB * br + D * j + D, :])
            for i, v in enumerate((g1, b1, g2, b2, b_proj, b_fc2)):
                load(cols[:, i:i + 1], v.rearrange("(c o) -> c o", o=1))
            for f in range(NF):
                load(cols[:, 10 + f:11 + f], b_fc1[P * f:P * f + P].rearrange("(c o) -> c o", o=1))

            def n_load(s, q):
                sp.dma_start(rows_in[:, q], x_rows[bass.ds(s * G8, G8)].rearrange("c h m -> h c m")) \
                    .then_inc(n_ld[q], DMA)

            def n_store(s, q):
                sp.wait_ge(n_nm, s + 3)
                settle(sp)
                sp.dma_start(xn_d[bass.ds(s * G8, G8)].rearrange("c h m -> h c m"), rows_out[:, q]) \
                    .then_inc(n_st[q], DMA)

            for q in range(2):
                n_load(q, q)
            with sp.Fori(0, STEPS // 2 - 1) as it:
                for q in range(2):
                    n_store(it * 2 + q, q)
                    n_load(it * 2 + q + 2, q)
            for q in range(2):
                n_store(STEPS - 2 + q, q)
            for q in range(2):
                sp.wait_ge(n_st[q], DMA * (STEPS // 2 + 1))
                settle(sp)
            phase_end(sp, 1)

            with sp.Fori(0, B) as b:
                with sp.Fori(0, NW // 8) as it:
                    for q in range(4):
                        for h in range(2):
                            i = it * 8 + 2 * q + h
                            if h == 0:
                                sp.wait_ge(a_e, b * NW + i + 2)
                                settle(sp)
                            sp.dma_start(xa[C0 * h:C0 * h + C0, q, :],
                                         xn_d[bass.ds(b * C0, C0), bass.ds(i * SS, SS), :]
                                         .rearrange("c y m -> c (y m)")).then_inc(a_ld[q], DMA)
                phase_end(sp, b * 3 + 2)

                def slot(t):
                    if t.L:
                        sp.wait_ge(s_cv, t.nL + 2)
                        settle(sp)
                        if t.L.branch == 0:
                            for a in range(2):
                                sp.dma_start(conv0_d[b, 16 * a:16 * a + 16, :, bass.ds(t.L.w * 16, 16)]
                                             .rearrange("i c x -> c i x"),
                                             cv_out[HB * a:HB * a + HB, :].rearrange("p (i x) -> p i x", x=16)) \
                                    .then_inc(s_cvd0, DMA)
                        else:
                            sp.dma_start(conv1_d[b, t.L.w].rearrange("a c n -> (a c) n"), cv_out[:, :]) \
                                .then_inc(s_cvd1, DMA)
                    if t.M:
                        sp.wait_ge(s_mxe, t.nM + 2)
                        settle(sp)
                        sp.dma_start(qcat[MAXROW:MAXROW + 2, t.M.q].rearrange("p j n -> p (j n)"), mxb[:, :]) \
                            .then_inc(s_mrow, DMA)
                    if t.P:
                        sp.wait_ge(s_lo, t.nP + 2)
                        settle(sp)
                        sp.wait_ge(s_st, U * (t.nP - 3) + 64)
                        settle(sp)
                        for j in range(NH):
                            for side, cat in ((0, qcat), (1, kcat)):
                                for half in range(2):
                                    s = parts[HB * side + D * j:HB * side + D * j + D, t.P.q % 2, :, :]
                                    rows = bass.AP(tensor=s.tensor, offset=s.offset + (0 if side else WT * half),
                                                   ap=[[s.ap[0][0], D], [WT if side else 0, 2], [1, WT]])
                                    sp.dma_start(cat[2 * D * half:2 * D * half + 2 * D, t.P.q, j, :], rows) \
                                        .then_inc(s_cat[t.P.q], DMA)

                pipeline(sp, b, slot)
                sp.wait_ge(s_cvd0, (b + 1) * (NW * 2 * DMA) + DMA)
                settle(sp)
                sp.wait_ge(s_cvd1, (b + 1) * (NW * DMA) + DMA)
                settle(sp)
                phase_end(sp, b * 3 + 3)

                sp.dma_start(fc1, w_fc1).then_inc(s_fc, DMA)
                sp.dma_start(fc2, w_fc2.rearrange("(f p) n -> p f n", p=P)).then_inc(s_fc, DMA)

                def c_load(i, q):
                    for h, src in enumerate((xn_d, x_rows)):
                        sp.dma_start(cx[C0 * h:C0 * h + C0, 0, q, :], src[bass.ds(b * C0, C0), bass.ds(i * SS, SS), :]
                                     .rearrange("c y m -> c (y m)")).then_inc(c_ld[q], DMA)
                    sp.dma_start(cx[0:HB, 1, q, :], conv0_d[b, i]).then_inc(c_ld[q], DMA)
                    sp.dma_start(cx[HB:P, 1, q, :].rearrange("p (a n) -> p a n", a=2),
                                 conv1_d[b, i].rearrange("a c n -> c a n")).then_inc(c_ld[q], DMA)

                def c_store(i, q):
                    sp.wait_ge(c_xo, b * NW + i + 2)
                    settle(sp)
                    sp.dma_start(x2_d[bass.ds(b * C0, C0), bass.ds(i * SS, SS), :].rearrange("c y m -> c (y m)"),
                                 cxo[:, q % 2, :]).then_inc(c_st[q % 2], DMA)

                for q in range(4):
                    c_load(q, q)
                with sp.Fori(0, NW // 4 - 1) as it:
                    for q in range(4):
                        c_store(it * 4 + q, q)
                        c_load(it * 4 + q + 4, q)
                for q in range(4):
                    c_store(NW - 4 + q, q)
                for q in range(2):
                    sp.wait_ge(c_st[q], (b + 1) * (DMA * NW // 2) + DMA)
                    settle(sp)
                phase_end(sp, b * 3 + 4)

            def d_load(s, q):
                sp.dma_start(d_x[:, q], x2_d[bass.ds(s * G8, G8)].rearrange("c h m -> h c m")) \
                    .then_inc(d_ld[q], DMA)

            def d_store(s, q):
                sp.wait_ge(d_out, G8 // 2 * (s + 1) + 3)
                settle(sp)
                sp.dma_start(out_rows[bass.ds(s * G8, G8)].rearrange("c h w -> h c w"), d_acc[:, q]) \
                    .then_inc(d_st[q], DMA)

            sp.dma_start(d_rw, router_w).then_inc(d_w, DMA)
            sp.dma_start(d_ew, expert_w.rearrange("e d c -> d e c")).then_inc(d_w, DMA)
            sp.wait_ge(d_set, 1)
            settle(sp)
            for t in range(G8):
                sp.dma_start(d_eb[E * t:E * t + E, t, :], expert_b).then_inc(d_w, DMA)
            sp.dma_start(d_rb, router_b.rearrange("(o e) -> o e", o=1).broadcast_to([P, E])) \
                .then_inc(d_w, DMA)
            for q in range(2):
                d_load(q, q)
            with sp.Fori(0, STEPS // 2 - 1) as it:
                for q in range(2):
                    sp.wait_ge(d_bi, 2 * (it * 2 + q) + 3)
                    settle(sp)
                    d_load(it * 2 + q + 2, q)
                    d_store(it * 2 + q, q)
            for q in range(2):
                d_store(STEPS - 2 + q, q)
            for q in range(2):
                sp.wait_ge(d_st[q], DMA * (STEPS // 2 + 1))
                settle(sp)

        @block.tensor
        def _(pe):
            start_up(pe, PE_OWNS)
            phase_end(pe, 1)
            pe.wait_ge(s_w, DMA * n_weights)
            pe.wait_ge(s_id, 2)
            pe.wait_ge(s_qs, 1)
            with pe.Fori(0, B) as b:
                def a_step(steps):
                    cur, _, new = steps
                    if new:
                        n = b * NW + new.i
                        pe.wait_ge(a_ld[new.k // 2], 2 * DMA * (b * (NW // 8) + new.fill))
                        pe.wait_ge(a_nm, n + 1)
                        for t in range(4):
                            mm = pe.matmul(EA[new.k % 4][:, P * t:P * t + P], xa[:, new.k // 2, P * t:P * t + P],
                                           wemb[:, new.k % 2, :], start=True, stop=True)
                        mm.then_inc(a_e, 1)
                    if cur:
                        n = b * NW + cur.i
                        pe.wait_ge(a_nm, n + 5)
                        pe.wait_ge(a_ev, n + 1)
                        for t in range(4):
                            mm = pe.transpose(TB[cur.k % 2][:, P * t:P * t + P],
                                              ihat[:, cur.k % 2, P * t:P * t + P], ident[:, :])
                        mm.then_inc(a_tr, 1)

                stages(pe, NW, 8, 3, a_step)
                phase_end(pe, b * 3 + 2)
                pe.wait_ge(s_kset, b + 1)

                def scores_for_max(t, k):
                    j, i = k // KC, k % KC
                    if k == 0:
                        pe.wait_ge(s_cat[t.M.q], DMA * CAT_DMAS * t.M.fills(0) + DMA)
                    pe.wait_ge(s_red, U * t.nM + k + 1)
                    pe.matmul(SM[k % 2], qcat[0:MAXROW, t.M.q, j, P * i:P * i + P], kcat[0:MAXROW, t.M.q, j, :],
                              start=True, stop=True).then_inc(s_sm, 1)

                def scores(t, u):
                    i, j = u // NH, u % NH
                    if u == 0:
                        pe.wait_ge(s_mrow, DMA * (t.nT + 2))
                    pe.wait_ge(s_exp, U * t.nT + u + 1)
                    pe.matmul(ST[u % 2], kcat[0:MAXROW + 2, t.T.q, j, P * i:P * i + P],
                          qcat[0:MAXROW + 2, t.T.q, j, :],
                              start=True, stop=True).then_inc(s_st, 1)

                def values(t, g):
                    if g == 0:
                        pe.wait_ge(s_vke, t.nT + 2)
                        pe.wait_ge(s_oev, t.nT + 1)
                    pe.wait_ge(s_exp, U * t.nT + NH * g + NH + 2)
                    for j in range(NH):
                        mm = pe.matmul(O[32 * j:32 * j + 32, :], vaug[:, t.T.q, 2 * (g % 2) + g // 2, j, :],
                                       probs[:, (NH * g + j) % 8, :], start=(g == 0), stop=(g == KC - 1),
                                       tile_position=(0, 32 * j), skip_group_check=True)
                    mm.then_inc(s_pv, 1)

                def slot(t):
                    if t.F:
                        pe.wait_ge(s_oev, t.nF + 2)
                        pe.wait_ge(s_lo, t.nP + 1)
                        pe.wait_ge(s_rec, t.nF + 1)
                        for c in range(KC):
                            mm = pe.transpose(X0[:, P * c:P * c + P], o_sb[:, P * c:P * c + P], ident[:, :])
                        mm.then_inc(s_ot, 1)
                    sm = 0
                    for g in range(KC):
                        for j in range(NH):
                            if t.T:
                                scores(t, NH * g + j)
                            if t.M and sm < U:
                                scores_for_max(t, sm)
                                sm += 1
                        if t.M and sm < U and g < 3:
                            for _ in range(1 if g < 2 else 2):
                                if sm < U:
                                    scores_for_max(t, sm)
                                    sm += 1
                        if t.T and g > 0:
                            values(t, g - 1)
                        if g == 0 and t.F:
                            pe.wait_ge(s_rw, t.nF + 1)
                            pe.wait_ge(s_vte, t.nP + 1)
                            pe.wait_ge(s_att, t.nF + 1)
                            for c in range(KC):
                                mm = pe.transpose(X1[:, P * c:P * c + P],
                                                  rec_wide[:, P * c:P * c + P], ident[:, :])
                            mm.then_inc(s_bt, 1)
                        if g == 2 and t.P:
                            pe.wait_ge(s_lo, t.nP + 1)
                            pe.wait_ge(s_rec, t.nF + (1 if t.F else 0) + 1)
                            pe.matmul(X0, wqk[:, t.P.branch, :], qk_view(t.P), start=True, stop=True) \
                                .then_inc(s_qk, 1)
                    if t.M:
                        pe.wait_ge(s_mxs, t.nM + 1)
                        pe.wait_ge(s_mxe, t.nM + 1)
                        pe.wait_ge(s_vke, t.nP + 1)
                        pe.transpose(X2[0:2 * U, 0:P], mx[:, t.M.q % 2, :], ident[:, :]).then_inc(s_mxt, 1)
                    if t.P:
                        pe.wait_ge(s_vte, t.nP + 1)
                        pe.wait_ge(s_att, t.nF + (1 if t.F else 0) + 1)
                        for a in range(2):
                            mm = pe.matmul(vt_psum(t.P, a), wv[:, t.P.branch, a, :], half_view(t.P, a),
                                           start=(a == 0), stop=(a == 1), skip_group_check=True)
                        mm.then_inc(s_vt, 1)
                    if t.T:
                        values(t, KC - 1)
                    if t.P:
                        pe.wait_ge(s_vte, t.nP + 2)
                        pe.wait_ge(s_mxe, t.nM + (1 if t.M else 0) + 1)
                        pe.wait_ge(s_vke, t.nP + 1)
                        for i in range(2):
                            mm = pe.transpose(X2[:, P * i:P * i + P], v_own[:, P * i:P * i + P], ident[:, :])
                        mm.then_inc(s_vk, 1)

                pipeline(pe, b, slot)
                phase_end(pe, b * 3 + 3)
                pe.wait_ge(s_fc, (b + 1) * 2 * DMA)

                def c_step(steps):
                    Y, M, N, A = steps
                    if M:
                        n = b * NW + M.i
                        pe.wait_ge(c_m, n + 2)
                        for f in range(NF):
                            pe.wait_ge(c_gl, NF * n + f + 1)
                            pe.matmul(CF[f % 2], fc1[:, P * f:P * f + P], c_mT, start=True, stop=True) \
                                .then_inc(c_f1, 1)
                    if Y:
                        n = b * NW + Y.i
                        pe.wait_ge(c_hf, n + 2)
                        pe.wait_ge(c_xo, n + 1)
                        pe.matmul(CY, wout[:, :], c_hfin, start=True, stop=True).then_inc(c_y, 1)
                    if N:
                        n = b * NW + N.i
                        pe.wait_ge(c_nm, n + 3)
                        pe.wait_ge(c_m, n + 1)
                        for t in range(4):
                            mm = pe.transpose(CT2[:, P * t:P * t + P], c_nh[:, P * t:P * t + P], ident[:, :])
                        mm.then_inc(c_t2, 1)
                    if A:
                        n = b * NW + A.i
                        pe.wait_ge(c_ld[A.k], 4 * DMA * (b * (NW // 4) + A.fill))
                        pe.wait_ge(c_hs, n + 1)
                        terms = [(wemb[:, 0, :], by_column(cx[:, 0, A.k, :])),
                                 (wpr[:, 0, :], att0[:, :].rearrange("p (m i x) -> p m i x", m=NW, i=NW)[:, :, A.i, :]),
                                 (wpr[:, 1, :], by_column(imgT[:, bass.ds(A.i * WT, WT)])),
                                 (wprc[:, :], cx[:, 1, A.k, :])]
                        for m, (w, v) in enumerate(terms):
                            mm = pe.matmul(CH, w, v, start=(m == 0), stop=(m == 3))
                        mm.then_inc(c_h, 1)

                    def second(fs):
                        n = b * NW + M.i
                        if fs[0] == 0:
                            pe.wait_ge(c_hf, n + 1)
                        for f in fs:
                            pe.wait_ge(c_gl, NF * n + f + 3)
                            mm = pe.matmul(CM, fc2[:, f, :], c_g[:, f, :], start=(f == 0), stop=(f == NF - 1))
                        if fs[-1] == NF - 1:
                            mm.then_inc(c_f2, 1)

                    if M:
                        second([0, 1])
                    if A:
                        n = b * NW + A.i
                        pe.wait_ge(c_hs, n + 2)
                        pe.wait_ge(c_nm, n + 2)
                        for t in range(4):
                            mm = pe.transpose(CT1[:, P * t:P * t + P], c_hT[:, A.k, P * t:P * t + P], ident[:, :])
                        mm.then_inc(c_t1, 1)
                    if M:
                        second([2, 3])

                stages(pe, NW, 4, 4, c_step)
                phase_end(pe, b * 3 + 4)

            pe.wait_ge(d_w, DMA * (G8 + 3))

            def d_step(cur, nxt):
                def turn():
                    pe.wait_ge(d_nm, nxt.i + 3)
                    pe.wait_ge(d_xt, 2 * nxt.i + 1)
                    for h in range(2):
                        for t in range(4):
                            mm = pe.transpose(DT[h][:, P * t:P * t + P], d_xl[:, 4 * h + t, :], ident[:, :])
                        mm.then_inc(d_tr, 1)

                def logits():
                    pe.wait_ge(d_xt, 2 * nxt.i + 3)
                    pe.wait_ge(d_g, nxt.i + 1)
                    for t in range(G8):
                        mm = pe.matmul(DL[:, E * t:E * t + E], d_xT[:, nxt.k, t, :], d_rw, start=True, stop=True)
                    mm.then_inc(d_lg, 1)

                def experts(ts):
                    for t in ts:
                        pe.wait_ge(d_cb, G8 * cur.i + t + 2)
                        pe.wait_ge(d_sc, G8 * cur.i + t + 2)
                        for h in range(2):
                            mm = pe.matmul(DY[t % 2][:, h, :], d_xT[:, cur.k, t, :],
                                           d_ew[:, 4 * h:4 * h + 4, :].rearrange("p e n -> p (e n)"),
                                           start=True, stop=True)
                        mm.then_inc(d_y, 1)

                if cur:
                    pe.wait_ge(d_g, cur.i + 2)
                    pe.wait_ge(d_bi, 2 * cur.i + 1)
                    settle(pe)
                    pe.transpose(DB[0:E * G8, 0:P], d_gate[:, cur.k, :, :].rearrange("p t e -> p (t e)"),
                                 ident[:, :]).then_inc(d_gt, 1)
                    experts([0])
                    for h in range(2):
                        pe.wait_ge(d_gte, cur.i + 2)
                        pe.wait_ge(d_bi, 2 * cur.i + h + 1)
                        pe.matmul(DB, d_gT, d_eb[:, 4 * h:4 * h + 4, :].rearrange("p t n -> p (t n)"),
                                  start=True, stop=True).then_inc(d_bm, 1)
                        experts([1 + h])
                if nxt:
                    turn()
                if cur:
                    experts([3, 4, 5])
                if nxt:
                    logits()
                if cur:
                    experts([6, 7])

            lookahead(pe, STEPS, 2, d_step)

        @block.scalar
        def _(act):
            start_up(act, ACT_OWNS)
            act.wait_ge(s_w, DMA * n_weights)
            act.mul(wqk[:, :, 0:HB], wqk[:, :, 0:HB], float(D) ** -0.5).then_inc(s_qs, 1)

            def n_step(cur, nxt):
                if cur:
                    act.wait_ge(n_rs, cur.i + 3)
                    act.wait_ge(n_st[cur.k], DMA * cur.fill)
                    for t in range(G8):
                        a = act.activation(rows_out[:, cur.k, t, :], rows_in[:, cur.k, t, :], ACT.Identity,
                                           bias=lnr[:, cur.k, 3, t:t + 1], scale=lnr[:, cur.k, 1, t:t + 1])
                    a.then_inc(n_nm, 1)

            lookahead(act, STEPS, 2, n_step)
            phase_end(act, 1)
            with act.Fori(0, B) as b:
                def a_step(cur, nxt):
                    if cur:
                        act.wait_ge(a_tr, b * NW + cur.i + 3)
                        act.activation(imgT[:, bass.ds(cur.i * WT, WT)], TB[cur.k % 2], ACT.Identity,
                                       bias=B1, scale=G1).then_inc(a_ev, 1)

                lookahead(act, NW, 8, a_step)
                phase_end(act, b * 3 + 2)

                def exponentials(t, u):
                    if u % NH == 0:
                        act.wait_ge(s_pv, KC * t.nT + u // NH + 15)
                    act.wait_ge(s_st, U * t.nT + u + 65)
                    act.activation(probs[:, u % 8, :], ST[u % 2], ACT.Exp).then_inc(s_exp, 1)

                def slot(t):
                    if t.T:
                        for u in range(12):
                            exponentials(t, u)
                    if t.P:
                        act.wait_ge(s_qk, t.nP + 1)
                        act.wait_ge(s_cat[(t.P.q + 2) % CATQ], DMA * CAT_DMAS * t.P.fills(2) + DMA)
                        act.copy(parts[:, t.P.q % 2, 0, :], X0).then_inc(s_hb, 1)
                    if t.T:
                        for u in range(12, U):
                            exponentials(t, u)
                    if t.M:
                        act.wait_ge(s_mxt, t.nM + 3)
                        act.wait_ge(s_mrow, DMA * (t.nM + 1))
                        act.mul(mxb[:, :], X2[0:2 * U, 0:P], 1 / MAXUNIT).then_inc(s_mxe, 1)
                    if t.P:
                        act.wait_ge(s_vt, t.nP + 1)
                        act.wait_ge(s_cv, t.nP + 1)
                        act.wait_ge(s_vk, t.nP + 1)
                        if t.P.branch == 0:
                            padded, made = vT[0][:, :, 1:5], X1[:, 0:264].rearrange("p (y c) -> p y c", c=SS)
                            own, inner = v_own[:, :].rearrange("p (y c) -> p y c", c=SS), made[:, 1:65, :]
                        else:
                            padded, made = vT[1][:, 1:5, :], X1[:, 0:264].rearrange("p (y c) -> p y c", y=SS)
                            own, inner = v_own[:, :].rearrange("p (y c) -> p y c", y=SS), made[:, :, 1:65]
                        act.copy(own, inner)
                        act.copy(padded, made).then_inc(s_vte, 1)
                    if t.T:
                        act.wait_ge(s_pv, KC * t.nT + KC + 16)
                        act.wait_ge(s_att, t.nT + 1)
                        act.copy(o_sb[:, :], O).then_inc(s_oev, 1)
                    if t.P:
                        act.wait_ge(s_vk, t.nP + 2)
                        act.wait_ge(s_pv, KC * (t.nP - 3) + 16)
                        act.copy(vaug[:, t.P.q, :, :, 0:D],
                                 X2[:, 0:KC * HB].rearrange("p (c j d) -> p c j d", c=KC, j=NH)) \
                            .then_inc(s_vke, 1)

                pipeline(act, b, slot)
                phase_end(act, b * 3 + 3)

                def c_step(steps):
                    M = steps[1]
                    if M:
                        n = b * NW + M.i
                        act.wait_ge(c_f2, n + 1)
                        for f in range(NF):
                            act.wait_ge(c_f1, NF * n + f + 2)
                            act.activation(c_g[:, f, :], CF[f % 2], ACT.Gelu, bias=BF1[f]).then_inc(c_gl, 1)

                stages(act, NW, 4, 4, c_step)
                phase_end(act, b * 3 + 4)

            def d_step(cur, nxt):
                def scale(ts):
                    for t in ts:
                        act.wait_ge(d_y, G8 * cur.i + t + 1)
                        act.wait_ge(d_out, G8 // 2 * cur.i + t // 2 + 2)
                        for e in range(E_ACT):
                            a = act.activation(d_scaled[:, e, t % 4, :],
                                               DY[t % 2][:, e // 4, P * (e % 4):P * (e % 4) + P],
                                               ACT.Copy, scale=d_gate[:, cur.k, t, e:e + 1])
                        a.then_inc(d_sc, 1)

                if cur:
                    act.wait_ge(d_gt, cur.i + 3)
                    act.wait_ge(d_bm, 2 * cur.i + 1)
                    act.copy(d_gT, DB[0:E * G8, 0:P]).then_inc(d_gte, 1)
                    scale([0, 1])
                if nxt:
                    act.wait_ge(d_rs, nxt.i + 3)
                    act.wait_ge(d_tr, 2 * nxt.i + 1)
                    for t in range(G8):
                        a = act.activation(d_xl[:, t, :], d_x[:, nxt.k, t, :], ACT.Identity,
                                           bias=lnr[:, nxt.k, 3, t:t + 1], scale=lnr[:, nxt.k, 1, t:t + 1])
                    a.then_inc(d_nm, 1)
                if cur:
                    scale([2, 3])
                if nxt:
                    for h in range(2):
                        act.wait_ge(d_tr, 2 * nxt.i + h + 2)
                        act.copy(d_xT[:, nxt.k, 4 * h:4 * h + 4, :].rearrange("p t n -> p (t n)"), DT[h]) \
                            .then_inc(d_xt, 1)
                if cur:
                    scale([4, 5, 6, 7])
                if nxt:
                    act.wait_ge(d_df, nxt.i + 1)
                    act.activation(d_s[:, 1, :], d_s[:, 0, :], ACT.Exp).then_inc(d_e2, 1)

            lookahead(act, STEPS, 2, d_step)

        @block.vector
        def _(dve):
            start_up(dve, DVE_OWNS)
            for tile in (wpr, wv, wemb, wout, vT[0], vT[1], vaug):
                shape = tile.shape
                dve.memset(tile[tuple(slice(None) for _ in shape)], 0.0).then_inc(s_dz, 1)
            dve.wait_ge(s_dz, 7)
            dve.memset(vaug[:, :, :, :, D:D + 1], 1.0)
            for i, v in enumerate((1e-6, 1e-5, -0.5, -1.0, 0.0)):
                dve.memset(konst[:, i, :], v)
            for e in range(E):
                dve.memset(konst[:, 5, e:e + 1], float(E - e))
            dve.drain().then_inc(s_set, 1)

            def moments(tiles, k, stats_sem, moments_sem, n):
                for t, tile in enumerate(tiles):
                    a = dve.bn_stats(stat[:, k, t, :], tile)
                a.then_inc(stats_sem, 1)
                dve.wait_ge(stats_sem, n + 1)
                settle(dve)
                for t in range(len(tiles)):
                    a = dve.bn_aggr(mv[:, k, t, :], stat[:, k, t, :])
                a.then_inc(moments_sem, 1)

            def n_step(cur, nxt):
                if nxt:
                    dve.wait_ge(n_ld[nxt.k], DMA * nxt.fill)
                    dve.wait_ge(n_rs, nxt.i + 1)
                    moments([rows_in[:, nxt.k, t, :] for t in range(G8)], nxt.k, n_bn, n_mv, nxt.i)

            lookahead(dve, STEPS, 2, n_step)
            phase_end(dve, 1)
            with dve.Fori(0, B) as b:
                def a_step(cur, nxt):
                    if nxt:
                        n = b * NW + nxt.i
                        dve.wait_ge(a_e, n + 9)
                        moments([EA[nxt.k % 4][:, P * t:P * t + P] for t in range(4)], nxt.k % 2, a_bn, a_mv, n)
                    if cur:
                        n = b * NW + cur.i
                        q = cur.k % 2
                        dve.wait_ge(a_rs, n + 1)
                        dve.wait_ge(a_tr, n + 1)
                        for t in range(4):
                            a = dve.tensor_scalar(ihat[:, q, P * t:P * t + P], EA[cur.k % 4][:, P * t:P * t + P],
                                                  lnr[:, q, 1, t:t + 1], lnr[:, q, 3, t:t + 1], ALU.mult, ALU.add)
                        a.then_inc(a_nm, 1)

                lookahead(dve, NW, 4, a_step)
                phase_end(dve, b * 3 + 2)

                def tile_max(t, k):
                    if k == 0:
                        dve.wait_ge(s_mxt, t.nM + 1)
                    j, i = k // KC, k % KC
                    dve.wait_ge(s_sm, U * t.nM + k + 1)
                    dve.tensor_reduce(mx[:, t.M.q % 2, k:k + 1], SM[k % 2], AX.X, ALU.max, negate=True) \
                        .then_inc(s_red, 1)

                def slot(t):
                    if t.M:
                        for k in range(3):
                            tile_max(t, k)
                    if t.F:
                        dve.wait_ge(s_ot, t.nF + 1)
                        dve.wait_ge(s_bt, t.nF + 1)
                        dve.reciprocal(rec[:, :, :], X0.rearrange("p (c j x) -> p c j x", c=KC, j=NH)[:, :, :, D]) \
                            .then_inc(s_rec, 1)
                        dve.wait_ge(s_rec, t.nF + 2)
                        dve.tensor_copy(rec_wide[:, :].rearrange("p (c j x) -> p (c j) x", c=KC, j=NH),
                                        rec[:, :, :].rearrange("p c j -> p (c j)").unsqueeze(2)
                                        .broadcast_to([P, KC * NH, 32])).then_inc(s_rw, 1)
                    if t.M:
                        for k in range(3, 9):
                            tile_max(t, k)
                    if t.F:
                        dve.wait_ge(s_bt, t.nF + 2)
                        if t.F.branch == 0:
                            dst, fold = att0[:, bass.ds(t.F.w * WT, WT)], lambda v: v
                        else:
                            dst = imgT[:, bass.ds(t.F.w * WT, WT)].rearrange("p (y a c) -> p a y c", y=SS, a=2)
                            fold = lambda v: v.rearrange("p (a y c) -> p a y c", a=2, y=SS)
                        dve.tensor_tensor(dst, fold(o_sb[:, :]), fold(X1), ALU.mult).then_inc(s_att, 1)
                    if t.M:
                        for k in range(9, U):
                            tile_max(t, k)
                        m = mx[:, t.M.q % 2, :]
                        dve.wait_ge(s_red, U * t.nM + U + 2)
                        dve.tensor_scalar(mxh[:, :], m[:, 0:U], 1 / MAXUNIT, None, ALU.mult).then_inc(s_mh, 1)
                        dve.wait_ge(s_mh, t.nM + 1)
                        dve.scalar_tensor_tensor(out=m[:, U:2 * U], in0=mxh[:, :], scalar=-MAXUNIT, in1=m[:, 0:U],
                                                 op0=ALU.mult, op1=ALU.add).then_inc(s_mxs, 1)
                    if t.P:
                        dve.wait_ge(s_hb, t.nP + 1)
                        dve.tensor_tensor(parts[:, t.P.q % 2, 1, :], X0, parts[:, t.P.q % 2, 0, :], ALU.subtract) \
                            .then_inc(s_lo, 1)

                pipeline(dve, b, slot)
                phase_end(dve, b * 3 + 3)

                def c_step(steps):
                    Y, M, N, A = steps
                    if N:
                        n = b * NW + N.i
                        q = N.k % 2
                        dve.wait_ge(c_rs, n + 1)
                        dve.wait_ge(c_t2, n + 1)
                        for t in range(4):
                            a = dve.tensor_scalar(c_nh[:, P * t:P * t + P], CT1[:, P * t:P * t + P],
                                                  lnr[:, q, 1, t:t + 1], lnr[:, q, 3, t:t + 1],
                                                  ALU.mult, ALU.add)
                        a.then_inc(c_nm, 1)
                    if Y:
                        n = b * NW + Y.i
                        q = Y.k % 2
                        dve.wait_ge(c_y, n + 2)
                        dve.wait_ge(c_st[q], DMA * (b * (NW // 2) + 2 * Y.fill - 1 + Y.k // 2))
                        dve.tensor_tensor(by_column(cxo[:, q, :]),
                                          CY[C0:P, :].rearrange("p (m y c) -> p m y c", m=NW, y=SS),
                                          by_column(cx[C0:P, 0, Y.k, :]), ALU.add).then_inc(c_xo, 1)
                    if N:
                        n = b * NW + N.i
                        dve.wait_ge(c_t2, n + 2)
                        dve.wait_ge(c_f1, NF * n + 1)
                        dve.tensor_scalar(c_mT, CT2, G2, B2, ALU.mult, ALU.add).then_inc(c_m, 1)
                    if A:
                        n = b * NW + A.i
                        dve.wait_ge(c_h, n + 1)
                        dve.tensor_scalar(c_hT[:, A.k, :], CH, BP, None, ALU.add).then_inc(c_hs, 1)
                        dve.wait_ge(c_t1, n + 1)
                        moments([CT1[:, P * t:P * t + P] for t in range(4)], A.k % 2, c_bn, c_mv, n)
                    if M:
                        n = b * NW + M.i
                        dve.wait_ge(c_f2, n + 2)
                        dve.scalar_tensor_tensor(out=c_hfin, in0=CM, scalar=BF2, in1=c_hT[:, M.k, :],
                                                 op0=ALU.add, op1=ALU.add).then_inc(c_hf, 1)

                stages(dve, NW, 4, 4, c_step)
                phase_end(dve, b * 3 + 4)

            dve.memset(d_eb, 0.0).then_inc(d_set, 1)
            dve.wait_ge(d_w, DMA * (G8 + 3))

            def spread(v):
                return v.unsqueeze(2).broadcast_to([P, G8, E])

            def over_tiles(v):
                return v.unsqueeze(1).broadcast_to([P, G8, E])

            GSTEP = 17

            def gating(j):
                base = GSTEP * j.i
                lg, pick, oh1, oh2, lg2 = (d_t[:, i, :, :] for i in range(5))
                m1, m2, top = d_s[:, 2, :], d_s[:, 3, :], d_s[:, 4, :]
                dve.tensor_tensor(lg, DL.rearrange("p (t e) -> p t e", e=E), over_tiles(d_rb), ALU.add) \
                    .then_inc(d_gs, 1)
                dve.wait_ge(d_gs, base + 1)
                dve.tensor_reduce(m1, lg, AX.X, ALU.max).then_inc(d_gs, 1)
                dve.wait_ge(d_gs, base + 2)
                dve.tensor_tensor(pick, lg, spread(m1), ALU.is_ge).then_inc(d_gs, 1)
                dve.wait_ge(d_gs, base + 3)
                dve.tensor_tensor(pick, pick, over_tiles(RANK), ALU.mult).then_inc(d_gs, 1)
                dve.wait_ge(d_gs, base + 4)
                dve.tensor_reduce(top, pick, AX.X, ALU.max).then_inc(d_gs, 1)
                dve.wait_ge(d_gs, base + 5)
                dve.tensor_tensor(oh1, pick, spread(top), ALU.is_equal).then_inc(d_gs, 1)
                dve.wait_ge(d_gs, base + 6)
                dve.scalar_tensor_tensor(out=lg2, in0=oh1, scalar=-1e38, in1=lg, op0=ALU.mult, op1=ALU.add) \
                    .then_inc(d_gs, 1)
                dve.wait_ge(d_gs, base + 7)
                dve.tensor_reduce(m2, lg2, AX.X, ALU.max).then_inc(d_gs, 1)
                dve.wait_ge(d_gs, base + 8)
                dve.wait_ge(d_e2, j.i + 1)
                dve.tensor_tensor(d_s[:, 0, :], m2, m1, ALU.subtract).then_inc(d_df, 1)
                dve.tensor_tensor(pick, lg2, spread(m2), ALU.is_ge).then_inc(d_gs, 1)
                dve.wait_ge(d_gs, base + 9)
                dve.tensor_tensor(pick, pick, over_tiles(RANK), ALU.mult).then_inc(d_gs, 1)
                dve.wait_ge(d_gs, base + 10)
                dve.tensor_reduce(top, pick, AX.X, ALU.max).then_inc(d_gs, 1)
                dve.wait_ge(d_gs, base + 11)
                dve.tensor_tensor(oh2, pick, spread(top), ALU.is_equal).then_inc(d_gs, 1)
                dve.wait_ge(d_gs, base + 12)
                dve.wait_ge(d_e2, j.i + 2)
                dve.tensor_scalar(d_s[:, 5, :], d_s[:, 1, :], 1.0, None, ALU.add).then_inc(d_gs, 1)
                dve.wait_ge(d_gs, base + 13)
                dve.reciprocal(d_s[:, 6, :], d_s[:, 5, :]).then_inc(d_gs, 1)
                dve.wait_ge(d_gs, base + 14)
                dve.tensor_tensor(d_s[:, 7, :], d_s[:, 6, :], d_s[:, 1, :], ALU.mult).then_inc(d_gs, 1)
                dve.wait_ge(d_gs, base + 15)
                dve.tensor_tensor(oh1, oh1, spread(d_s[:, 6, :]), ALU.mult).then_inc(d_gs, 1)
                dve.wait_ge(d_gs, base + 16)
                dve.tensor_tensor(oh2, oh2, spread(d_s[:, 7, :]), ALU.mult).then_inc(d_gs, 1)
                dve.wait_ge(d_gs, base + GSTEP)
                dve.wait_ge(d_gt, j.i + 1)
                dve.tensor_tensor(d_gate[:, j.k, :, :], oh1, oh2, ALU.add).then_inc(d_g, 1)

            def d_step(cur, nxt):
                if nxt:
                    dve.wait_ge(d_ld[nxt.k], DMA * nxt.fill)
                    dve.wait_ge(d_rs, nxt.i + 1)
                    moments([d_x[:, nxt.k, t, :] for t in range(G8)], nxt.k, d_bn, d_mv, nxt.i)
                if cur:
                    for t in range(G8):
                        if t in (1, 2):
                            h = t - 1
                            dve.wait_ge(d_st[cur.k], DMA * cur.fill)
                            dve.wait_ge(d_bm, 2 * cur.i + h + 2)
                            dve.tensor_tensor(d_acc[:, cur.k, 4 * h:4 * h + 4, :].rearrange("p t n -> p (t n)"), DB,
                                              d_x[:, cur.k, 4 * h:4 * h + 4, :].rearrange("p t n -> p (t n)"),
                                              ALU.add).then_inc(d_bi, 1)
                        dve.wait_ge(d_y, G8 * cur.i + t + 1)
                        dve.wait_ge(d_out, G8 // 2 * cur.i + t // 2 + 2)
                        half = (E - E_ACT) // 2
                        for m in range(half):
                            for z in range(2):
                                e = E_ACT + 2 * m + z
                                y, g = DY[t % 2][:, e // 4, P * (e % 4):P * (e % 4) + P], d_gate[:, cur.k, t, e:e + 1]
                                s = d_scaled[:, E_ACT + z, t % 4, :]
                                if m == 0:
                                    ins = dve.tensor_scalar(s, y, g, None, ALU.mult)
                                else:
                                    dve.wait_ge(d_ac, (half - 1) * 2 * (G8 * cur.i + t) + 2 * (m - 1) + z + 1)
                                    ins = dve.scalar_tensor_tensor(out=s, in0=y, scalar=g, in1=s,
                                                                   op0=ALU.mult, op1=ALU.add)
                                if m < half - 1:
                                    ins.then_inc(d_ac, 1)
                        ins.then_inc(d_cb, 1)
                if nxt:
                    dve.wait_ge(d_lg, nxt.i + 1)
                    gating(nxt)

            lookahead(dve, STEPS, 2, d_step)

        @block.gpsimd
        def _(pool):
            start_up(pool, POOL_OWNS)
            pool.memset(ident[:, :], 0.0).then_inc(s_id, 1)
            pool.wait_ge(s_id, 1)
            pool.affine_select(out=ident[:, :], in_=ident[:, :], compare_op=ALU.not_equal, fill=1.0, base=0,
                               pattern=[[-1, P]], channel_multiplier=1).then_inc(s_id, 1)
            pool.wait_ge(s_set, 1)

            def ln_small(m, to, n, eps, step, steps_before, done):
                pool.tensor_tensor(to[:, 0, 0:n], m[:, 0:n, 1], eps[:, 0:n], ALU.add).then_inc(step, 1)
                pool.wait_ge(step, steps_before + 1)
                pool.tensor_tensor(to[:, 1, 0:n], to[:, 0, 0:n], NHALF[:, 0:n], ALU.pow).then_inc(step, 1)
                pool.wait_ge(step, steps_before + 2)
                pool.tensor_tensor(to[:, 2, 0:n], m[:, 0:n, 0], to[:, 1, 0:n], ALU.mult).then_inc(step, 1)
                pool.wait_ge(step, steps_before + 3)
                pool.tensor_tensor(to[:, 3, 0:n], to[:, 2, 0:n], NEG1[:, 0:n], ALU.mult).then_inc(done, 1)

            def n_step(cur, nxt):
                if nxt:
                    pool.wait_ge(n_mv, nxt.i + 1)
                    pool.wait_ge(n_nm, nxt.i + 1)
                    ln_small(mv[:, nxt.k], lnr[:, nxt.k], G8, EPS6, n_ln, 3 * nxt.i, n_rs)

            lookahead(pool, STEPS, 2, n_step)
            phase_end(pool, 1)
            with pool.Fori(0, B) as b:
                def a_step(cur, nxt):
                    if nxt:
                        n = b * NW + nxt.i
                        pool.wait_ge(a_mv, n + 1)
                        pool.wait_ge(a_nm, n + 3)
                        ln_small(mv[:, nxt.k % 2], lnr[:, nxt.k % 2], 4, EPS5, a_ln, 3 * n, a_rs)

                lookahead(pool, NW, 4, a_step)
                phase_end(pool, b * 3 + 2)
                pool.memset(workb[PAIRS:MAXROW, 0:16384], 0.0)
                pool.memset(kcat[MAXROW:MAXROW + 2, :, :, :].rearrange("p q j n -> p (q j n)"), MAXUNIT)
                pool.drain().then_inc(s_kset, 1)
                CVS = 16

                def slot(t):
                    if not t.P:
                        return
                    br = t.P.branch
                    pool.wait_ge(s_vte, t.nP + 2)
                    pool.wait_ge(s_cvd0, t.P.conv_free[0] + DMA)
                    pool.wait_ge(s_cvd1, t.P.conv_free[1] + DMA)
                    shape = dict(y=64) if br == 0 else dict(y=SS)

                    def grid(v):
                        return v.rearrange("p (y c) -> p y c", **shape)

                    def tap(n):
                        y, c = n // 3, n % 3
                        return vT[0][:, y:y + 64, c:c + 4] if br == 0 else vT[1][:, y:y + 4, c:c + 64]

                    base = CVS * t.nP
                    pool.wait_ge(s_cv, t.nP + 1)
                    settle(pool)
                    pool.tensor_scalar(grid(cv_acc[:, :]), tap(0), cw[:, br, 0:1], cb[:, br:br + 1],
                                       ALU.mult, ALU.add).then_inc(s_cvc, 1)
                    for n in range(1, 9):
                        pool.tensor_scalar(grid(cv_tmp[:, :]), tap(n), cw[:, br, n:n + 1], 0.0,
                                           ALU.mult, ALU.add).then_inc(s_cvc, 1)
                        pool.wait_ge(s_cvc, base + 2 * n)
                        if n < 8:
                            pool.tensor_tensor(cv_acc[:, :], cv_acc[:, :], cv_tmp[:, :], ALU.add) \
                                .then_inc(s_cvc, 1)
                            pool.wait_ge(s_cvc, base + 2 * n + 1)
                            settle(pool)
                    if br == 0:
                        ins = pool.tensor_tensor(cv_out[:, :], cv_acc[:, :], cv_tmp[:, :], ALU.add)
                    else:
                        v = [z[:, :].rearrange("p (y m c) -> p y m c", y=SS, m=16) for z in (cv_acc, cv_tmp)]
                        ins = pool.tensor_tensor(cv_out[:, :].rearrange("p (m y c) -> p y m c", y=SS, m=16),
                                                 v[0], v[1], ALU.add)
                    ins.then_inc(s_cv, 1)

                pipeline(pool, b, slot)
                phase_end(pool, b * 3 + 3)

                def c_step(steps):
                    A = steps[3]
                    if A:
                        n = b * NW + A.i
                        pool.wait_ge(c_mv, n + 1)
                        pool.wait_ge(c_nm, n + 1)
                        ln_small(mv[:, A.k % 2], lnr[:, A.k % 2], 4, EPS5, c_ln, 3 * n, c_rs)

                stages(pool, NW, 4, 4, c_step)
                phase_end(pool, b * 3 + 4)

            SUMS = E_ACT

            def d_step(cur, nxt):
                def total(pairs):
                    for h in pairs:
                        n = G8 // 2 * cur.i + h
                        pool.wait_ge(d_sc, G8 * cur.i + 2 * h + 5)
                        pool.wait_ge(d_cb, G8 * cur.i + 2 * h + 5)
                        pool.wait_ge(d_bi, 2 * cur.i + h // 2 + 2)
                        v = [d_scaled[:, e, 2 * (h % 2):2 * (h % 2) + 2, :] for e in range(E_ACT + 2)]
                        acc = d_acc[:, cur.k, 2 * h:2 * h + 2, :]
                        pool.tensor_tensor(v[0], v[0], v[1], ALU.add).then_inc(d_sum, 1)
                        pool.tensor_tensor(v[2], v[2], v[3], ALU.add).then_inc(d_sum, 1)
                        pool.tensor_tensor(v[4], v[4], v[5], ALU.add).then_inc(d_sum, 1)
                        pool.wait_ge(d_sum, SUMS * n + 2)
                        pool.tensor_tensor(v[0], v[0], v[2], ALU.add).then_inc(d_sum, 1)
                        pool.wait_ge(d_sum, SUMS * n + 3)
                        pool.tensor_tensor(acc, acc, v[4], ALU.add).then_inc(d_ps, 1)
                        pool.wait_ge(d_sum, SUMS * n + 4)
                        pool.wait_ge(d_ps, n + 1)
                        pool.tensor_tensor(acc, acc, v[0], ALU.add).then_inc(d_out, 1)

                if nxt:
                    pool.wait_ge(d_mv, nxt.i + 1)
                    pool.wait_ge(d_nm, nxt.i + 1)
                    ln_small(mv[:, nxt.k], lnr[:, nxt.k], G8, EPS5, d_ln, 3 * nxt.i, d_rs)
                if cur:
                    total(range(G8 // 2))

            lookahead(pool, STEPS, 2, d_step)


_INS = ["x", "L0_conv_w_embed", "L0_conv_g1", "L0_conv_b1", "L0_conv_w_qkv", "L0_conv_conv_w0", "L0_conv_conv_b0",
        "L0_conv_conv_w1", "L0_conv_conv_b1", "L0_conv_w_proj", "L0_conv_b_proj", "L0_conv_g2", "L0_conv_b2",
        "L0_conv_w_fc1", "L0_conv_b_fc1", "L0_conv_w_fc2", "L0_conv_b_fc2", "L0_conv_w_out", "L0_ffn_router_w",
        "L0_ffn_router_b", "L0_ffn_expert_w", "L0_ffn_expert_b"]


def kernel(**inputs):
    import numpy as _np
    import concourse.bacc as _bacc
    from concourse.bass_utils import run_bass_kernel_spmd as _run

    nc = _bacc.Bacc("TRN2", target_bir_lowering=False, num_devices=1)
    arrays, args = {}, []
    for name in _INS:
        a = _np.ascontiguousarray(inputs[name])
        arrays[f"in_{name}"] = a
        args.append(nc.dram_tensor(f"in_{name}", a.shape, mybir.dt.from_np(a.dtype), kind="ExternalInput").ap())
    args.append(nc.dram_tensor("out", (B, C0, H, W), F32, kind="ExternalOutput").ap())
    build(nc, *args)
    r = _run(nc, [arrays], core_ids=[0])
    return r.results[0]["out"]
```

```python
from contextlib import ExitStack

import concourse.bass as bass
from concourse import mybir

F32 = mybir.dt.float32
FP16 = mybir.dt.float16
ALU = mybir.AluOpType
ACT = mybir.ActivationFunctionType
AX = mybir.AxisListType

P = 128
B, C0, H, W = 4, 64, 128, 128
C = 2 * C0
NBR = 2
HB = C // 2
NH = 4
D = HB // NH
SS = 4
WT = H * SS
NW = H // SS
TOK = H * W
KC = WT // P
FF = 4 * C
NF = FF // P
E = 8
E_ACT = 4
U = NH * KC
CATQ = 4
PAIRS = 4 * D
MAXROW = 96
MAXUNIT = 1024.0
G8 = 8
STEPS = B * C0 // G8
DMA = 16
CAT_DMAS = 4 * NH // 2


class Window:

    def __init__(self, b, it, k):
        self.branch = 1 if k >= NW else 0
        self.q = k % CATQ
        self.w = 4 * it + (k - NW * self.branch)
        self.g = b * (NBR * NW) + 4 * it + k
        before = [b * NW + (self.w if self.branch == br else NW * self.branch) for br in range(NBR)]
        self.conv_free = (2 * DMA * before[0], DMA * before[1])
        self._quads = b * (NBR * NW // 4) + it
        self._k = k

    def fills(self, back):
        return self._quads + (self._k - back) // 4 + 1


class Step:

    def __init__(self, it, k, u):
        self.i, self.k, self.fill = u * it + k, k % u, it + k // u + 1


def stages(eng, n, u, depth, body):
    def peeled(slots):
        for s in slots:
            body([Step(0, s + a, u) if 0 <= s + a < n else None for a in range(depth)])

    its = (n - depth + 1) // u
    peeled(range(1 - depth, 0))
    with eng.Fori(0, its) as it:
        for k in range(u):
            body([Step(it, k + a, u) for a in range(depth)])
    peeled(range(its * u, n))


def lookahead(eng, n, u, body):
    stages(eng, n, u, 2, lambda steps: body(*steps))


class Slot:

    def __init__(self, b, it, s, loop):
        def stage(ahead):
            c = s + ahead
            n = NBR * NW
            inside = loop or 0 <= c < n
            window = Window(b, it, c) if inside else None
            count = window.g if inside else b * n + min(max(c, 0), n)
            return window, count

        self.P, self.nP = stage(3)
        self.L, self.nL = stage(2)
        self.M, self.nM = stage(2)
        self.first_M = not loop and s == -2
        self.R, self.nR = stage(1)
        self.T, self.nT = stage(0)
        self.F, self.nF = stage(-1)


def pipeline(eng, b, body):
    for s in range(-3, 1):
        body(Slot(b, 0, s, False))
    with eng.Fori(0, 7) as it:
        for k in range(1, 5):
            body(Slot(b, it, k, True))
    for s in range(29, 33):
        body(Slot(b, 0, s, False))
    with eng.Fori(0, 7) as it:
        for k in range(1, 5):
            body(Slot(b, it, NW + k, True))
    for s in range(61, 65):
        body(Slot(b, 0, s, False))


def build(nc, x, w_embed, g1, b1, w_qkv, conv_w0, conv_b0, conv_w1, conv_b1, w_proj, b_proj, g2, b2,
          w_fc1, b_fc1, w_fc2, b_fc2, w_out, router_w, router_b, expert_w, expert_b, out):
    xn_d = nc.dram_tensor("xn_scratch", (B * C0, H, W), F32).ap()
    x2_d = nc.dram_tensor("x2_scratch", (B * C0, H, W), F32).ap()
    conv0_d = nc.dram_tensor("conv0_scratch", (B, NW, HB, WT), F32).ap()
    conv1_d = nc.dram_tensor("conv1_scratch", (B, NW, 2, HB, WT // 2), F32).ap()
    x_rows = x.rearrange("b c h m -> (b c) h m")
    out_rows = out.rearrange("b c h m -> (b c) h m")

    with ExitStack() as ctx:
        def sb(name, shape, dt=F32):
            return ctx.enter_context(nc.sbuf_tensor(name, shape, dt))

        def sem(name):
            return ctx.enter_context(nc.semaphore(name))

        imgT = sb("imgT", [P, TOK])
        att0 = sb("att0", [P, TOK])
        work = sb("work", [P, 12288])
        vaug = sb("vaug", [P, 4, KC, NH, 32])
        parts = sb("parts", [P, 2, 2, WT], FP16)
        o_sb = sb("o_sb", [P, WT])
        vT = [sb("vT0", [P, 66, 6]), sb("vT1", [P, 6, 66])]
        v_own = sb("v_own", [P, 256])
        cv_acc = sb("cv_acc", [P, 256])
        cv_tmp = [sb(f"cv_tmp{i}", [P, 256]) for i in range(2)]
        cv_out = sb("cv_out", [P, 256])
        wqk = sb("wqk", [P, NBR, P])
        wv = sb("wv", [P, NBR, 3 * HB])
        ident = sb("ident", [P, P])
        wemb = sb("wemb", [P, 2, C])
        wpr = sb("wpr", [P, NBR, C])
        wprc = sb("wprc", [P, C])
        wout = sb("wout", [P, P])
        cw = sb("cw", [P, NBR, 9])
        cb = sb("cb", [P, NBR])
        cols = sb("cols", [P, 10 + NF])
        mx = sb("mx", [P, 2, 32])
        mxh = sb("mxh", [P, U], FP16)
        mxb = sb("mxb", [2 * U, P], FP16)
        rec = sb("rec", [P, KC, NH])
        rec_wide = sb("rec_wide", [P, WT])
        stat = sb("stat", [P, 2, 8, 6])
        mv = sb("mv", [P, 2, 8, 2])
        lnr = sb("lnr", [P, 2, 4, 8])
        konst = sb("konst", [P, 5, 8])
        G1, B1, G2, B2, BP, BF2 = (cols[:, i:i + 1] for i in range(6))
        BF1 = [cols[:, 10 + i:11 + i] for i in range(NF)]
        EPS6, EPS5, NHALF, NEG1 = (konst[:, i, :] for i in range(4))
        RANK = konst[:, 4, :]

        workb = work[:, :].bitcast(FP16)
        qcat = workb[:, 0:8192].rearrange("p (q j n) -> p q j n", q=CATQ, j=NH)
        kcat = workb[:, 8192:16384].rearrange("p (q j n) -> p q j n", q=CATQ, j=NH)
        probs = work[:, 8192:12288].rearrange("p (u n) -> p u n", u=8)
        rows_in = work[:, 0:4096].rearrange("p (q t m) -> p q t m", q=4, t=G8)
        rows_out = work[:, 4096:8192].rearrange("p (q t m) -> p q t m", q=4, t=G8)
        xa = work[:, 0:2048].rearrange("p (q n) -> p q n", q=4)
        ihat = work[:, 2048:3072].rearrange("p (q n) -> p q n", q=2)
        cx = work[:, 0:4096].rearrange("p (t q n) -> p t q n", t=2, q=4)
        cxo = work[C0:P, 4096:5120].rearrange("p (q n) -> p q n", q=2)
        c_hT = work[:, 5120:7168].rearrange("p (q n) -> p q n", q=4)
        c_nh, c_mT, c_hfin = work[:, 7168:7680], work[:, 7680:8192], work[:, 8192:8704]
        fc1 = work[:, 8704:9216]
        fc2 = work[:, 9216:9728].rearrange("p (f n) -> p f n", f=NF)
        c_g = work[:, 9728:11776].rearrange("p (f n) -> p f n", f=NF)
        d_x = att0[:, 0:4096].rearrange("p (q t m) -> p q t m", q=4, t=G8)
        d_acc = work[:, 2048:4096].rearrange("p (q t m) -> p q t m", q=2, t=G8)
        d_xl = work[:, 4096:5120].rearrange("p (t m) -> p t m", t=G8)
        d_xT = att0[:, 4096:8192].rearrange("p (q t m) -> p q t m", q=4, t=G8)
        d_ew = work[:, 7168:8192].rearrange("p (e m) -> p e m", e=E)
        d_eb = work[0:E * G8, 8192:9216].rearrange("p (t m) -> p t m", t=G8)
        d_gT = work[0:E * G8, 9216:9344]
        d_gate = work[:, 9344:9472].rearrange("p (q t e) -> p q t e", q=2, t=G8)
        d_t = work[:, 9472:9792].rearrange("p (i t e) -> p i t e", i=5, t=G8)
        d_s = work[:, 9792:9856].rearrange("p (i t) -> p i t", i=8)
        d_scaled = imgT[:, 0:4096].rearrange("p (e u n) -> p e u n", e=8, u=4)
        d_rw, d_rb = work[:, 9856:9864], work[:, 9864:9872]

        ps = ctx.enter_context(nc.psum_tensor("ps", [P, 8, 512], F32))
        bank = [ps[:, i, :] for i in range(8)]
        SM, ST, O, X0, X1, X2 = bank[0:2], bank[2:4], bank[4], bank[5], bank[6], bank[7]
        EA, TB = bank[0:4], bank[4:6]
        CH, CT1, CT2, CF, CM, CY = bank[0], bank[1], bank[2], bank[3:5], bank[5], bank[6]
        DT, DL, DB, DY = bank[0:2], bank[2][:, 0:E * G8], bank[3], [ps[:, 4:6, :], ps[:, 6:8, :]]

        s_settled = sem("settled")
        s_phase = sem("phase")
        s_w, s_fc, d_w = sem("weights"), sem("mlp_weights"), sem("expert_weights")
        n_ld = [sem(f"n_load{i}") for i in range(4)]
        n_st = [sem(f"n_written{i}") for i in range(4)]
        a_ld = [sem(f"a_load{i}") for i in range(4)]
        s_cat = [[sem(f"cat_heads{2 * h}_{i}") for i in range(CATQ)] for h in range(2)]
        s_mrow = sem("max_rows_filled")
        s_cvd0, s_cvd1 = sem("conv0_written"), sem("conv1_written")
        c_ld = [sem(f"c_load{i}") for i in range(4)]
        c_st = [sem(f"c_written{i}") for i in range(2)]
        d_ld = [sem(f"d_load{i}") for i in range(4)]
        d_st = [sem(f"d_written{i}") for i in range(2)]
        SP_OWNS = {DMA: n_st + s_cat[0] + s_cat[1] + [s_mrow, s_cvd0, s_cvd1] + c_st + d_st}

        s_qk, s_vt, s_vk = sem("qk_made"), sem("vT_made"), sem("v_by_key_made")
        s_mxt, s_sm, s_st = sem("max_turned"), sem("max_scores"), sem("scores")
        s_pv, s_ot, s_bt = sem("values_summed"), sem("out_turned"), sem("recip_spread")
        a_e, a_tr = sem("a_embedded"), sem("a_turned")
        c_h, c_t1, c_t2 = sem("c_h"), sem("c_turned"), sem("c_turned_back")
        c_f1, c_f2, c_y = sem("c_fc1"), sem("c_fc2"), sem("c_y")
        d_tr, d_lg, d_gt = sem("d_turned"), sem("d_logits"), sem("d_gates_turned")
        d_bm, d_y = sem("d_bias_made"), sem("d_experts")
        PE_OWNS = {1: [s_vk, s_bt, c_t2, c_f1, c_f2, c_y, d_tr, d_bm],
                   2: [s_mxt, a_tr, d_gt],
                   8: [a_e],
                   16: [s_pv],
                   64: [s_st]}

        s_qs, s_exp = sem("q_scaled"), sem("exp_done")
        s_hb = sem("high_part")
        s_vte, s_vke, s_mxe = sem("vT_stored"), sem("v_by_key_stored"), sem("max_stored")
        s_oev = sem("out_stored")
        n_nm, a_nm, a_ev = sem("n_normed"), sem("a_normed"), sem("a_image")
        c_hs, c_gl, c_m = sem("c_h_stored"), sem("c_gelu"), sem("c_mlp_in")
        d_nm, d_xt, d_gte, d_e2 = sem("d_normed"), sem("d_xT"), sem("d_gT"), sem("d_exp")
        d_sc = sem("d_experts_scaled")
        ACT_OWNS = {1: [s_vte, s_vke, s_mxe, s_oev, d_xt, d_gte, d_e2],
                    2: [s_exp, n_nm, a_ev, c_gl, d_nm],
                    4: [a_nm],
                    3: [d_sc]}

        s_dz, s_set, d_set = sem("zeros_set"), sem("constants_set"), sem("d_zeros_set")
        s_red, s_mh, s_mxs = sem("tile_max"), sem("max_high"), sem("max_split")
        s_lo, s_rec, s_att = sem("low_part"), sem("recip_done"), sem("att_stored")
        s_rw = sem("recip_widened")
        n_bn, n_mv, a_bn, a_mv = sem("n_stats"), sem("n_moments"), sem("a_stats"), sem("a_moments")
        c_bn, c_mv, d_bn, d_mv = sem("c_stats"), sem("c_moments"), sem("d_stats"), sem("d_moments")
        c_nm, c_hf, c_xo = sem("c_normed"), sem("c_sum"), sem("c_x_out")
        d_gs, d_df, d_g = sem("d_gate_step"), sem("d_logit_gap"), sem("d_gates")
        d_bi, d_ac, d_cb = sem("d_bias_added"), sem("d_expert_added"), sem("d_combined")
        DVE_OWNS = {1: [s_lo, s_rec, s_att, c_m, c_hs, c_hf, c_xo, d_g, d_bi],
                    2: [c_nm],
                    2 * U + 2: [s_red],
                    3: [d_cb]}

        s_id, s_kset = sem("identity_set"), sem("fixed_rows_set")
        s_cv, s_cvc = sem("conv_done"), sem("conv_step")
        n_ln, n_rs, a_ln, a_rs = sem("n_ln_step"), sem("n_rstd"), sem("a_ln_step"), sem("a_rstd")
        c_ln, c_rs, d_ln, d_rs = sem("c_ln_step"), sem("c_rstd"), sem("d_ln_step"), sem("d_rstd")
        d_sum, d_out = sem("d_sum_step"), sem("d_summed")
        POOL_OWNS = {1: [s_cv],
                     2: [n_rs, a_rs, d_rs],
                     3: [d_out]}

        block = ctx.enter_context(nc.Block())
        ENGINES = 5

        def settle(eng):
            eng.sem_inc(s_settled, 1)

        def phase_end(eng, n):
            settle(eng)
            eng.drain().then_inc(s_phase, 1)
            eng.wait_ge(s_phase, ENGINES * n)
            settle(eng)

        n_weights = 36

        def start_up(eng, owns):
            for start, sems in owns.items():
                for s in sems:
                    eng.sem_inc(s, start)

        def qk_view(win):
            if win.branch == 0:
                return imgT[:, :].rearrange("p (h m c) -> p h m c", m=NW, c=SS)[:, :, win.w, :]
            return imgT[:, bass.ds(win.w * WT, WT)].rearrange("p (y a c) -> p a y c", y=SS, a=2)

        def half_view(win, a):
            if win.branch == 0:
                return imgT[:, :].rearrange("p (h m c) -> p h m c", m=NW, c=SS)[:, 63 * a:63 * a + 65, win.w, :]
            return imgT[:, bass.ds(win.w * WT, WT)].rearrange("p (y c) -> p y c", y=SS)[:, :, 63 * a:63 * a + 65]

        def vt_psum(win, a):
            lo = 1 - a
            if win.branch == 0:
                return X1[:, 0:264].rearrange("p (y c) -> p y c", c=SS)[:, lo:lo + 65, :]
            return X1[:, 0:264].rearrange("p (y c) -> p y c", y=SS)[:, :, lo:lo + 65]

        def by_column(ap):
            return ap.rearrange("p (y m c) -> p m y c", y=SS, m=NW)

        @block.sync
        def _(sp):
            start_up(sp, SP_OWNS)

            def n_load(s, q):
                sp.dma_start(rows_in[:, q], x_rows[bass.ds(s * G8, G8)].rearrange("c h m -> h c m")) \
                    .then_inc(n_ld[q], DMA)

            for q in range(4):
                n_load(q, q)

            def load(dst, src):
                sp.dma_start(dst, src).then_inc(s_w, DMA)

            sp.wait_ge(s_set, 1)
            for h in range(2):
                load(wemb[C0 * h:C0 * h + C0, h, :], w_embed)
            load(wout[:, C0:P], w_out)
            load(wprc[:, :], w_proj)
            for br in range(NBR):
                load(wqk[:, br, 0:HB], w_qkv[:, HB * br:HB * br + HB])
                load(wqk[:, br, HB:P], w_qkv[:, C + HB * br:C + HB * br + HB])
                load(wv[:, br, HB:2 * HB], w_qkv[:, 2 * C + HB * br:2 * C + HB * br + HB])
                for a in range(2):
                    load(cw[HB * a:HB * a + HB, br, :],
                         (conv_w0, conv_w1)[br].rearrange("c o y s -> c (o y s)"))
                    load(cb[HB * a:HB * a + HB, br:br + 1], (conv_b0, conv_b1)[br].rearrange("(c o) -> c o", o=1))
                for j in range(NH):
                    load(wpr[32 * j:32 * j + D, br, :], w_proj[HB * br + D * j:HB * br + D * j + D, :])
            for i, v in enumerate((g1, b1, g2, b2, b_proj, b_fc2)):
                load(cols[:, i:i + 1], v.rearrange("(c o) -> c o", o=1))
            for f in range(NF):
                load(cols[:, 10 + f:11 + f], b_fc1[P * f:P * f + P].rearrange("(c o) -> c o", o=1))

            def n_store(s, q):
                sp.wait_ge(n_nm, s + 3)
                settle(sp)
                sp.dma_start(xn_d[bass.ds(s * G8, G8)].rearrange("c h m -> h c m"), rows_out[:, q]) \
                    .then_inc(n_st[q], DMA)

            with sp.Fori(0, STEPS // 4 - 1) as it:
                for q in range(4):
                    n_store(it * 4 + q, q)
                    n_load(it * 4 + q + 4, q)
            for q in range(4):
                n_store(STEPS - 4 + q, q)
            for q in range(4):
                sp.wait_ge(n_st[q], DMA * (STEPS // 4 + 1))
                settle(sp)
            phase_end(sp, 1)

            with sp.Fori(0, B) as b:
                with sp.Fori(0, NW // 8) as it:
                    for q in range(4):
                        for h in range(2):
                            i = it * 8 + 2 * q + h
                            if h == 0:
                                sp.wait_ge(a_e, b * NW + i + 2)
                                settle(sp)
                            sp.dma_start(xa[C0 * h:C0 * h + C0, q, :],
                                         xn_d[bass.ds(b * C0, C0), bass.ds(i * SS, SS), :]
                                         .rearrange("c y m -> c (y m)")).then_inc(a_ld[q], DMA)
                phase_end(sp, b * 3 + 2)

                def slot(t):
                    if t.P:
                        sp.wait_ge(s_lo, t.nP + 2)
                        sp.wait_ge(s_st, U * (t.nP - 3) + 64)
                        settle(sp)
                    for j in range(NH):
                        if t.P:
                            for side, cat in ((0, qcat), (1, kcat)):
                                for half in range(2):
                                    s = parts[HB * side + D * j:HB * side + D * j + D, t.P.q % 2, :, :]
                                    rows = bass.AP(tensor=s.tensor, offset=s.offset + (0 if side else WT * half),
                                                   ap=[[s.ap[0][0], D], [WT if side else 0, 2], [1, WT]])
                                    sp.dma_start(cat[2 * D * half:2 * D * half + 2 * D, t.P.q, j, :], rows) \
                                        .then_inc(s_cat[j // 2][t.P.q], DMA)
                        if j == 0 and t.R:
                            sp.wait_ge(s_mxe, t.nR + 2)
                            settle(sp)
                            sp.dma_start(qcat[MAXROW:MAXROW + 2, t.R.q].rearrange("p j n -> p (j n)"), mxb[:, :]) \
                                .then_inc(s_mrow, DMA)
                        if j == 1 and t.L:
                            sp.wait_ge(s_cv, t.nL + 2)
                            settle(sp)
                            if t.L.branch == 0:
                                for a in range(2):
                                    sp.dma_start(conv0_d[b, 16 * a:16 * a + 16, :, bass.ds(t.L.w * 16, 16)]
                                                 .rearrange("i c x -> c i x"),
                                                 cv_out[HB * a:HB * a + HB, :].rearrange("p (i x) -> p i x", x=16)) \
                                        .then_inc(s_cvd0, DMA)
                            else:
                                sp.dma_start(conv1_d[b, t.L.w].rearrange("a c n -> (a c) n"), cv_out[:, :]) \
                                    .then_inc(s_cvd1, DMA)

                pipeline(sp, b, slot)
                sp.wait_ge(s_cvd0, (b + 1) * (NW * 2 * DMA) + DMA)
                settle(sp)
                sp.wait_ge(s_cvd1, (b + 1) * (NW * DMA) + DMA)
                settle(sp)
                phase_end(sp, b * 3 + 3)

                sp.dma_start(fc1, w_fc1).then_inc(s_fc, DMA)
                sp.dma_start(fc2, w_fc2.rearrange("(f p) n -> p f n", p=P)).then_inc(s_fc, DMA)

                def c_load(i, q):
                    for h, src in enumerate((xn_d, x_rows)):
                        sp.dma_start(cx[C0 * h:C0 * h + C0, 0, q, :], src[bass.ds(b * C0, C0), bass.ds(i * SS, SS), :]
                                     .rearrange("c y m -> c (y m)")).then_inc(c_ld[q], DMA)
                    sp.dma_start(cx[0:HB, 1, q, :], conv0_d[b, i]).then_inc(c_ld[q], DMA)
                    sp.dma_start(cx[HB:P, 1, q, :].rearrange("p (a n) -> p a n", a=2),
                                 conv1_d[b, i].rearrange("a c n -> c a n")).then_inc(c_ld[q], DMA)

                def c_store(i, q):
                    sp.wait_ge(c_xo, b * NW + i + 2)
                    settle(sp)
                    sp.dma_start(x2_d[bass.ds(b * C0, C0), bass.ds(i * SS, SS), :].rearrange("c y m -> c (y m)"),
                                 cxo[:, q % 2, :]).then_inc(c_st[q % 2], DMA)

                for q in range(4):
                    c_load(q, q)
                with sp.Fori(0, NW // 4 - 1) as it:
                    for q in range(4):
                        c_store(it * 4 + q, q)
                        c_load(it * 4 + q + 4, q)
                for q in range(4):
                    c_store(NW - 4 + q, q)
                for q in range(2):
                    sp.wait_ge(c_st[q], (b + 1) * (DMA * NW // 2) + DMA)
                    settle(sp)
                phase_end(sp, b * 3 + 4)

            def d_load(s, q):
                sp.dma_start(d_x[:, q], x2_d[bass.ds(s * G8, G8)].rearrange("c h m -> h c m")) \
                    .then_inc(d_ld[q], DMA)

            def d_store(s, q):
                sp.wait_ge(d_out, G8 // 2 * (s + 1) + 3)
                settle(sp)
                sp.dma_start(out_rows[bass.ds(s * G8, G8)].rearrange("c h w -> h c w"), d_acc[:, q]) \
                    .then_inc(d_st[q], DMA)

            sp.dma_start(d_rw, router_w).then_inc(d_w, DMA)
            sp.dma_start(d_ew, expert_w.rearrange("e d c -> d e c")).then_inc(d_w, DMA)
            sp.wait_ge(d_set, 1)
            settle(sp)
            for t in range(G8):
                sp.dma_start(d_eb[E * t:E * t + E, t, :], expert_b).then_inc(d_w, DMA)
            sp.dma_start(d_rb, router_b.rearrange("(o e) -> o e", o=1).broadcast_to([P, E])) \
                .then_inc(d_w, DMA)
            for q in range(4):
                d_load(q, q)
            with sp.Fori(0, STEPS // 4 - 1) as it:
                for q in range(4):
                    sp.wait_ge(d_bi, 2 * (it * 4 + q) + 3)
                    settle(sp)
                    d_load(it * 4 + q + 4, q)
                    d_store(it * 4 + q, q % 2)
            for q in range(4):
                d_store(STEPS - 4 + q, q % 2)
            for q in range(2):
                sp.wait_ge(d_st[q], DMA * (STEPS // 2 + 1))
                settle(sp)

        @block.tensor
        def _(pe):
            start_up(pe, PE_OWNS)
            phase_end(pe, 1)
            pe.wait_ge(s_w, DMA * n_weights)
            pe.wait_ge(s_id, 2)
            pe.wait_ge(s_qs, 1)
            with pe.Fori(0, B) as b:
                def a_step(steps):
                    cur, _, new = steps
                    if new:
                        n = b * NW + new.i
                        pe.wait_ge(a_ld[new.k // 2], 2 * DMA * (b * (NW // 8) + new.fill))
                        pe.wait_ge(a_nm, n + 1)
                        for t in range(4):
                            mm = pe.matmul(EA[new.k % 4][:, P * t:P * t + P], xa[:, new.k // 2, P * t:P * t + P],
                                           wemb[:, new.k % 2, :], start=True, stop=True)
                        mm.then_inc(a_e, 1)
                    if cur:
                        n = b * NW + cur.i
                        pe.wait_ge(a_nm, n + 5)
                        pe.wait_ge(a_ev, n + 1)
                        for t in range(4):
                            mm = pe.transpose(TB[cur.k % 2][:, P * t:P * t + P],
                                              ihat[:, cur.k % 2, P * t:P * t + P], ident[:, :])
                        mm.then_inc(a_tr, 1)

                stages(pe, NW, 8, 3, a_step)
                phase_end(pe, b * 3 + 2)

                def scores_for_max(t, k):
                    j, i = k // KC, k % KC
                    if k == 0 and t.first_M:
                        pe.wait_ge(s_kset, 2 * (b + 1))
                    if k % (U // 2) == 0:
                        pe.wait_ge(s_cat[2 * k // U][t.M.q], DMA * CAT_DMAS * t.M.fills(0) + DMA)
                    pe.wait_ge(s_red, U * (t.nM + 2) + k + 1)
                    pe.matmul(SM[k % 2], qcat[0:MAXROW, t.M.q, j, P * i:P * i + P], kcat[0:MAXROW, t.M.q, j, :],
                              start=True, stop=True).then_inc(s_sm, 1)

                def scores(t, u):
                    i, j = u // NH, u % NH
                    if u == 0:
                        pe.wait_ge(s_mrow, DMA * (t.nT + 2))
                    pe.wait_ge(s_exp, U * t.nT + u + 1)
                    pe.matmul(ST[u % 2], kcat[0:MAXROW + 2, t.T.q, j, P * i:P * i + P],
                          qcat[0:MAXROW + 2, t.T.q, j, :],
                              start=True, stop=True).then_inc(s_st, 1)

                def values(win, n, g):
                    if g == 0:
                        pe.wait_ge(s_vke, n + 2)
                        pe.wait_ge(s_oev, n + 1)
                    pe.wait_ge(s_exp, U * n + NH * g + NH + 2)
                    for j in range(NH):
                        mm = pe.matmul(O[32 * j:32 * j + 32, :], vaug[:, win.q, 2 * (g % 2) + g // 2, j, :],
                                       probs[:, (NH * g + j) % 8, :], start=(g == 0), stop=(g == KC - 1),
                                       tile_position=(0, 32 * j), skip_group_check=True)
                    mm.then_inc(s_pv, 1)

                def slot(t):
                    if t.P:
                        pe.wait_ge(s_lo, t.nP + 1)
                        pe.wait_ge(s_rec, t.nF + 1)
                        pe.matmul(X0, wqk[:, t.P.branch, :], qk_view(t.P), start=True, stop=True) \
                            .then_inc(s_qk, 1)
                    for k in range(U):
                        if t.T:
                            scores(t, k)
                        if t.M:
                            scores_for_max(t, k)
                        if k == 1 and t.R:
                            pe.wait_ge(s_mxs, t.nR + 1)
                            pe.wait_ge(s_mxe, t.nR + 1)
                            pe.wait_ge(s_vke, t.nP + 1)
                            pe.transpose(X2[0:2 * U, 0:P], mx[:, t.R.q % 2, :], ident[:, :]).then_inc(s_mxt, 1)
                        if k == 1 and t.F:
                            values(t.F, t.nF, KC - 1)
                        if k == 3 and t.P:
                            pe.wait_ge(s_vte, t.nP + 1)
                            pe.wait_ge(s_att, t.nF + 1)
                            for a in range(2):
                                mm = pe.matmul(vt_psum(t.P, a), wv[:, t.P.branch, HB * (1 - a):HB * (1 - a) + P], half_view(t.P, a),
                                               start=(a == 0), stop=(a == 1), skip_group_check=True)
                            mm.then_inc(s_vt, 1)
                        if k % NH == 1 and k > 1 and t.T:
                            values(t.T, t.nT, k // NH - 1)
                        if k == 7 and t.F:
                            pe.wait_ge(s_oev, t.nF + 2)
                            pe.wait_ge(s_lo, t.nP + (2 if t.P else 1))
                            pe.wait_ge(s_rec, t.nF + 1)
                            for c in range(KC):
                                mm = pe.transpose(X0[:, P * c:P * c + P], o_sb[:, P * c:P * c + P], ident[:, :])
                            mm.then_inc(s_ot, 1)
                        if k == 7 and t.P:
                            pe.wait_ge(s_vte, t.nP + 2)
                            pe.wait_ge(s_mxe, t.nR + (2 if t.R else 1))
                            pe.wait_ge(s_vke, t.nP + 1)
                            for i in range(2):
                                mm = pe.transpose(X2[:, P * i:P * i + P], v_own[:, P * i:P * i + P], ident[:, :])
                            mm.then_inc(s_vk, 1)
                        if k == 11 and t.F:
                            pe.wait_ge(s_rw, t.nF + 1)
                            pe.wait_ge(s_vte, t.nP + (2 if t.P else 1))
                            pe.wait_ge(s_att, t.nF + 1)
                            for c in range(KC):
                                mm = pe.transpose(X1[:, P * c:P * c + P], rec_wide[:, P * c:P * c + P], ident[:, :])
                            mm.then_inc(s_bt, 1)

                pipeline(pe, b, slot)
                phase_end(pe, b * 3 + 3)
                pe.wait_ge(s_fc, (b + 1) * 2 * DMA)

                def c_step(steps):
                    Y, M, N, A = steps
                    if M:
                        n = b * NW + M.i
                        pe.wait_ge(c_m, n + 2)
                        for f in range(NF):
                            pe.wait_ge(c_gl, NF * n + f + 1)
                            pe.matmul(CF[f % 2], fc1[:, P * f:P * f + P], c_mT, start=True, stop=True) \
                                .then_inc(c_f1, 1)
                    if Y:
                        n = b * NW + Y.i
                        pe.wait_ge(c_hf, n + 2)
                        pe.wait_ge(c_xo, n + 1)
                        pe.matmul(CY, wout[:, :], c_hfin, start=True, stop=True).then_inc(c_y, 1)
                    if N:
                        n = b * NW + N.i
                        pe.wait_ge(c_nm, n + 3)
                        pe.wait_ge(c_m, n + 1)
                        for t in range(4):
                            mm = pe.transpose(CT2[:, P * t:P * t + P], c_nh[:, P * t:P * t + P], ident[:, :])
                        mm.then_inc(c_t2, 1)
                    if A:
                        n = b * NW + A.i
                        pe.wait_ge(c_ld[A.k], 4 * DMA * (b * (NW // 4) + A.fill))
                        pe.wait_ge(c_hs, n + 1)
                        terms = [(wemb[:, 0, :], by_column(cx[:, 0, A.k, :])),
                                 (wpr[:, 0, :], att0[:, :].rearrange("p (m i x) -> p m i x", m=NW, i=NW)[:, :, A.i, :]),
                                 (wpr[:, 1, :], by_column(imgT[:, bass.ds(A.i * WT, WT)])),
                                 (wprc[:, :], cx[:, 1, A.k, :])]
                        for m, (w, v) in enumerate(terms):
                            mm = pe.matmul(CH, w, v, start=(m == 0), stop=(m == 3))
                        mm.then_inc(c_h, 1)

                    def second(fs):
                        n = b * NW + M.i
                        if fs[0] == 0:
                            pe.wait_ge(c_hf, n + 1)
                        for f in fs:
                            pe.wait_ge(c_gl, NF * n + f + 3)
                            mm = pe.matmul(CM, fc2[:, f, :], c_g[:, f, :], start=(f == 0), stop=(f == NF - 1))
                        if fs[-1] == NF - 1:
                            mm.then_inc(c_f2, 1)

                    if M:
                        second([0, 1])
                    if A:
                        n = b * NW + A.i
                        pe.wait_ge(c_hs, n + 2)
                        pe.wait_ge(c_nm, n + 2)
                        for t in range(4):
                            mm = pe.transpose(CT1[:, P * t:P * t + P], c_hT[:, A.k, P * t:P * t + P], ident[:, :])
                        mm.then_inc(c_t1, 1)
                    if M:
                        second([2, 3])

                stages(pe, NW, 4, 4, c_step)
                phase_end(pe, b * 3 + 4)

            pe.wait_ge(d_w, DMA * (G8 + 3))

            def d_step(steps):
                cur, nxt, new, newest = steps

                def experts(ts):
                    for t in ts:
                        pe.wait_ge(d_cb, G8 * cur.i + t + 2)
                        pe.wait_ge(d_sc, G8 * cur.i + t + 2)
                        for h in range(2):
                            mm = pe.matmul(DY[t % 2][:, h, :], d_xT[:, cur.k, t, :],
                                           d_ew[:, 4 * h:4 * h + 4, :].rearrange("p e n -> p (e n)"),
                                           start=True, stop=True)
                        mm.then_inc(d_y, 1)

                if cur:
                    for h in range(2):
                        pe.wait_ge(d_gte, cur.i + 2)
                        pe.wait_ge(d_bi, 2 * cur.i + h + 1)
                        pe.matmul(DB, d_gT, d_eb[:, 4 * h:4 * h + 4, :].rearrange("p t n -> p (t n)"),
                                  start=True, stop=True).then_inc(d_bm, 1)
                        experts([h])
                    experts([2, 3])
                if new:
                    pe.wait_ge(d_nm, new.i + 3)
                    pe.wait_ge(d_xt, 2 * new.i + 1)
                    for h in range(2):
                        for t in range(4):
                            mm = pe.transpose(DT[h][:, P * t:P * t + P], d_xl[:, 4 * h + t, :], ident[:, :])
                        mm.then_inc(d_tr, 1)
                if cur:
                    experts([4, 5])
                if nxt:
                    pe.wait_ge(d_g, nxt.i + 2)
                    pe.wait_ge(d_bi, 2 * nxt.i + 1)
                    settle(pe)
                    pe.transpose(DB[0:E * G8, 0:P], d_gate[:, nxt.k % 2, :, :].rearrange("p t e -> p (t e)"),
                                 ident[:, :]).then_inc(d_gt, 1)
                if cur:
                    experts([6])
                if new:
                    pe.wait_ge(d_xt, 2 * new.i + 3)
                    pe.wait_ge(d_g, new.i + 1)
                    for t in range(G8):
                        mm = pe.matmul(DL[:, E * t:E * t + E], d_xT[:, new.k, t, :], d_rw, start=True, stop=True)
                    mm.then_inc(d_lg, 1)
                if cur:
                    experts([7])

            stages(pe, STEPS, 4, 4, d_step)

        @block.scalar
        def _(act):
            start_up(act, ACT_OWNS)
            act.wait_ge(s_w, DMA * n_weights)
            act.mul(wqk[:, :, 0:HB], wqk[:, :, 0:HB], float(D) ** -0.5).then_inc(s_qs, 1)

            def n_step(cur, nxt):
                if cur:
                    act.wait_ge(n_rs, cur.i + 3)
                    act.wait_ge(n_st[cur.k], DMA * cur.fill)
                    for t in range(G8):
                        a = act.activation(rows_out[:, cur.k, t, :], rows_in[:, cur.k, t, :], ACT.Identity,
                                           bias=lnr[:, cur.k % 2, 3, t:t + 1], scale=lnr[:, cur.k % 2, 1, t:t + 1])
                    a.then_inc(n_nm, 1)

            lookahead(act, STEPS, 4, n_step)
            phase_end(act, 1)
            with act.Fori(0, B) as b:
                def a_step(cur, nxt):
                    if nxt:
                        n = b * NW + nxt.i
                        q = nxt.k % 2
                        act.wait_ge(a_rs, n + 3)
                        act.wait_ge(a_tr, n + 1)
                        for t in range(4):
                            a = act.activation(ihat[:, q, P * t:P * t + P], EA[nxt.k % 4][:, P * t:P * t + P],
                                               ACT.Identity, bias=lnr[:, q, 3, t:t + 1],
                                               scale=lnr[:, q, 1, t:t + 1])
                        a.then_inc(a_nm, 1)
                    if cur:
                        act.wait_ge(a_tr, b * NW + cur.i + 3)
                        act.activation(imgT[:, bass.ds(cur.i * WT, WT)], TB[cur.k % 2], ACT.Identity,
                                       bias=B1, scale=G1).then_inc(a_ev, 1)

                lookahead(act, NW, 8, a_step)
                phase_end(act, b * 3 + 2)

                def exponentials(t, u):
                    if u % NH == 0:
                        act.wait_ge(s_pv, KC * t.nT + u // NH + 15)
                    act.wait_ge(s_st, U * t.nT + u + 65)
                    act.activation(probs[:, u % 8, :], ST[u % 2], ACT.Exp).then_inc(s_exp, 1)

                def slot(t):
                    if t.P:
                        act.wait_ge(s_qk, t.nP + 1)
                        for h in range(2):
                            act.wait_ge(s_cat[h][(t.P.q + 2) % CATQ], DMA * CAT_DMAS * t.P.fills(2) + DMA)
                        act.copy(parts[:, t.P.q % 2, 0, :], X0).then_inc(s_hb, 1)
                    for u in range(U):
                        if t.T:
                            exponentials(t, u)
                        if u == 1 and t.R:
                            act.wait_ge(s_mxt, t.nR + 3)
                            act.wait_ge(s_mrow, DMA * (t.nR + 1))
                            act.mul(mxb[:, :], X2[0:2 * U, 0:P], 1 / MAXUNIT).then_inc(s_mxe, 1)
                        if u == 1 and t.F:
                            act.wait_ge(s_pv, KC * t.nF + KC + 16)
                            act.wait_ge(s_att, t.nF + 1)
                            act.copy(o_sb[:, :], O).then_inc(s_oev, 1)
                        if u == 4 and t.P:
                            act.wait_ge(s_vt, t.nP + 1)
                            act.wait_ge(s_cv, t.nP + 1)
                            act.wait_ge(s_vk, t.nP + 1)
                            if t.P.branch == 0:
                                padded, made = vT[0][:, :, 1:5], X1[:, 0:264].rearrange("p (y c) -> p y c", c=SS)
                                own, inner = v_own[:, :].rearrange("p (y c) -> p y c", c=SS), made[:, 1:65, :]
                            else:
                                padded, made = vT[1][:, 1:5, :], X1[:, 0:264].rearrange("p (y c) -> p y c", y=SS)
                                own, inner = v_own[:, :].rearrange("p (y c) -> p y c", y=SS), made[:, :, 1:65]
                            act.copy(own, inner)
                            act.copy(padded, made).then_inc(s_vte, 1)
                        if u == 9 and t.P:
                            act.wait_ge(s_vk, t.nP + 2)
                            act.wait_ge(s_pv, KC * (t.nP - 3) + 16)
                            act.copy(vaug[:, t.P.q, :, :, 0:D],
                                     X2[:, 0:KC * HB].rearrange("p (c j d) -> p c j d", c=KC, j=NH)) \
                                .then_inc(s_vke, 1)

                pipeline(act, b, slot)
                phase_end(act, b * 3 + 3)

                def c_step(steps):
                    M = steps[1]
                    if M:
                        n = b * NW + M.i
                        act.wait_ge(c_f2, n + 1)
                        for f in range(NF):
                            act.wait_ge(c_f1, NF * n + f + 2)
                            act.activation(c_g[:, f, :], CF[f % 2], ACT.Gelu, bias=BF1[f]).then_inc(c_gl, 1)

                stages(act, NW, 4, 4, c_step)
                phase_end(act, b * 3 + 4)

            def d_step(steps):
                cur, nxt, new, newest = steps

                def scale(ts):
                    for t in ts:
                        act.wait_ge(d_y, G8 * cur.i + t + 1)
                        act.wait_ge(d_out, G8 // 2 * cur.i + t // 2 + 2)
                        for e in range(E_ACT):
                            a = act.activation(d_scaled[:, e, t % 4, :],
                                               DY[t % 2][:, e // 4, P * (e % 4):P * (e % 4) + P],
                                               ACT.Copy, scale=d_gate[:, cur.k % 2, t, e:e + 1])
                        a.then_inc(d_sc, 1)

                def norm(h):
                    q = new.k % 2
                    if h == 0:
                        act.wait_ge(d_rs, new.i + 3)
                        act.wait_ge(d_tr, 2 * new.i + 1)
                    for t in range(4 * h, 4 * h + 4):
                        a = act.activation(d_xl[:, t, :], d_x[:, new.k, t, :], ACT.Identity,
                                           bias=lnr[:, q, 3, t:t + 1], scale=lnr[:, q, 1, t:t + 1])
                    if h == 1:
                        a.then_inc(d_nm, 1)

                if new:
                    norm(0)
                if cur:
                    scale([0])
                if new:
                    norm(1)
                if cur:
                    scale([1, 2, 3])
                if new:
                    for h in range(2):
                        act.wait_ge(d_tr, 2 * new.i + h + 2)
                        act.copy(d_xT[:, new.k, 4 * h:4 * h + 4, :].rearrange("p t n -> p (t n)"), DT[h]) \
                            .then_inc(d_xt, 1)
                if nxt:
                    act.wait_ge(d_df, nxt.i + 1)
                    act.activation(d_s[:, 1, :], d_s[:, 0, :], ACT.Exp).then_inc(d_e2, 1)
                if cur:
                    scale([4, 5])
                if nxt:
                    act.wait_ge(d_gt, nxt.i + 3)
                    act.wait_ge(d_bm, 2 * nxt.i + 1)
                    act.copy(d_gT, DB[0:E * G8, 0:P]).then_inc(d_gte, 1)
                if cur:
                    scale([6, 7])

            stages(act, STEPS, 4, 4, d_step)

        @block.vector
        def _(dve):
            start_up(dve, DVE_OWNS)
            for tile in (wpr, wv, wemb, wout, vT[0], vT[1], vaug):
                shape = tile.shape
                dve.memset(tile[tuple(slice(None) for _ in shape)], 0.0).then_inc(s_dz, 1)
            dve.wait_ge(s_dz, 7)
            dve.memset(vaug[:, :, :, :, D:D + 1], 1.0)
            for i, v in enumerate((1e-6, 1e-5, -0.5, -1.0)):
                dve.memset(konst[:, i, :], v)
            for e in range(E):
                dve.memset(konst[:, 4, e:e + 1], float(E - e))
            dve.drain().then_inc(s_set, 1)

            def moments(tiles, k, stats_sem, moments_sem, n):
                for t, tile in enumerate(tiles):
                    a = dve.bn_stats(stat[:, k, t, :], tile)
                a.then_inc(stats_sem, 1)
                dve.wait_ge(stats_sem, n + 1)
                settle(dve)
                for t in range(len(tiles)):
                    a = dve.bn_aggr(mv[:, k, t, :], stat[:, k, t, :])
                a.then_inc(moments_sem, 1)

            def n_step(cur, nxt):
                if nxt:
                    dve.wait_ge(n_ld[nxt.k], DMA * nxt.fill)
                    dve.wait_ge(n_rs, nxt.i + 1)
                    moments([rows_in[:, nxt.k, t, :] for t in range(G8)], nxt.k % 2, n_bn, n_mv, nxt.i)

            lookahead(dve, STEPS, 4, n_step)
            phase_end(dve, 1)
            with dve.Fori(0, B) as b:
                def a_step(cur, nxt):
                    if nxt:
                        n = b * NW + nxt.i
                        dve.wait_ge(a_e, n + 9)
                        dve.wait_ge(a_rs, n + 1)
                        moments([EA[nxt.k % 4][:, P * t:P * t + P] for t in range(4)], nxt.k % 2, a_bn, a_mv, n)

                lookahead(dve, NW, 4, a_step)
                phase_end(dve, b * 3 + 2)

                dve.memset(workb[PAIRS:MAXROW, 4096:16384], 0.0).then_inc(s_kset, 1)

                def tile_max(t, k):
                    if k == 0:
                        dve.wait_ge(s_mxt, t.nM + 1)
                    j, i = k // KC, k % KC
                    dve.wait_ge(s_sm, U * t.nM + k + 1)
                    dve.tensor_reduce(mx[:, t.M.q % 2, k:k + 1], SM[k % 2], AX.X, ALU.max, negate=True) \
                        .then_inc(s_red, 1)

                def slot(t):
                    for k in range(U):
                        if t.M:
                            tile_max(t, k)
                        if k == 0 and t.P:
                            dve.wait_ge(s_hb, t.nP + 1)
                            dve.tensor_tensor(parts[:, t.P.q % 2, 1, :], X0, parts[:, t.P.q % 2, 0, :],
                                              ALU.subtract).then_inc(s_lo, 1)
                        if k == 8 and t.F:
                            dve.wait_ge(s_ot, t.nF + 1)
                            dve.wait_ge(s_bt, t.nF + 1)
                            dve.reciprocal(rec[:, :, :],
                                           X0.rearrange("p (c j x) -> p c j x", c=KC, j=NH)[:, :, :, D]) \
                                .then_inc(s_rec, 1)
                            dve.wait_ge(s_rec, t.nF + 2)
                            dve.tensor_copy(rec_wide[:, :].rearrange("p (c j x) -> p (c j) x", c=KC, j=NH),
                                            rec[:, :, :].rearrange("p c j -> p (c j)").unsqueeze(2)
                                            .broadcast_to([P, KC * NH, 32])).then_inc(s_rw, 1)
                        if k == 12 and t.F:
                            dve.wait_ge(s_bt, t.nF + 2)
                            if t.F.branch == 0:
                                dst, fold = att0[:, bass.ds(t.F.w * WT, WT)], lambda v: v
                            else:
                                dst = imgT[:, bass.ds(t.F.w * WT, WT)].rearrange("p (y a c) -> p a y c", y=SS, a=2)
                                fold = lambda v: v.rearrange("p (a y c) -> p a y c", a=2, y=SS)
                            dve.tensor_tensor(dst, fold(o_sb[:, :]), fold(X1), ALU.mult).then_inc(s_att, 1)
                    if t.M:
                        m = mx[:, t.M.q % 2, :]
                        dve.wait_ge(s_red, U * (t.nM + 2) + U + 2)
                        dve.tensor_scalar(mxh[:, :], m[:, 0:U], 1 / MAXUNIT, None, ALU.mult).then_inc(s_mh, 1)
                        dve.wait_ge(s_mh, t.nM + 1)
                        dve.scalar_tensor_tensor(out=m[:, U:2 * U], in0=mxh[:, :], scalar=-MAXUNIT, in1=m[:, 0:U],
                                                 op0=ALU.mult, op1=ALU.add).then_inc(s_mxs, 1)

                pipeline(dve, b, slot)
                phase_end(dve, b * 3 + 3)

                def c_step(steps):
                    Y, M, N, A = steps
                    if N:
                        n = b * NW + N.i
                        q = N.k % 2
                        dve.wait_ge(c_rs, n + 1)
                        dve.wait_ge(c_t2, n + 1)
                        for t in range(4):
                            a = dve.tensor_scalar(c_nh[:, P * t:P * t + P], CT1[:, P * t:P * t + P],
                                                  lnr[:, q, 1, t:t + 1], lnr[:, q, 3, t:t + 1],
                                                  ALU.mult, ALU.add)
                        a.then_inc(c_nm, 1)
                    if Y:
                        n = b * NW + Y.i
                        q = Y.k % 2
                        dve.wait_ge(c_y, n + 2)
                        dve.wait_ge(c_st[q], DMA * (b * (NW // 2) + 2 * Y.fill - 1 + Y.k // 2))
                        dve.tensor_tensor(by_column(cxo[:, q, :]),
                                          CY[C0:P, :].rearrange("p (m y c) -> p m y c", m=NW, y=SS),
                                          by_column(cx[C0:P, 0, Y.k, :]), ALU.add).then_inc(c_xo, 1)
                    if N:
                        n = b * NW + N.i
                        dve.wait_ge(c_t2, n + 2)
                        dve.wait_ge(c_f1, NF * n + 1)
                        dve.tensor_scalar(c_mT, CT2, G2, B2, ALU.mult, ALU.add).then_inc(c_m, 1)
                    if A:
                        n = b * NW + A.i
                        dve.wait_ge(c_h, n + 1)
                        dve.tensor_scalar(c_hT[:, A.k, :], CH, BP, None, ALU.add).then_inc(c_hs, 1)
                        dve.wait_ge(c_t1, n + 1)
                        moments([CT1[:, P * t:P * t + P] for t in range(4)], A.k % 2, c_bn, c_mv, n)
                    if M:
                        n = b * NW + M.i
                        dve.wait_ge(c_f2, n + 2)
                        dve.scalar_tensor_tensor(out=c_hfin, in0=CM, scalar=BF2, in1=c_hT[:, M.k, :],
                                                 op0=ALU.add, op1=ALU.add).then_inc(c_hf, 1)

                stages(dve, NW, 4, 4, c_step)
                phase_end(dve, b * 3 + 4)

            dve.memset(d_eb, 0.0).then_inc(d_set, 1)
            dve.wait_ge(d_w, DMA * (G8 + 3))

            def spread(v):
                return v.unsqueeze(2).broadcast_to([P, G8, E])

            def over_tiles(v):
                return v.unsqueeze(1).broadcast_to([P, G8, E])

            GSTEP = 17

            def gating(j, part):
                base = GSTEP * j.i
                lg, pick, oh1, oh2, lg2 = (d_t[:, i, :, :] for i in range(5))
                m1, m2, top = d_s[:, 2, :], d_s[:, 3, :], d_s[:, 4, :]
                if part == 0:
                    dve.tensor_tensor(lg, DL.rearrange("p (t e) -> p t e", e=E), over_tiles(d_rb), ALU.add) \
                        .then_inc(d_gs, 1)
                    dve.wait_ge(d_gs, base + 1)
                    dve.tensor_reduce(m1, lg, AX.X, ALU.max).then_inc(d_gs, 1)
                    dve.wait_ge(d_gs, base + 2)
                    dve.tensor_tensor(pick, lg, spread(m1), ALU.is_ge).then_inc(d_gs, 1)
                    dve.wait_ge(d_gs, base + 3)
                    dve.tensor_tensor(pick, pick, over_tiles(RANK), ALU.mult).then_inc(d_gs, 1)
                    dve.wait_ge(d_gs, base + 4)
                if part == 1:
                    dve.tensor_reduce(top, pick, AX.X, ALU.max).then_inc(d_gs, 1)
                    dve.wait_ge(d_gs, base + 5)
                    dve.tensor_tensor(oh1, pick, spread(top), ALU.is_equal).then_inc(d_gs, 1)
                    dve.wait_ge(d_gs, base + 6)
                    dve.scalar_tensor_tensor(out=lg2, in0=oh1, scalar=-1e38, in1=lg, op0=ALU.mult, op1=ALU.add) \
                        .then_inc(d_gs, 1)
                    dve.wait_ge(d_gs, base + 7)
                    dve.tensor_reduce(m2, lg2, AX.X, ALU.max).then_inc(d_gs, 1)
                    dve.wait_ge(d_gs, base + 8)
                    dve.wait_ge(d_e2, j.i + 1)
                    dve.tensor_tensor(d_s[:, 0, :], m2, m1, ALU.subtract).then_inc(d_df, 1)
                if part == 2:
                    dve.tensor_tensor(pick, lg2, spread(m2), ALU.is_ge).then_inc(d_gs, 1)
                    dve.wait_ge(d_gs, base + 9)
                    dve.tensor_tensor(pick, pick, over_tiles(RANK), ALU.mult).then_inc(d_gs, 1)
                    dve.wait_ge(d_gs, base + 10)
                    dve.tensor_reduce(top, pick, AX.X, ALU.max).then_inc(d_gs, 1)
                    dve.wait_ge(d_gs, base + 11)
                    dve.tensor_tensor(oh2, pick, spread(top), ALU.is_equal).then_inc(d_gs, 1)
                    dve.wait_ge(d_gs, base + 12)
                if part == 3:
                    dve.wait_ge(d_e2, j.i + 2)
                    dve.tensor_scalar(d_s[:, 5, :], d_s[:, 1, :], 1.0, None, ALU.add).then_inc(d_gs, 1)
                    dve.wait_ge(d_gs, base + 13)
                    dve.reciprocal(d_s[:, 6, :], d_s[:, 5, :]).then_inc(d_gs, 1)
                    dve.wait_ge(d_gs, base + 14)
                    dve.tensor_tensor(d_s[:, 7, :], d_s[:, 6, :], d_s[:, 1, :], ALU.mult).then_inc(d_gs, 1)
                    dve.wait_ge(d_gs, base + 15)
                    dve.tensor_tensor(oh1, oh1, spread(d_s[:, 6, :]), ALU.mult).then_inc(d_gs, 1)
                    dve.wait_ge(d_gs, base + 16)
                    dve.tensor_tensor(oh2, oh2, spread(d_s[:, 7, :]), ALU.mult).then_inc(d_gs, 1)
                    dve.wait_ge(d_gs, base + GSTEP)
                    dve.wait_ge(d_gt, j.i + 1)
                    dve.tensor_tensor(d_gate[:, j.k % 2, :, :], oh1, oh2, ALU.add).then_inc(d_g, 1)

            def d_step(steps):
                cur, nxt, new, newest = steps

                def bias(h):
                    q = cur.k % 2
                    dve.wait_ge(d_st[q], DMA * (2 * cur.fill - 1 + cur.k // 2))
                    dve.wait_ge(d_bm, 2 * cur.i + h + 2)
                    dve.tensor_tensor(d_acc[:, q, 4 * h:4 * h + 4, :].rearrange("p t n -> p (t n)"), DB,
                                      d_x[:, cur.k, 4 * h:4 * h + 4, :].rearrange("p t n -> p (t n)"),
                                      ALU.add).then_inc(d_bi, 1)

                def combine(t):
                    q = cur.k % 2
                    dve.wait_ge(d_bi, 2 * cur.i + t // 4 + 2)
                    dve.wait_ge(d_y, G8 * cur.i + t + 1)
                    dve.wait_ge(d_out, G8 // 2 * cur.i + t // 2 + 2)
                    acc, other = d_acc[:, q, t, :], d_scaled[:, E_ACT, t % 4, :]
                    half = (E - E_ACT) // 2
                    for m in range(half):
                        before = 2 * (half - 1) * (G8 * cur.i + t) + 2 * (m - 1)
                        for z, s in enumerate((acc, other)):
                            e = E_ACT + 2 * m + z
                            y, g = DY[t % 2][:, e // 4, P * (e % 4):P * (e % 4) + P], d_gate[:, q, t, e:e + 1]
                            if m > 0:
                                dve.wait_ge(d_ac, before + z + 1)
                            if m == 0 and z == 1:
                                ins = dve.tensor_scalar(s, y, g, None, ALU.mult)
                            else:
                                ins = dve.scalar_tensor_tensor(out=s, in0=y, scalar=g, in1=s,
                                                               op0=ALU.mult, op1=ALU.add)
                            if m < half - 1:
                                ins.then_inc(d_ac, 1)
                    ins.then_inc(d_cb, 1)

                for t in range(G8):
                    if cur and t < 2:
                        bias(t)
                    if cur:
                        combine(t)
                    if t == 0 and nxt:
                        dve.wait_ge(d_lg, nxt.i + 1)
                    if t in (0, 1, 3, 4) and nxt:
                        gating(nxt, (0, 1, 3, 4).index(t))
                    if t == 5 and newest:
                        q = newest.k % 2
                        dve.wait_ge(d_ld[newest.k], DMA * newest.fill)
                        dve.wait_ge(d_rs, newest.i + 1)
                        moments([d_x[:, newest.k, i, :] for i in range(G8)], q, d_bn, d_mv, newest.i)

            stages(dve, STEPS, 4, 4, d_step)

        @block.gpsimd
        def _(pool):
            start_up(pool, POOL_OWNS)
            pool.memset(ident[:, :], 0.0).then_inc(s_id, 1)
            pool.wait_ge(s_id, 1)
            pool.affine_select(out=ident[:, :], in_=ident[:, :], compare_op=ALU.not_equal, fill=1.0, base=0,
                               pattern=[[-1, P]], channel_multiplier=1).then_inc(s_id, 1)
            pool.wait_ge(s_set, 1)

            def ln_small(m, to, n, eps, step, steps_before, done):
                pool.tensor_tensor(to[:, 0, 0:n], m[:, 0:n, 1], eps[:, 0:n], ALU.add).then_inc(step, 1)
                pool.wait_ge(step, steps_before + 1)
                pool.tensor_tensor(to[:, 1, 0:n], to[:, 0, 0:n], NHALF[:, 0:n], ALU.pow).then_inc(step, 1)
                pool.wait_ge(step, steps_before + 2)
                pool.tensor_tensor(to[:, 2, 0:n], m[:, 0:n, 0], to[:, 1, 0:n], ALU.mult).then_inc(step, 1)
                pool.wait_ge(step, steps_before + 3)
                pool.tensor_tensor(to[:, 3, 0:n], to[:, 2, 0:n], NEG1[:, 0:n], ALU.mult).then_inc(done, 1)

            def n_step(cur, nxt):
                if nxt:
                    pool.wait_ge(n_mv, nxt.i + 1)
                    pool.wait_ge(n_nm, nxt.i + 1)
                    ln_small(mv[:, nxt.k % 2], lnr[:, nxt.k % 2], G8, EPS6, n_ln, 3 * nxt.i, n_rs)

            lookahead(pool, STEPS, 4, n_step)
            phase_end(pool, 1)
            with pool.Fori(0, B) as b:
                def a_step(cur, nxt):
                    if nxt:
                        n = b * NW + nxt.i
                        pool.wait_ge(a_mv, n + 1)
                        pool.wait_ge(a_nm, n + 3)
                        ln_small(mv[:, nxt.k % 2], lnr[:, nxt.k % 2], 4, EPS5, a_ln, 3 * n, a_rs)

                lookahead(pool, NW, 4, a_step)
                phase_end(pool, b * 3 + 2)
                pool.memset(workb[PAIRS:MAXROW, 0:4096], 0.0)
                pool.memset(kcat[MAXROW:MAXROW + 2, :, :, :].rearrange("p q j n -> p (q j n)"), MAXUNIT)
                pool.drain().then_inc(s_kset, 1)
                CVS = 16

                def slot(t):
                    if not t.P:
                        return
                    br = t.P.branch
                    pool.wait_ge(s_vte, t.nP + 2)
                    shape = dict(y=64) if br == 0 else dict(y=SS)

                    def grid(v):
                        return v.rearrange("p (y c) -> p y c", **shape)

                    def tap(n):
                        y, c = n // 3, n % 3
                        return vT[0][:, y:y + 64, c:c + 4] if br == 0 else vT[1][:, y:y + 4, c:c + 64]

                    base = CVS * t.nP
                    pool.wait_ge(s_cv, t.nP + 1)
                    settle(pool)
                    pool.tensor_scalar(grid(cv_acc[:, :]), tap(0), cw[:, br, 0:1], cb[:, br:br + 1],
                                       ALU.mult, ALU.add).then_inc(s_cvc, 1)
                    for n in range(1, 9):
                        if n > 2:
                            pool.wait_ge(s_cvc, base + 2 * n - 2)
                            settle(pool)
                        pool.tensor_scalar(grid(cv_tmp[n % 2][:, :]), tap(n), cw[:, br, n:n + 1], 0.0,
                                           ALU.mult, ALU.add).then_inc(s_cvc, 1)
                        if n > 1:
                            if n == 2:
                                pool.wait_ge(s_cvc, base + 2 * n - 2)
                            pool.tensor_tensor(cv_acc[:, :], cv_acc[:, :], cv_tmp[(n - 1) % 2][:, :], ALU.add) \
                                .then_inc(s_cvc, 1)
                            settle(pool)
                    pool.wait_ge(s_cvc, base + CVS)
                    pool.wait_ge(s_cvd0, t.P.conv_free[0] + DMA)
                    pool.wait_ge(s_cvd1, t.P.conv_free[1] + DMA)
                    if br == 0:
                        ins = pool.tensor_tensor(cv_out[:, :], cv_acc[:, :], cv_tmp[0][:, :], ALU.add)
                    else:
                        v = [z[:, :].rearrange("p (y m c) -> p y m c", y=SS, m=16) for z in (cv_acc, cv_tmp[0])]
                        ins = pool.tensor_tensor(cv_out[:, :].rearrange("p (m y c) -> p y m c", y=SS, m=16),
                                                 v[0], v[1], ALU.add)
                    ins.then_inc(s_cv, 1)

                pipeline(pool, b, slot)
                phase_end(pool, b * 3 + 3)

                def c_step(steps):
                    A = steps[3]
                    if A:
                        n = b * NW + A.i
                        pool.wait_ge(c_mv, n + 1)
                        pool.wait_ge(c_nm, n + 1)
                        ln_small(mv[:, A.k % 2], lnr[:, A.k % 2], 4, EPS5, c_ln, 3 * n, c_rs)

                stages(pool, NW, 4, 4, c_step)
                phase_end(pool, b * 3 + 4)

            SUMS = 4

            def d_step(steps):
                cur, new = steps[0], steps[3]

                def total(h):
                    q = cur.k % 2
                    n = G8 // 2 * cur.i + h
                    pool.wait_ge(d_sc, G8 * cur.i + 2 * h + 5)
                    pool.wait_ge(d_cb, G8 * cur.i + 2 * h + 5)
                    v = [d_scaled[:, e, 2 * (h % 2):2 * (h % 2) + 2, :] for e in range(E_ACT + 1)]
                    acc = d_acc[:, q, 2 * h:2 * h + 2, :]
                    pool.tensor_tensor(v[0], v[0], v[1], ALU.add).then_inc(d_sum, 1)
                    pool.tensor_tensor(v[2], v[2], v[3], ALU.add).then_inc(d_sum, 1)
                    pool.tensor_tensor(acc, acc, v[4], ALU.add).then_inc(d_sum, 1)
                    pool.wait_ge(d_sum, SUMS * n + 2)
                    pool.tensor_tensor(v[0], v[0], v[2], ALU.add).then_inc(d_sum, 1)
                    pool.wait_ge(d_sum, SUMS * n + SUMS)
                    pool.tensor_tensor(acc, acc, v[0], ALU.add).then_inc(d_out, 1)

                if cur:
                    for h in range(3):
                        total(h)
                if new:
                    pool.wait_ge(d_mv, new.i + 1)
                    pool.wait_ge(d_nm, new.i + 1)
                    ln_small(mv[:, new.k % 2], lnr[:, new.k % 2], G8, EPS5, d_ln, 3 * new.i, d_rs)
                if cur:
                    total(3)

            stages(pool, STEPS, 4, 4, d_step)


_INS = ["x", "L0_conv_w_embed", "L0_conv_g1", "L0_conv_b1", "L0_conv_w_qkv", "L0_conv_conv_w0", "L0_conv_conv_b0",
        "L0_conv_conv_w1", "L0_conv_conv_b1", "L0_conv_w_proj", "L0_conv_b_proj", "L0_conv_g2", "L0_conv_b2",
        "L0_conv_w_fc1", "L0_conv_b_fc1", "L0_conv_w_fc2", "L0_conv_b_fc2", "L0_conv_w_out", "L0_ffn_router_w",
        "L0_ffn_router_b", "L0_ffn_expert_w", "L0_ffn_expert_b"]


def kernel(**inputs):
    import numpy as _np
    import concourse.bacc as _bacc
    from concourse.bass_utils import run_bass_kernel_spmd as _run

    nc = _bacc.Bacc("TRN2", target_bir_lowering=False, num_devices=1)
    arrays, args = {}, []
    for name in _INS:
        a = _np.ascontiguousarray(inputs[name])
        arrays[f"in_{name}"] = a
        args.append(nc.dram_tensor(f"in_{name}", a.shape, mybir.dt.from_np(a.dtype), kind="ExternalInput").ap())
    args.append(nc.dram_tensor("out", (B, C0, H, W), F32, kind="ExternalOutput").ap())
    build(nc, *args)
    r = _run(nc, [arrays], core_ids=[0])
    return r.results[0]["out"]
```
